# Optimizing a Trainium2 kernel written in Bass

```python
import numpy as np
import jax
import jax.numpy as jnp

def _softmax(x, axis=-1):
    return jax.nn.softmax(x, axis=axis)

def _gelu(x):
    return jax.nn.gelu(x, approximate=True)

def _silu(x):
    return jax.nn.silu(x)

def _sigmoid(x):
    return jax.nn.sigmoid(x)

def _layernorm(x, axis=-1, eps=1e-05):
    m = jnp.mean(x, axis=axis, keepdims=True)
    v = jnp.var(x, axis=axis, keepdims=True)
    return (x - m) / jnp.sqrt(v + eps)

def _scatter_add(tgt, idx, src, axis=0):
    return tgt.at[idx].add(src)

def _segment_sum(src, seg, n):
    return jax.ops.segment_sum(src, seg, n)
kernel_name = 'mk_adaln_d2_jaxref_r4_f5cc38'

def setup_inputs(seed: int=0):
    np.random.seed(seed)
    _w = jnp.asarray

    def _L0_attn_setup():
        import jax, jax.numpy as jnp
        import numpy as np
        B, T, C = (4, 1024, 256)
        NUM_LAYERS = 24
        LAYER_ID = 0
        EPS = 1e-05

        def _ln(x, w, b):
            m = x.mean(-1, keepdims=True)
            v = x.var(-1, keepdims=True)
            return (x - m) / jnp.sqrt(v + EPS) * w + b

        def _time_shift(x):
            return jnp.pad(x, ((0, 0), (1, 0), (0, 0)))[:, :-1]

        def _wkv(w, u, k, v):

            def step(carry, kv_t):
                aa, bb, pp = carry
                kt, vt = kv_t
                ww = u + kt
                p = jnp.maximum(pp, ww)
                e1 = jnp.exp(pp - p)
                e2 = jnp.exp(ww - p)
                y = (e1 * aa + e2 * vt) / (e1 * bb + e2)
                ww2 = pp + w
                p2 = jnp.maximum(ww2, kt)
                e1 = jnp.exp(ww2 - p2)
                e2 = jnp.exp(kt - p2)
                return ((e1 * aa + e2 * vt, e1 * bb + e2, p2), y)
            Bz, Tz, Cz = k.shape
            init = (jnp.zeros((Bz, Cz), k.dtype), jnp.zeros((Bz, Cz), k.dtype), jnp.full((Bz, Cz), -1e+38, k.dtype))
            kT = jnp.swapaxes(k, 0, 1)
            vT = jnp.swapaxes(v, 0, 1)
            _, y = jax.lax.scan(step, init, (kT, vT))
            return jnp.swapaxes(y, 0, 1)
        key = jax.random.key(seed)
        ks = jax.random.split(key, 9)
        s = 0.02
        ratio_0_to_1 = LAYER_ID / (NUM_LAYERS - 1)
        ratio_1_to_almost0 = 1.0 - LAYER_ID / NUM_LAYERS
        h = np.arange(C, dtype=np.float64)
        time_decay = (-5.0 + 8.0 * (h / (C - 1)) ** (0.7 + 1.3 * ratio_0_to_1)).astype(np.float32)
        zigzag = ((np.arange(C) + 1) % 3 - 1) * 0.5
        time_first = (np.ones(C) * np.log(0.3) + zigzag).astype(np.float32)
        xi = np.arange(C, dtype=np.float64) / C
        tmk = (xi ** ratio_1_to_almost0).astype(np.float32)
        tmv = (xi ** ratio_1_to_almost0 + 0.3 * ratio_0_to_1).astype(np.float32)
        tmr = (xi ** (0.5 * ratio_1_to_almost0)).astype(np.float32)
        cmk = (xi ** ratio_1_to_almost0).astype(np.float32)
        H = 4 * C
        return {'x': jax.random.normal(ks[0], (B, T, C), jnp.float32), 'ln0_w': jnp.ones(C), 'ln0_b': jnp.zeros(C), 'ln1_w': jnp.ones(C), 'ln1_b': jnp.zeros(C), 'ln2_w': jnp.ones(C), 'ln2_b': jnp.zeros(C), 'time_decay': jnp.asarray(time_decay), 'time_first': jnp.asarray(time_first), 'tmk': jnp.asarray(tmk), 'tmv': jnp.asarray(tmv), 'tmr': jnp.asarray(tmr), 'Wk': jax.random.normal(ks[1], (C, C), jnp.float32) * s, 'Wv': jax.random.normal(ks[2], (C, C), jnp.float32) * s, 'Wr': jax.random.normal(ks[3], (C, C), jnp.float32) * s, 'Wo': jax.random.normal(ks[4], (C, C), jnp.float32) * s, 'cmk': jnp.asarray(cmk), 'cmr': jnp.asarray(cmk), 'Wfk': jax.random.normal(ks[5], (H, C), jnp.float32) * s, 'Wfr': jax.random.normal(ks[6], (C, C), jnp.float32) * s, 'Wfv': jax.random.normal(ks[7], (C, H), jnp.float32) * s}
    _L0_attn_in = _L0_attn_setup()

    def _L0_ffn_setup():
        import jax, jax.numpy as jnp
        import numpy as np

        def _binarize(w):
            alpha = jax.lax.stop_gradient(jnp.mean(jnp.abs(w), axis=1, keepdims=True))
            bw = alpha * jnp.sign(w)
            return w + jax.lax.stop_gradient(bw - w)
        key = jax.random.key(seed)
        k1, k2, k3, k4, k5 = jax.random.split(key, 5)
        D, H = (256, 1024)
        x = jax.random.normal(k1, (64, 196, D), dtype=jnp.float32)
        w1 = jax.random.normal(k2, (H, D), dtype=jnp.float32) * 0.02
        b1 = jax.random.normal(k3, (H,), dtype=jnp.float32) * 0.02
        w2 = jax.random.normal(k4, (D, H), dtype=jnp.float32) * 0.02
        b2 = jax.random.normal(k5, (D,), dtype=jnp.float32) * 0.02
        return {'x': x, 'w1': w1, 'b1': b1, 'w2': w2, 'b2': b2}
    _L0_ffn_in = _L0_ffn_setup()
    _L0_c = _w((lambda *s: np.random.randn(*s).astype(np.float32) * 0.05)(2, 256))
    _L0_wmod = _w((lambda *s: np.random.randn(*s).astype(np.float32) * 0.05)(256, 6 * 256) * 256 ** (-0.5))

    def _L1_attn_setup():
        import jax, jax.numpy as jnp
        import numpy as np
        B, T, D, H = (4, 512, 256, 16)
        HD = D // H
        NEG = -np.finfo(np.float32).max
        key = jax.random.key(seed)
        ks = jax.random.split(key, 9)
        s = 1.0 / np.sqrt(D)
        return {'x': jax.random.normal(ks[0], (B, T, D), jnp.float32), 'wq': jax.random.normal(ks[1], (D, D), jnp.float32) * s, 'bq': jax.random.normal(ks[2], (D,), jnp.float32) * 0.02, 'wk': jax.random.normal(ks[3], (D, D), jnp.float32) * s, 'bk': jax.random.normal(ks[4], (D,), jnp.float32) * 0.02, 'wv': jax.random.normal(ks[5], (D, D), jnp.float32) * s, 'bv': jax.random.normal(ks[6], (D,), jnp.float32) * 0.02, 'wo': jax.random.normal(ks[7], (D, D), jnp.float32) * s, 'bo': jax.random.normal(ks[8], (D,), jnp.float32) * 0.02}
    _L1_attn_in = _L1_attn_setup()

    def _L1_ffn_setup():
        import jax, jax.numpy as jnp
        import numpy as np
        B, N, D = (4, 2048, 256)
        HEADS, DH = (8, 64)
        HID = HEADS * DH
        WIN = 128
        NQ, NKV = (256, 512)
        EPS, N_ITERS, FETCH_K = (1.0, 50, 9.0 / 8.0)
        SCALE = DH ** (-0.5)

        def rmsnorm(x, gamma):
            norm = jnp.maximum(jnp.linalg.norm(x, axis=-1, keepdims=True), 1e-12)
            return x / norm * x.shape[-1] ** 0.5 * gamma

        def coor_descent(s, k):
            logk = jnp.log(jnp.asarray(k, s.dtype))

            def body(_, ab):
                a, b = ab
                a = EPS * (logk - jax.nn.logsumexp((s + b) / EPS, axis=-1, keepdims=True))
                b = -jax.nn.relu(s + a)
                return (a, b)
            a, b = jax.lax.fori_loop(0, N_ITERS, body, (jnp.zeros_like(s[..., :1]), -s))
            return jnp.exp((s + a + b) / EPS)

        def route(x, routing_token, num_tokens):
            s = jnp.einsum('bnd,d->bn', x, routing_token)
            k = min(num_tokens * FETCH_K, x.shape[1])
            scores = coor_descent(s, k)
            sel_scores, sel_idx = jax.lax.top_k(scores, num_tokens)
            sel_scores = sel_scores + jax.lax.stop_gradient(1.0 - sel_scores)
            return (sel_scores, sel_idx)

        def light_local_attn(x, gamma, wq, wkv, wo):
            b, n, d = x.shape
            xn = rmsnorm(x, gamma)
            q = xn @ wq
            k, v = jnp.split(xn @ wkv, 2, axis=-1)

            def win(t):
                return t.reshape(b, n // WIN, WIN, HEADS, DH).transpose(0, 1, 3, 2, 4)
            q, k, v = (win(q) * SCALE, win(k), win(v))
            attn = jax.nn.softmax(jnp.einsum('bwhid,bwhjd->bwhij', q, k), axis=-1)
            out = jnp.einsum('bwhij,bwhjd->bwhid', attn, v)
            out = out.transpose(0, 1, 3, 2, 4).reshape(b, n, HID)
            return out @ wo

        def heavy_attn(xq, context, scores_kv, gamma, wq, wkv_t, wo):
            b, nq, d = xq.shape
            nkv = context.shape[1]
            xqn = rmsnorm(xq, gamma)
            ctx = rmsnorm(context, gamma)[:, None]
            q = (xqn @ wq).reshape(b, nq, HEADS, DH).transpose(0, 2, 1, 3) * SCALE
            kvw = wkv_t.reshape(1, HEADS, 2 * DH, d)
            kv = jnp.einsum('rhdi,brni->brhnd', kvw, ctx)
            k, v = jnp.split(kv, 2, axis=-1)
            v = v * scores_kv[:, None, None, :, None]
            k = k.reshape(b, HEADS, nkv, DH)
            v = v.reshape(b, HEADS, nkv, DH)
            attn = jax.nn.softmax(jnp.einsum('bhid,bhjd->bhij', q, k), axis=-1)
            out = jnp.einsum('bhij,bhjd->bhid', attn, v)
            out = out.transpose(0, 2, 1, 3).reshape(b, nq, HID)
            return out @ wo
        key = jax.random.key(seed)
        ks = jax.random.split(key, 10)
        lin = lambda k, shape, fan: jax.random.normal(k, shape, jnp.float32) * fan ** (-0.5)
        return dict(x=jax.random.normal(ks[0], (B, N, D), jnp.float32), gamma_light=jnp.ones((D,), jnp.float32), wq_light=lin(ks[1], (D, HID), D), wkv_light=lin(ks[2], (D, 2 * HID), D), wo_light=lin(ks[3], (HID, D), HID), q_routing_token=jax.random.normal(ks[4], (D,), jnp.float32), kv_routing_token=jax.random.normal(ks[5], (D,), jnp.float32), gamma_heavy=jnp.ones((D,), jnp.float32), wq_heavy=lin(ks[6], (D, HID), D), wkv_heavy=lin(ks[7], (2 * HID, D), D), wo_heavy=lin(ks[8], (HID, D), HID))
    _L1_ffn_in = _L1_ffn_setup()
    _L1_c = _w((lambda *s: np.random.randn(*s).astype(np.float32) * 0.05)(2, 256))
    _L1_wmod = _w((lambda *s: np.random.randn(*s).astype(np.float32) * 0.05)(256, 6 * 256) * 256 ** (-0.5))
    _d = {'L0_attn_x': _L0_attn_in['x'], 'L0_attn_ln0_w': _L0_attn_in['ln0_w'], 'L0_attn_ln0_b': _L0_attn_in['ln0_b'], 'L0_attn_ln1_w': _L0_attn_in['ln1_w'], 'L0_attn_ln1_b': _L0_attn_in['ln1_b'], 'L0_attn_ln2_w': _L0_attn_in['ln2_w'], 'L0_attn_ln2_b': _L0_attn_in['ln2_b'], 'L0_attn_time_decay': _L0_attn_in['time_decay'], 'L0_attn_time_first': _L0_attn_in['time_first'], 'L0_attn_tmk': _L0_attn_in['tmk'], 'L0_attn_tmv': _L0_attn_in['tmv'], 'L0_attn_tmr': _L0_attn_in['tmr'], 'L0_attn_Wk': _L0_attn_in['Wk'], 'L0_attn_Wv': _L0_attn_in['Wv'], 'L0_attn_Wr': _L0_attn_in['Wr'], 'L0_attn_Wo': _L0_attn_in['Wo'], 'L0_attn_cmk': _L0_attn_in['cmk'], 'L0_attn_cmr': _L0_attn_in['cmr'], 'L0_attn_Wfk': _L0_attn_in['Wfk'], 'L0_attn_Wfr': _L0_attn_in['Wfr'], 'L0_attn_Wfv': _L0_attn_in['Wfv'], 'L0_ffn_w1': _L0_ffn_in['w1'], 'L0_ffn_b1': _L0_ffn_in['b1'], 'L0_ffn_w2': _L0_ffn_in['w2'], 'L0_ffn_b2': _L0_ffn_in['b2'], 'L0_c': _L0_c, 'L0_wmod': _L0_wmod, 'L1_attn_wq': _L1_attn_in['wq'], 'L1_attn_bq': _L1_attn_in['bq'], 'L1_attn_wk': _L1_attn_in['wk'], 'L1_attn_bk': _L1_attn_in['bk'], 'L1_attn_wv': _L1_attn_in['wv'], 'L1_attn_bv': _L1_attn_in['bv'], 'L1_attn_wo': _L1_attn_in['wo'], 'L1_attn_bo': _L1_attn_in['bo'], 'L1_ffn_gamma_light': _L1_ffn_in['gamma_light'], 'L1_ffn_wq_light': _L1_ffn_in['wq_light'], 'L1_ffn_wkv_light': _L1_ffn_in['wkv_light'], 'L1_ffn_wo_light': _L1_ffn_in['wo_light'], 'L1_ffn_q_routing_token': _L1_ffn_in['q_routing_token'], 'L1_ffn_kv_routing_token': _L1_ffn_in['kv_routing_token'], 'L1_ffn_gamma_heavy': _L1_ffn_in['gamma_heavy'], 'L1_ffn_wq_heavy': _L1_ffn_in['wq_heavy'], 'L1_ffn_wkv_heavy': _L1_ffn_in['wkv_heavy'], 'L1_ffn_wo_heavy': _L1_ffn_in['wo_heavy'], 'L1_c': _L1_c, 'L1_wmod': _L1_wmod}
    _x0 = _d['L0_attn_x']
    _d['L0_attn_x'] = jax.random.normal(jax.random.fold_in(jax.random.key(seed), 1), (2, 2048, 256), dtype=_x0.dtype)
    del _x0
    return _d

def reference(L0_attn_x, L0_attn_ln0_w, L0_attn_ln0_b, L0_attn_ln1_w, L0_attn_ln1_b, L0_attn_ln2_w, L0_attn_ln2_b, L0_attn_time_decay, L0_attn_time_first, L0_attn_tmk, L0_attn_tmv, L0_attn_tmr, L0_attn_Wk, L0_attn_Wv, L0_attn_Wr, L0_attn_Wo, L0_attn_cmk, L0_attn_cmr, L0_attn_Wfk, L0_attn_Wfr, L0_attn_Wfv, L0_ffn_w1, L0_ffn_b1, L0_ffn_w2, L0_ffn_b2, L0_c, L0_wmod, L1_attn_wq, L1_attn_bq, L1_attn_wk, L1_attn_bk, L1_attn_wv, L1_attn_bv, L1_attn_wo, L1_attn_bo, L1_ffn_gamma_light, L1_ffn_wq_light, L1_ffn_wkv_light, L1_ffn_wo_light, L1_ffn_q_routing_token, L1_ffn_kv_routing_token, L1_ffn_gamma_heavy, L1_ffn_wq_heavy, L1_ffn_wkv_heavy, L1_ffn_wo_heavy, L1_c, L1_wmod):

    def _L0_attn_ref(x, ln0_w, ln0_b, ln1_w, ln1_b, ln2_w, ln2_b, time_decay, time_first, tmk, tmv, tmr, Wk, Wv, Wr, Wo, cmk, cmr, Wfk, Wfr, Wfv):
        import jax, jax.numpy as jnp
        import numpy as np
        B, T, C = (4, 1024, 256)
        NUM_LAYERS = 24
        LAYER_ID = 0
        EPS = 1e-05

        def _ln(x, w, b):
            m = x.mean(-1, keepdims=True)
            v = x.var(-1, keepdims=True)
            return (x - m) / jnp.sqrt(v + EPS) * w + b

        def _time_shift(x):
            return jnp.pad(x, ((0, 0), (1, 0), (0, 0)))[:, :-1]

        def _wkv(w, u, k, v):

            def step(carry, kv_t):
                aa, bb, pp = carry
                kt, vt = kv_t
                ww = u + kt
                p = jnp.maximum(pp, ww)
                e1 = jnp.exp(pp - p)
                e2 = jnp.exp(ww - p)
                y = (e1 * aa + e2 * vt) / (e1 * bb + e2)
                ww2 = pp + w
                p2 = jnp.maximum(ww2, kt)
                e1 = jnp.exp(ww2 - p2)
                e2 = jnp.exp(kt - p2)
                return ((e1 * aa + e2 * vt, e1 * bb + e2, p2), y)
            Bz, Tz, Cz = k.shape
            init = (jnp.zeros((Bz, Cz), k.dtype), jnp.zeros((Bz, Cz), k.dtype), jnp.full((Bz, Cz), -1e+38, k.dtype))
            kT = jnp.swapaxes(k, 0, 1)
            vT = jnp.swapaxes(v, 0, 1)
            _, y = jax.lax.scan(step, init, (kT, vT))
            return jnp.swapaxes(y, 0, 1)
        x = _ln(x, ln0_w, ln0_b)
        h = _ln(x, ln1_w, ln1_b)
        xx = _time_shift(h)
        xk = h * tmk + xx * (1 - tmk)
        xv = h * tmv + xx * (1 - tmv)
        xr = h * tmr + xx * (1 - tmr)
        k = jnp.einsum('btc,oc->bto', xk, Wk)
        v = jnp.einsum('btc,oc->bto', xv, Wv)
        sr = jax.nn.sigmoid(jnp.einsum('btc,oc->bto', xr, Wr))
        w = -jnp.exp(time_decay)
        att = _wkv(w, time_first, k, v)
        rwkv = jnp.einsum('btc,oc->bto', sr * att, Wo)
        x = x + rwkv
        h2 = _ln(x, ln2_w, ln2_b)
        xx2 = _time_shift(h2)
        xk2 = h2 * cmk + xx2 * (1 - cmk)
        xr2 = h2 * cmr + xx2 * (1 - cmr)
        kf = jnp.einsum('btc,hc->bth', xk2, Wfk)
        kf = jnp.square(jax.nn.relu(kf))
        kv = jnp.einsum('bth,ch->btc', kf, Wfv)
        rkv = jax.nn.sigmoid(jnp.einsum('btc,oc->bto', xr2, Wfr)) * kv
        return x + rkv

    def _L0_ffn_ref(x, w1, b1, w2, b2):
        import jax, jax.numpy as jnp
        import numpy as np

        def _binarize(w):
            alpha = jax.lax.stop_gradient(jnp.mean(jnp.abs(w), axis=1, keepdims=True))
            bw = alpha * jnp.sign(w)
            return w + jax.lax.stop_gradient(bw - w)
        bw1 = _binarize(w1)
        h = jnp.einsum('bsd,hd->bsh', x, bw1) + b1
        h = jax.nn.gelu(h, approximate=False)
        bw2 = _binarize(w2)
        out = jnp.einsum('bsh,dh->bsd', h, bw2) + b2
        return out

    def _L1_attn_ref(x, wq, bq, wk, bk, wv, bv, wo, bo):
        import jax, jax.numpy as jnp
        import numpy as np
        B, T, D, H = (4, 512, 256, 16)
        HD = D // H
        NEG = -np.finfo(np.float32).max
        b, t, d = x.shape

        def proj(w, bias):
            y = x @ w + bias
            return y.reshape(b, t, H, HD).transpose(0, 2, 1, 3)
        q = proj(wq, bq)
        k = proj(wk, bk)
        v = proj(wv, bv)
        scale = 1.0 / np.sqrt(HD).astype(np.float32)
        scores = jnp.einsum('bhqd,bhkd->bhqk', q, k) * scale
        mask = jnp.triu(jnp.full((t, t), NEG, jnp.float32), k=1)
        attn = jax.nn.softmax(scores + mask, axis=-1)
        out = jnp.einsum('bhqk,bhkd->bhqd', attn, v)
        out = out.transpose(0, 2, 1, 3).reshape(b, t, d)
        return out @ wo + bo

    def _L1_ffn_ref(x, gamma_light, wq_light, wkv_light, wo_light, q_routing_token, kv_routing_token, gamma_heavy, wq_heavy, wkv_heavy, wo_heavy):
        import jax, jax.numpy as jnp
        import numpy as np
        B, N, D = (4, 2048, 256)
        HEADS, DH = (8, 64)
        HID = HEADS * DH
        WIN = 128
        NQ, NKV = (256, 512)
        EPS, N_ITERS, FETCH_K = (1.0, 50, 9.0 / 8.0)
        SCALE = DH ** (-0.5)

        def rmsnorm(x, gamma):
            norm = jnp.maximum(jnp.linalg.norm(x, axis=-1, keepdims=True), 1e-12)
            return x / norm * x.shape[-1] ** 0.5 * gamma

        def coor_descent(s, k):
            logk = jnp.log(jnp.asarray(k, s.dtype))

            def body(_, ab):
                a, b = ab
                a = EPS * (logk - jax.nn.logsumexp((s + b) / EPS, axis=-1, keepdims=True))
                b = -jax.nn.relu(s + a)
                return (a, b)
            a, b = jax.lax.fori_loop(0, N_ITERS, body, (jnp.zeros_like(s[..., :1]), -s))
            return jnp.exp((s + a + b) / EPS)

        def route(x, routing_token, num_tokens):
            s = jnp.einsum('bnd,d->bn', x, routing_token)
            k = min(num_tokens * FETCH_K, x.shape[1])
            scores = coor_descent(s, k)
            sel_scores, sel_idx = jax.lax.top_k(scores, num_tokens)
            sel_scores = sel_scores + jax.lax.stop_gradient(1.0 - sel_scores)
            return (sel_scores, sel_idx)

        def light_local_attn(x, gamma, wq, wkv, wo):
            b, n, d = x.shape
            xn = rmsnorm(x, gamma)
            q = xn @ wq
            k, v = jnp.split(xn @ wkv, 2, axis=-1)

            def win(t):
                return t.reshape(b, n // WIN, WIN, HEADS, DH).transpose(0, 1, 3, 2, 4)
            q, k, v = (win(q) * SCALE, win(k), win(v))
            attn = jax.nn.softmax(jnp.einsum('bwhid,bwhjd->bwhij', q, k), axis=-1)
            out = jnp.einsum('bwhij,bwhjd->bwhid', attn, v)
            out = out.transpose(0, 1, 3, 2, 4).reshape(b, n, HID)
            return out @ wo

        def heavy_attn(xq, context, scores_kv, gamma, wq, wkv_t, wo):
            b, nq, d = xq.shape
            nkv = context.shape[1]
            xqn = rmsnorm(xq, gamma)
            ctx = rmsnorm(context, gamma)[:, None]
            q = (xqn @ wq).reshape(b, nq, HEADS, DH).transpose(0, 2, 1, 3) * SCALE
            kvw = wkv_t.reshape(1, HEADS, 2 * DH, d)
            kv = jnp.einsum('rhdi,brni->brhnd', kvw, ctx)
            k, v = jnp.split(kv, 2, axis=-1)
            v = v * scores_kv[:, None, None, :, None]
            k = k.reshape(b, HEADS, nkv, DH)
            v = v.reshape(b, HEADS, nkv, DH)
            attn = jax.nn.softmax(jnp.einsum('bhid,bhjd->bhij', q, k), axis=-1)
            out = jnp.einsum('bhij,bhjd->bhid', attn, v)
            out = out.transpose(0, 2, 1, 3).reshape(b, nq, HID)
            return out @ wo
        b = x.shape[0]
        light_out = light_local_attn(x, gamma_light, wq_light, wkv_light, wo_light)
        scores_q, idx_q = route(x, q_routing_token, NQ)
        scores_kv, idx_kv = route(x, kv_routing_token, NKV)
        routed_q = jnp.take_along_axis(x, idx_q[..., None], axis=1)
        routed_kv = jnp.take_along_axis(x, idx_kv[..., None], axis=1)
        routed_out = heavy_attn(routed_q, routed_kv, scores_kv, gamma_heavy, wq_heavy, wkv_heavy, wo_heavy)
        routed_out = routed_out * scores_q[..., None]
        heavy_out = jnp.zeros_like(x).at[jnp.arange(b)[:, None], idx_q].set(routed_out)
        return light_out + heavy_out
    x = L0_attn_x
    mod = (_silu(L0_c) @ L0_wmod).reshape(L0_c.shape[0], 6, 1, -1)
    sa, ca, ga, sb, cb, gb = (mod[:, 0], mod[:, 1], mod[:, 2], mod[:, 3], mod[:, 4], mod[:, 5])
    ga = (2 * (ga >= 0) - 1) * jnp.maximum(jnp.abs(ga), 0.25)
    gb = (2 * (gb >= 0) - 1) * jnp.maximum(jnp.abs(gb), 0.25)
    h = _layernorm(x, axis=-1) * (1 + ca) + sa
    x = x + ga * _L0_attn_ref(h, L0_attn_ln0_w, L0_attn_ln0_b, L0_attn_ln1_w, L0_attn_ln1_b, L0_attn_ln2_w, L0_attn_ln2_b, L0_attn_time_decay, L0_attn_time_first, L0_attn_tmk, L0_attn_tmv, L0_attn_tmr, L0_attn_Wk, L0_attn_Wv, L0_attn_Wr, L0_attn_Wo, L0_attn_cmk, L0_attn_cmr, L0_attn_Wfk, L0_attn_Wfr, L0_attn_Wfv)
    h = _layernorm(x, axis=-1) * (1 + cb) + sb
    x = x + gb * _L0_ffn_ref(h, L0_ffn_w1, L0_ffn_b1, L0_ffn_w2, L0_ffn_b2)
    mod = (_silu(L1_c) @ L1_wmod).reshape(L1_c.shape[0], 6, 1, -1)
    sa, ca, ga, sb, cb, gb = (mod[:, 0], mod[:, 1], mod[:, 2], mod[:, 3], mod[:, 4], mod[:, 5])
    ga = (2 * (ga >= 0) - 1) * jnp.maximum(jnp.abs(ga), 0.25)
    gb = (2 * (gb >= 0) - 1) * jnp.maximum(jnp.abs(gb), 0.25)
    h = _layernorm(x, axis=-1) * (1 + ca) + sa
    x = x + ga * _L1_attn_ref(h, L1_attn_wq, L1_attn_bq, L1_attn_wk, L1_attn_bk, L1_attn_wv, L1_attn_bv, L1_attn_wo, L1_attn_bo)
    h = _layernorm(x, axis=-1) * (1 + cb) + sb
    x = x + gb * _L1_ffn_ref(h, L1_ffn_gamma_light, L1_ffn_wq_light, L1_ffn_wkv_light, L1_ffn_wo_light, L1_ffn_q_routing_token, L1_ffn_kv_routing_token, L1_ffn_gamma_heavy, L1_ffn_wq_heavy, L1_ffn_wkv_heavy, L1_ffn_wo_heavy)
    return x

_drawn_inputs = setup_inputs


def setup_inputs(seed=0):
    import zlib

    import numpy as np

    out = dict(_drawn_inputs(seed))
    spreads = {'L0_attn_ln0_w': (1.0, 0.2),
     'L0_attn_ln0_b': (0.0, 0.338),
     'L0_attn_ln1_w': (1.0, 0.6),
     'L0_attn_ln1_b': (0.0, 0.8),
     'L0_attn_ln2_w': (1.0, 0.6),
     'L0_attn_ln2_b': (0.0, 0.8),
     'L1_ffn_gamma_light': (1.0, 0.6),
     'L1_ffn_gamma_heavy': (1.0, 0.6)}
    factors = {'L0_attn_time_decay': 8.0,
     'L0_attn_time_first': 8.0,
     'L0_attn_tmk': 8.0,
     'L0_attn_tmv': 8.0,
     'L0_attn_tmr': 8.0,
     'L0_attn_Wk': 8.0,
     'L0_attn_Wv': 7.931,
     'L0_attn_Wr': 8.0,
     'L0_attn_Wo': 7.923,
     'L0_attn_cmk': 8.0,
     'L0_attn_cmr': 8.0,
     'L0_attn_Wfk': 8.0,
     'L0_attn_Wfr': 8.0,
     'L0_attn_Wfv': 7.205,
     'L0_ffn_w1': 26.664,
     'L0_ffn_b1': 64.0,
     'L0_ffn_w2': 25.384,
     'L0_ffn_b2': 64.0,
     'L1_attn_bq': 64.0,
     'L1_attn_bk': 64.0,
     'L1_attn_bv': 64.0,
     'L1_attn_bo': 64.0,
     'L1_ffn_q_routing_token': 40.616,
     'L1_ffn_kv_routing_token': 49.888,
     'L1_ffn_wq_heavy': 48.768,
     'L1_ffn_wkv_heavy': 37.184,
     'L1_ffn_wo_heavy': 37.592,
     'L1_attn_wq': 8.0,
     'L1_attn_wk': 8.0,
     'L1_attn_wv': 8.0,
     'L1_attn_wo': 8.0,
     'L1_ffn_wq_light': 8.0,
     'L1_ffn_wkv_light': 8.0,
     'L1_ffn_wo_light': 8.0,
     'L1_c': 8.0,
     'L1_wmod': 8.0}
    for name, (base, spread) in spreads.items():
        noise = np.random.default_rng([zlib.crc32(name.encode()), seed]).standard_normal(out[name].shape)
        drawn = base * np.exp(spread * noise) if base else spread * noise
        out[name] = jnp.asarray(drawn.astype(out[name].dtype))
    for name, factor in factors.items():
        out[name] = (out[name] * factor).astype(out[name].dtype)
    return out
```

```python
import math
from contextlib import ExitStack

import numpy as np
import concourse.bass as bass
from concourse import mybir

F32 = mybir.dt.float32
BF16 = mybir.dt.bfloat16
I32 = mybir.dt.int32
ALU = mybir.AluOpType
ACT = mybir.ActivationFunctionType
AX = mybir.AxisListType

P = 128
B = 2
T = 2048
D = 256
KD = D // P
NT = B * T // P
TT = T // P
CH = 512
CT = CH // P
NC = T // CH
H = 1024
KH = H // P
EPS = 1e-5
SHIFT, SCALE, GATE = 0, 1, 2
NEG = -1.0e30


class Kit:

    def __init__(self, nc, ins, ctx):
        self.nc, self.ins, self.ctx = nc, ins, ctx
        self.begun = ctx.enter_context(nc.semaphore("begun"))


def take(eng, sem, n=1):
    eng.wait_ge(sem, n)
    eng.sem_inc(sem, -n)


class Room:

    def __init__(self, nc, name):
        self.nc, self.name, self.stack, self.sems = nc, name, ExitStack(), []

    def __enter__(self):
        self.stack.__enter__()
        return self

    def __exit__(self, *a):
        if self.sems and a[0] is None:
            self.nc.clear_and_free_semaphores(self.sems)
            self.nc.all_engine_barrier()
        return self.stack.__exit__(*a)

    def sb(self, name, shape, dt=F32):
        return self.stack.enter_context(self.nc.sbuf_tensor(f"{self.name}_{name}", shape, dt))

    def ps(self, name, shape, dt=F32):
        return self.stack.enter_context(self.nc.psum_tensor(f"{self.name}_{name}", shape, dt))

    def sem(self, name):
        self.sems.append(self.nc.alloc_semaphore(name=f"{self.name}_{name}"))
        return self.sems[-1]


class Chain:

    def __init__(self, eng, sem):
        self.eng, self.sem = eng, sem

    def link(self, ins):
        ins.then_inc(self.sem, 1)
        take(self.eng, self.sem)


def flat(ap):
    return ap.rearrange("p a b -> p (a b)")


def row4(row, n=CT):
    return row.unsqueeze(1).broadcast_to([row.shape[0], n, row.shape[1]])


def phase_modulation(kit, S):
    nc, ins = kit.nc, kit.ins
    with Room(nc, "mod") as r:
        cT = r.sb("cT", [P, 2, KD, B])
        silu_c = r.sb("silu_c", [P, 2, KD, B])
        wmod = r.sb("wmod", [P, 2, KD, 6 * D])
        ones = r.sb("ones", [P, P])
        rep = r.sb("rep", [P, 2 * KD * B, P])
        t1 = r.sb("t1", [P, 4, 2 * D])
        t2 = r.sb("t2", [P, 4, 2 * D])
        ps = r.ps("ps", [P, 4, 512])
        psc = r.ps("psc", [P, 32])
        loaded, silu_done, rep_done = r.sem("loaded"), r.sem("silu_done"), r.sem("rep_done")
        mm_done, evac_done, cols_done, steps = (r.sem("mm_done"), r.sem("evac_done"),
                                                r.sem("cols_done"), r.sem("steps"))
        rows, cols = S["rows"], S["cols"]
        with nc.Block() as block:
            @block.sync
            def _(sp):
                for l in range(2):
                    sp.dma_start(cT[:, l], ins[f"cT{l}"].rearrange("(k p) b -> p k b", p=P)).then_inc(loaded, 16)
                    sp.dma_start(wmod[:, l], ins[f"L{l}_wmod"].rearrange("(k p) n -> p k n", p=P)).then_inc(loaded, 16)

            @block.scalar
            def _(act):
                act.wait_ge(loaded, 64)
                act.activation(silu_c[:], cT[:], ACT.Silu).then_inc(silu_done, 1)

            @block.vector
            def _(dve):
                dve.memset(ones[:], 1.0).then_inc(kit.begun, 1)
                dve.wait_ge(kit.begun, 1)
                dve.wait_ge(silu_done, 1)
                sc = silu_c[:].rearrange("p l k b -> p (l k b)")
                for n in range(2 * KD * B):
                    last = dve.tensor_scalar(rep[:, n], ones[:], sc[:, n:n + 1], None, ALU.mult)
                last.then_inc(rep_done, 1)
                for n in range(12):
                    l, b, m = n // 6, n // 3 % 2, n % 3
                    dve.wait_ge(mm_done, n + 1)
                    dve.tensor_copy(rows[:, l, b, 512 * m:512 * m + 512], ps[:, n % 4]).then_inc(evac_done, 1)
                dve.wait_ge(evac_done, 12)
                n = 0
                for l in range(2):
                    for tr in range(2):
                        sc_row = rows[:, l, :, (3 * tr + SCALE) * D:(3 * tr + SCALE + 1) * D]
                        dve.tensor_scalar(sc_row, sc_row, 1.0, None, ALU.add)
                for l in range(2):
                    for tr in range(2):
                        g = rows[:, l, :, (3 * tr + GATE) * D:(3 * tr + GATE + 1) * D]
                        v = t1[:, 2 * l + tr].rearrange("p (b n) -> p b n", b=2)
                        w = t2[:, 2 * l + tr].rearrange("p (b n) -> p b n", b=2)
                        dve.tensor_scalar(v, g, 0.0, 2.0, ALU.is_ge, ALU.mult).then_inc(steps, 1)
                        dve.scalar_tensor_tensor(w, g, -1.0, g, ALU.mult, ALU.max).then_inc(steps, 1)
                        n += 2
                        dve.wait_ge(steps, n)
                        dve.tensor_scalar(v, v, -1.0, None, ALU.add).then_inc(steps, 1)
                        n += 1
                        dve.wait_ge(steps, n)
                        dve.scalar_tensor_tensor(g, w, 0.25, v, ALU.max, ALU.mult)
                dve.wait_ge(cols_done, 1)
                pc = psc[:, 0:16].rearrange("p (l m k b) -> p l m k b", l=2, m=2, k=2)
                dve.tensor_copy(cols[:, :, 0], pc[:, :, 0])
                dve.tensor_scalar(cols[:, :, 1], pc[:, :, 1], 1.0, None, ALU.add)

            @block.tensor
            def _(pe):
                pe.wait_ge(rep_done, 1)
                n = 0
                for l in range(2):
                    for b in range(B):
                        for m in range(3):
                            if n >= 4:
                                pe.wait_ge(evac_done, n - 3)
                            for k in range(KD):
                                mm = pe.matmul(ps[:, n % 4], rep[:, (l * KD + k) * B + b],
                                               wmod[:, l, k, 512 * m:512 * m + 512],
                                               start=(k == 0), stop=(k == KD - 1))
                            mm.then_inc(mm_done, 1)
                            n += 1
                for l in range(2):
                    for m in range(2):
                        for h in range(KD):
                            at = (3 * (1 - l) + m) * D + h * P
                            o = ((l * 2 + m) * KD + h) * B
                            for k in range(KD):
                                mm = pe.matmul(psc[:, o:o + B], wmod[:, l, k, at:at + P], silu_c[:, l, k],
                                               start=(k == 0), stop=(k == KD - 1))
                mm.then_inc(cols_done, 1)


class Norm:

    def __init__(self, r, name=""):
        self.st = r.sb(name + "st", [P, B, CT, 6])
        self.mv = r.sb(name + "mv", [P, B, CT, 2])
        self.rs = r.sb(name + "rs", [P, B, CT])
        self.eps = r.sb(name + "eps", [P, 1])
        self.mean_ready, self.root_ready = r.sem(name + "mean_ready"), r.sem(name + "root_ready")

    def stats(self, dve, chain, s, src, src_ready=None):
        for j in range(CT):
            last = dve.bn_stats(self.st[:, s, j], src[:, j])
            if j == 0 and src_ready is not None:
                last.then_inc(src_ready, 1)
        chain.link(last)
        for j in range(CT):
            last = dve.bn_aggr(self.mv[:, s, j], self.st[:, s, j])
        last.then_inc(self.mean_ready, 1)

    def stats_at(self, dve, chain, s, x, at):
        for j in range(CT):
            last = dve.bn_stats(self.st[:, s, j], flat(x[:, bass.ds(at + j, 1)]))
        chain.link(last)
        for j in range(CT):
            last = dve.bn_aggr(self.mv[:, s, j], self.st[:, s, j])
        last.then_inc(self.mean_ready, 1)

    def apply_at(self, dve, chain, s, out, x, at):
        take(dve, self.root_ready)
        chain.link(dve.reciprocal(self.rs[:, s], self.rs[:, s]))
        for j in range(CT):
            last = dve.tensor_scalar(out[:, j:j + 1], x[:, bass.ds(at + j, 1)], self.mv[:, s, j, 0:1],
                                     self.rs[:, s, j:j + 1], ALU.subtract, ALU.mult)
        return last

    def root(self, act, s):
        take(act, self.mean_ready)
        act.activation(self.rs[:, s], self.mv[:, s, :, 1], ACT.Sqrt, bias=self.eps[:]).then_inc(self.root_ready, 1)

    def apply(self, dve, chain, s, out, src):
        take(dve, self.root_ready)
        chain.link(dve.reciprocal(self.rs[:, s], self.rs[:, s]))
        for j in range(CT):
            last = dve.tensor_scalar(out[:, j], src[:, j], self.mv[:, s, j, 0:1], self.rs[:, s, j:j + 1],
                                     ALU.subtract, ALU.mult)
        return last


def transposes(pe, out, src, ident):
    for h in range(KD):
        for j in range(CT):
            last = pe.transpose(out[:, h, j * P:(j + 1) * P], src[:, j, h * P:(h + 1) * P], ident)
    return last


def phase_norms(kit, S):
    nc, ins = kit.nc, kit.ins
    x0, hT, rows, ident = S["x0"], S["hT"], S["rows"], S["ident"]
    with Room(nc, "nrm") as r:
        xin = r.sb("xin", [P, B, CT, D])
        w = r.sb("w", [P, B, CT, D])
        n3 = r.sb("n3", [P, B, CT, D])
        ln0 = r.sb("ln0", [P, 2, D])
        lncol = S["lncol"]
        pT = r.ps("pT", [P, B, KD, CH])
        loads, x_in, x_used = r.sem("loads"), [r.sem("x_in0"), r.sem("x_in1")], r.sem("x_used")
        steps, zeroed = r.sem("steps"), r.sem("zeroed")
        n3_free, n3_ready, turned, h_ready = r.sem("n3_free"), r.sem("n3_ready"), r.sem("turned"), r.sem("h_ready")
        norm = Norm(r)
        x_d = ins["x"].rearrange("(s c j p) d -> s c p j d", s=B, c=NC, p=P)
        with nc.Block() as block:
            @block.sync
            def _(sp):
                sp.dma_start(ident[:], ins["ident"]).then_inc(loads, 16)
                for n, name in enumerate(("ln0_w", "ln0_b")):
                    sp.dma_start(ln0[:, n], ins[name].partition_broadcast(P)).then_inc(loads, 16)
                sp.dma_start(lncol[:], ins["lncol"]).then_inc(loads, 16)
                with sp.Fori(0, NC) as i:
                    for s in range(B):
                        take(sp, x_used)
                        sp.dma_start(xin[:, s], x_d[s, bass.ds(i, 1)].rearrange("a p j d -> p (a j) d")).then_inc(x_in[s], 16)

            @block.gpsimd
            def _(pool):
                pool.memset(hT[:, :, :, 0:1], 0.0).then_inc(zeroed, 1)

            @block.vector
            def _(dve):
                dve.wait_ge(loads, 64)
                dve.memset(norm.eps[:], EPS).then_inc(zeroed, 1)
                dve.sem_inc(x_used, 2)
                dve.sem_inc(n3_free, 2)
                with dve.Fori(0, NC) as i:
                    c = Chain(dve, steps)
                    for s in range(B):
                        take(dve, x_in[s], 16)
                        norm.stats(dve, c, s, xin[:, s])
                    for s in range(B):
                        c.link(norm.apply(dve, c, s, w[:, s], xin[:, s]))
                        c.link(dve.tensor_tensor(w[:, s], w[:, s], row4(rows[:, 0, s, SCALE * D:(SCALE + 1) * D]), ALU.mult))
                        c.link(dve.tensor_tensor(w[:, s], w[:, s], row4(rows[:, 0, s, SHIFT * D:(SHIFT + 1) * D]), ALU.add))
                        norm.stats(dve, c, s, w[:, s], x_used)
                    for s in range(B):
                        c.link(norm.apply(dve, c, s, w[:, s], w[:, s]))
                        c.link(dve.tensor_tensor(w[:, s], w[:, s], row4(ln0[:, 0]), ALU.mult))
                        x0c = x0[:, bass.ds(i * CT + s * TT, CT)]
                        c.link(dve.tensor_tensor(x0c, w[:, s], row4(ln0[:, 1]), ALU.add))
                        norm.stats_at(dve, c, s, x0, i * CT + s * TT)
                    for s in range(B):
                        take(dve, n3_free)
                        norm.apply_at(dve, c, s, n3[:, s], x0, i * CT + s * TT).then_inc(n3_ready, 1)

            @block.tensor
            def _(pe):
                pe.wait_ge(loads, 64)
                with pe.Fori(0, NC) as i:
                    for s in range(B):
                        take(pe, h_ready)
                        take(pe, n3_ready)
                        transposes(pe, pT[:, s], n3[:, s], ident[:]).then_inc(turned, 1)

            @block.scalar
            def _(act):
                act.wait_ge(loads, 64)
                act.wait_ge(zeroed, 2)
                act.sem_inc(h_ready, 2)
                with act.Fori(0, NC) as i:
                    for n in range(3):
                        for s in range(B):
                            norm.root(act, s)
                    for s in range(B):
                        take(act, turned)
                        for h in range(KD):
                            last = act.activation(hT[:, h, s, bass.ds(i * CH + 1, CH)], pT[:, s, h], ACT.Identity,
                                                  scale=lncol[:, 0, h:h + 1], bias=lncol[:, 1, h:h + 1])
                            if h == 0:
                                last.then_inc(n3_free, 1)
                        last.then_inc(h_ready, 1)


def phase_wkv(kit, S):
    nc, ins = kit.nc, kit.ins
    hT, yT = S["hT"], S["hT"]
    with Room(nc, "wkv") as r:
        W = r.sb("W", [P, 3, KD, D])
        tm = r.sb("tm", [P, 3, KD])
        omt = r.sb("omt", [P, 3, KD])
        uw = r.sb("uw", [P, 2, KD])
        xm = r.sb("xm", [P, B, 3, KD, CH])
        kv = r.sb("kv", [P, B, 2, KD, CH])
        sr = r.sb("sr", [P, B, KD, CH])
        pp = r.sb("pp", [P, B, KD, CH + 1])
        aa = r.sb("aa", [P, B, KD, CH + 1])
        bb = r.sb("bb", [P, B, KD, CH + 1])
        pm = r.sb("pm", [P, KD, CH])
        ex = r.sb("ex", [P, B, 4, KD, CH])
        ps = r.ps("ps", [P, 3, KD, CH])
        loads, consts, a_ready, xm_ready = r.sem("loads"), r.sem("consts"), r.sem("a_ready"), r.sem("xm_ready")
        proj_done, kv_ready, ex_ready, e_ready = r.sem("proj_done"), r.sem("kv_ready"), r.sem("ex_ready"), r.sem("e_ready")
        y_ready, steps, ps_free = r.sem("y_ready"), r.sem("steps"), r.sem("ps_free")

        def halves(t):
            return t.rearrange("p h n -> p (h n)")

        with nc.Block() as block:
            @block.sync
            def _(sp):
                for n, name in enumerate(("WkT", "WvT", "WrT")):
                    sp.dma_start(W[:, n], ins[name].rearrange("(k p) n -> p k n", p=P)).then_inc(loads, 16)
                sp.dma_start(tm[:], ins["tmcol"]).then_inc(loads, 16)
                sp.dma_start(uw[:], ins["uwcol"]).then_inc(loads, 16)

            @block.scalar
            def _(act):
                act.wait_ge(loads, 80)
                act.activation(uw[:, 1], uw[:, 1], ACT.Exp).then_inc(consts, 1)
                act.wait_ge(consts, 5)
                with act.Fori(0, NC) as i:
                    for s in range(B):
                        for n in range(3):
                            for h in range(KD):
                                last = act.activation(xm[:, s, n, h], hT[:, h, s, bass.ds(i * CH, CH)],
                                                      ACT.Copy, scale=omt[:, n, h:h + 1])
                        last.then_inc(a_ready, 1)
                    for s in range(B):
                        take(act, proj_done)
                        take(act, y_ready)
                        for n in range(2):
                            for h in range(KD):
                                act.activation(kv[:, s, n, h], ps[:, n, h], ACT.Copy)
                        for h in range(KD):
                            last = act.activation(sr[:, s, h], ps[:, 2, h], ACT.Sigmoid)
                        last.then_inc(kv_ready, 1)
                    for s in range(B):
                        take(act, ex_ready)
                        ee = ex[:, s].rearrange("p a h n -> p (a h n)")
                        act.activation(ee, ee, ACT.Exp).then_inc(e_ready, 1)

            @block.tensor
            def _(pe):
                pe.wait_ge(loads, 80)
                pe.wait_ge(consts, 5)
                with pe.Fori(0, NC) as i:
                    for s in range(B):
                        take(pe, xm_ready)
                        take(pe, ps_free)
                        for n in range(3):
                            for o in range(KD):
                                for k in range(KD):
                                    mm = pe.matmul(ps[:, n, o], W[:, n, k, o * P:(o + 1) * P], xm[:, s, n, k],
                                                   start=(k == 0), stop=(k == KD - 1))
                        mm.then_inc(proj_done, 1)

            @block.vector
            def _(dve):
                dve.wait_ge(consts, 1)
                dve.tensor_scalar(uw[:, 1], uw[:, 1], -1.0, None, ALU.mult).then_inc(consts, 1)
                dve.tensor_scalar(omt[:], tm[:], -1.0, 1.0, ALU.mult, ALU.add).then_inc(consts, 1)
                dve.memset(pp[:, :, :, 0:1], -1e38)
                dve.memset(aa[:, :, :, 0:1], 0.0)
                dve.memset(bb[:, :, :, 0:1], 0.0).then_inc(consts, 1)
                dve.sem_inc(y_ready, 2)
                dve.sem_inc(ps_free, 1)
                dve.wait_ge(consts, 4)
                dve.sem_inc(consts, 1)
                with dve.Fori(0, NC) as i:
                    c = Chain(dve, steps)
                    for s in range(B):
                        take(dve, a_ready)
                        for n in range(3):
                            for h in range(KD):
                                last = dve.scalar_tensor_tensor(xm[:, s, n, h], hT[:, h, s, bass.ds(i * CH + 1, CH)],
                                                                tm[:, n, h:h + 1], xm[:, s, n, h], ALU.mult, ALU.add)
                        last.then_inc(xm_ready, 1)
                    for s in range(B):
                        take(dve, kv_ready)
                        k_t, v_t = kv[:, s, 0], kv[:, s, 1]
                        now, old = pp[:, s, :, 1:CH + 1], pp[:, s, :, 0:CH]
                        for h in range(KD):
                            last = dve.tensor_tensor_scan(pp[:, s, h, 1:CH + 1], uw[:, 1, h:h + 1].broadcast_to([P, CH]),
                                                          kv[:, s, 0, h], pp[:, s, h, 0:1], ALU.add, ALU.max)
                            if h == 0:
                                last.then_inc(ps_free, 1)
                        c.link(last)
                        for h in range(KD):
                            dve.scalar_tensor_tensor(ex[:, s, 0, h], pp[:, s, h, 0:CH], uw[:, 1, h:h + 1],
                                                     pp[:, s, h, 1:CH + 1], ALU.add, ALU.subtract)
                            last = dve.scalar_tensor_tensor(pm[:, h], kv[:, s, 0, h], uw[:, 0, h:h + 1],
                                                            pp[:, s, h, 0:CH], ALU.add, ALU.max)
                        c.link(last)
                        dve.tensor_tensor(ex[:, s, 1], k_t, now, ALU.subtract)
                        dve.tensor_tensor(ex[:, s, 2], old, pm[:], ALU.subtract)
                        for h in range(KD):
                            last = dve.scalar_tensor_tensor(ex[:, s, 3, h], kv[:, s, 0, h], uw[:, 0, h:h + 1],
                                                            pm[:, h], ALU.add, ALU.subtract)
                        last.then_inc(ex_ready, 1)
                    for s in range(B):
                        v_t = kv[:, s, 1]
                        take(dve, e_ready)
                        k_v = kv[:, s, 0]
                        c.link(dve.tensor_tensor(k_v, ex[:, s, 1], v_t, ALU.mult))
                        for h in range(KD):
                            dve.tensor_tensor_scan(aa[:, s, h, 1:CH + 1], ex[:, s, 0, h], kv[:, s, 0, h],
                                                   aa[:, s, h, 0:1], ALU.mult, ALU.add)
                            last = dve.tensor_tensor_scan(bb[:, s, h, 1:CH + 1], ex[:, s, 0, h], ex[:, s, 1, h],
                                                          bb[:, s, h, 0:1], ALU.mult, ALU.add)
                        c.link(last)
                        f = ex[:, s, 3]
                        dve.tensor_tensor(k_v, ex[:, s, 2], aa[:, s, :, 0:CH], ALU.mult)
                        dve.tensor_tensor(v_t, f, v_t, ALU.mult)
                        c.link(dve.tensor_tensor(ex[:, s, 1], ex[:, s, 2], bb[:, s, :, 0:CH], ALU.mult))
                        dve.tensor_tensor(k_v, k_v, v_t, ALU.add)
                        c.link(dve.tensor_tensor(ex[:, s, 1], ex[:, s, 1], f, ALU.add))
                        dve.tensor_tensor(k_v, k_v, sr[:, s], ALU.mult)
                        c.link(dve.reciprocal(ex[:, s, 1], ex[:, s, 1]))
                        c.link(dve.tensor_tensor(yT[:, :, s, bass.ds(i * CH, CH)], k_v, ex[:, s, 1], ALU.mult))
                        for t in (pp, aa, bb):
                            last = dve.tensor_copy(t[:, s, :, 0:1], t[:, s, :, CH:CH + 1])
                        dve.drain().then_inc(y_ready, 1)


def phase_channel_mix(kit, S):
    nc, ins = kit.nc, kit.ins
    x0, hT, rows, ident = S["x0"], S["hT"], S["rows"], S["ident"]
    with Room(nc, "cmx") as r:
        Wo = r.sb("Wo", [P, KD, D])
        Wfk = r.sb("Wfk", [P, KD, H])
        Wfv = r.sb("Wfv", [P, KH, D])
        Wfr = r.sb("Wfr", [P, KD, D])
        ln2 = r.sb("ln2", [P, 2, KD])
        cm = r.sb("cm", [P, 2, KD])
        omc = r.sb("omc", [P, 2, KD])
        xin = r.sb("xin", [P, B, CT, D])
        yc = r.sb("yc", [P, B, KD, CH])
        x1 = r.sb("x1", [P, B, CT, D])
        n2 = r.sb("n2", [P, B, CT, D])
        h2T = r.sb("h2T", [P, B, KD, CH + 1])
        xm = r.sb("xm", [P, B, 2, KD, CH])
        kf = r.sb("kf", [P, B, KH, CH])
        sg = r.sb("sg", [P, B, CT, D])
        norm = Norm(r)
        pA = r.ps("pA", [P, CT, D])
        pT = r.ps("pT", [P, KD, CH])
        pF = r.ps("pF", [P, 2, CH])
        pO = r.ps("pO", [P, 2, 512])
        loads, consts, x_in, x_free = r.sem("loads"), r.sem("consts"), [r.sem("x_in0"), r.sem("x_in1")], r.sem("x_free")
        y_ready, wo_done, pA_free = r.sem("y_ready"), r.sem("wo_done"), r.sem("pA_free")
        n_ready, turned, t_free = r.sem("n_ready"), r.sem("turned"), r.sem("t_free")
        a_steps, a_ready, xm_ready = r.sem("a_steps"), r.sem("a_ready"), r.sem("xm_ready")
        fk_done, relu_ready, fk_free, kf_ready = r.sem("fk_done"), r.sem("relu_ready"), r.sem("fk_free"), r.sem("kf_ready")
        r_done, kv_done, o_free, sg_ready = r.sem("r_done"), r.sem("kv_done"), r.sem("o_free"), r.sem("sg_ready")
        steps = r.sem("steps")
        x_d = ins["x"].rearrange("(s c j p) d -> s c p j d", s=B, c=NC, p=P)
        with nc.Block() as block:
            @block.sync
            def _(sp):
                for w, name in ((Wo, "WoT"), (Wfk, "WfkT"), (Wfv, "WfvT"), (Wfr, "WfrT")):
                    sp.dma_start(w[:], ins[name].rearrange("(k p) n -> p k n", p=P)).then_inc(loads, 16)
                sp.dma_start(ln2[:], ins["ln2col"]).then_inc(loads, 16)
                sp.dma_start(cm[:], ins["cmcol"]).then_inc(loads, 16)
                with sp.Fori(0, NC) as i:
                    for s in range(B):
                        take(sp, x_free)
                        sp.dma_start(xin[:, s], x_d[s, bass.ds(i, 1)].rearrange("a p j d -> p (a j) d")).then_inc(x_in[s], 16)

            @block.scalar
            def _(act):
                act.wait_ge(loads, 96)
                act.wait_ge(consts, 1)
                c = Chain(act, a_steps)
                with act.Fori(0, NC) as i:
                    for s in range(B):
                        for h in range(KD):
                            last = act.activation(yc[:, s, h], hT[:, h, s, bass.ds(i * CH, CH)], ACT.Copy)
                        last.then_inc(y_ready, 1)
                    for s in range(B):
                        norm.root(act, s)
                    for s in range(B):
                        take(act, turned)
                        c.link(act.activation(h2T[:, s, :, 0:1], h2T[:, s, :, CH:CH + 1], ACT.Copy))
                        for h in range(KD):
                            last = act.activation(h2T[:, s, h, 1:CH + 1], pT[:, h], ACT.Identity,
                                                  scale=ln2[:, 0, h:h + 1], bias=ln2[:, 1, h:h + 1])
                        c.link(last)
                        for n in range(2):
                            for h in range(KD):
                                last = act.activation(xm[:, s, n, h], h2T[:, s, h, 0:CH], ACT.Copy, scale=omc[:, n, h:h + 1])
                                if n == h == 0:
                                    last.then_inc(t_free, 1)
                        last.then_inc(a_ready, 1)
                    for s in range(B):
                        for o in range(KH):
                            take(act, fk_done)
                            act.activation(kf[:, s, o], pF[:, o % 2], ACT.Relu).then_inc(relu_ready, 1)
                    for s in range(B):
                        take(act, r_done)
                        act.activation(sg[:, s], pA[:], ACT.Sigmoid).then_inc(sg_ready, 1)

            @block.tensor
            def _(pe):
                pe.wait_ge(loads, 96)
                pe.sem_inc(x_free, 2)
                with pe.Fori(0, NC) as i:
                    for s in range(B):
                        take(pe, pA_free)
                        take(pe, y_ready)
                        for j in range(CT):
                            for k in range(KD):
                                mm = pe.matmul(pA[:, j], yc[:, s, k, j * P:(j + 1) * P], Wo[:, k],
                                               start=(k == 0), stop=(k == KD - 1))
                        mm.then_inc(wo_done, 1)
                    for s in range(B):
                        take(pe, n_ready)
                        take(pe, t_free)
                        transposes(pe, pT, n2[:, s], ident[:]).then_inc(turned, 1)
                    for s in range(B):
                        take(pe, xm_ready)
                        for o in range(KH):
                            take(pe, fk_free)
                            for k in range(KD):
                                mm = pe.matmul(pF[:, o % 2], Wfk[:, k, o * P:(o + 1) * P], xm[:, s, 0, k],
                                               start=(k == 0), stop=(k == KD - 1))
                            mm.then_inc(fk_done, 1)
                    for s in range(B):
                        take(pe, pA_free)
                        for j in range(CT):
                            for k in range(KD):
                                mm = pe.matmul(pA[:, j], xm[:, s, 1, k, j * P:(j + 1) * P], Wfr[:, k],
                                               start=(k == 0), stop=(k == KD - 1))
                        mm.then_inc(r_done, 1)
                        take(pe, kf_ready)
                        for j in range(CT):
                            take(pe, o_free)
                            for k in range(KH):
                                mm = pe.matmul(pO[:, j % 2, 0:D], kf[:, s, k, j * P:(j + 1) * P], Wfv[:, k],
                                               start=(k == 0), stop=(k == KH - 1))
                            mm.then_inc(kv_done, 1)

            @block.vector
            def _(dve):
                dve.wait_ge(loads, 96)
                dve.tensor_scalar(omc[:], cm[:], -1.0, 1.0, ALU.mult, ALU.add)
                dve.memset(h2T[:, :, :, CH:CH + 1], 0.0)
                dve.memset(norm.eps[:], EPS).then_inc(consts, 1)
                dve.sem_inc(pA_free, 1)
                dve.sem_inc(t_free, 1)
                dve.sem_inc(fk_free, 2)
                dve.sem_inc(o_free, 2)
                c = Chain(dve, steps)
                with dve.Fori(0, NC) as i:
                    for s in range(B):
                        take(dve, wo_done)
                        c.link(dve.tensor_tensor(x1[:, s], x0[:, bass.ds(i * CT + s * TT, CT)], pA[:], ALU.add))
                        norm.stats(dve, c, s, x1[:, s], pA_free)
                    for s in range(B):
                        norm.apply(dve, c, s, n2[:, s], x1[:, s]).then_inc(n_ready, 1)
                    for s in range(B):
                        take(dve, a_ready)
                        for n in range(2):
                            for h in range(KD):
                                last = dve.scalar_tensor_tensor(xm[:, s, n, h], h2T[:, s, h, 1:CH + 1], cm[:, n, h:h + 1],
                                                                xm[:, s, n, h], ALU.mult, ALU.add)
                        last.then_inc(xm_ready, 1)
                    for s in range(B):
                        for o in range(KH):
                            take(dve, relu_ready)
                            last = dve.tensor_tensor(kf[:, s, o], kf[:, s, o], kf[:, s, o], ALU.mult)
                            last.then_inc(fk_free, 1)
                        dve.drain().then_inc(kf_ready, 1)
                    for s in range(B):
                        take(dve, sg_ready)
                        dve.sem_inc(pA_free, 1)
                        for j in range(CT):
                            take(dve, kv_done)
                            last = dve.tensor_tensor(sg[:, s, j], sg[:, s, j], pO[:, j % 2, 0:D], ALU.mult)
                            last.then_inc(o_free, 1)
                        dve.drain()
                        take(dve, x_in[s], 16)
                        c.link(dve.tensor_tensor(sg[:, s], sg[:, s], x1[:, s], ALU.add))
                        c.link(dve.tensor_tensor(sg[:, s], sg[:, s], row4(rows[:, 0, s, GATE * D:(GATE + 1) * D]), ALU.mult))
                        dve.tensor_tensor(x0[:, bass.ds(i * CT + s * TT, CT)], sg[:, s], xin[:, s], ALU.add).then_inc(x_free, 1)


def binarized(kit, r, S, w1T, w2T):
    nc, ins, ident = kit.nc, kit.ins, S["ident"]
    with Room(nc, "bin") as q:
        w = [q.sb(f"w{n}", [P, H // P * D]) for n in range(2)]
        sgn = [q.sb(f"s{n}", [P, H // P * D]) for n in range(2)]
        al = [q.sb("al0", [P, KH]), q.sb("al1", [P, KD])]
        ps = q.ps("ps", [P, 4, 4, P])
        loaded, signed, ready, turned, freed, steps = (q.sem("loaded"), q.sem("signed"), q.sem("ready"),
                                                       q.sem("turned"), q.sem("freed"), q.sem("steps"))
        shape = [(KH, D), (KD, H)]
        blocks = [(n, a, k) for n in range(2) for a in range(shape[n][1] // P) for k in range(shape[n][0])]

        def view(t, n):
            return t[n][:].rearrange("p (k m) -> p k m", k=shape[n][0])

        with nc.Block() as block:
            @block.sync
            def _(sp):
                for n, name in enumerate(("w1", "w2")):
                    sp.dma_start(view(w, n), ins[name].rearrange("(k p) m -> p k m", p=P)).then_inc(loaded, 16)

            @block.scalar
            def _(act):
                act.wait_ge(loaded, 32)
                for n in range(2):
                    act.activation(sgn[n][:], w[n][:], ACT.Sign).then_inc(signed, 1)

            @block.vector
            def _(dve):
                dve.wait_ge(loaded, 32)
                dve.wait_ge(signed, 2)
                c = Chain(dve, steps)
                for n in range(2):
                    k, m = shape[n]
                    c.link(dve.tensor_reduce(al[n][:], view(w, n), AX.X, ALU.add, apply_absolute_value=True))
                    c.link(dve.tensor_scalar(al[n][:], al[n][:], 1.0 / m, None, ALU.mult))
                    for j in range(k):
                        last = dve.scalar_tensor_tensor(view(sgn, n)[:, j], view(sgn, n)[:, j], al[n][:, j:j + 1],
                                                        view(w, n)[:, j], ALU.mult, ALU.subtract)
                    c.link(last)
                    dve.tensor_tensor(w[n][:], w[n][:], sgn[n][:], ALU.add).then_inc(ready, 1)
                for g in range(len(blocks) // 4):
                    dve.wait_ge(turned, g + 1)
                    n, a, k = blocks[4 * g]
                    out = (w1T, w2T)[n]
                    if n == 0:
                        dve.tensor_copy(out[:, a, k * P:(k + 4) * P], ps[:, g % 4].rearrange("p a b -> p (a b)")).then_inc(freed, 1)
                    else:
                        dve.tensor_copy(out[:, a:a + 2].rearrange("p a b -> p (a b)"), ps[:, g % 4].rearrange("p a b -> p (a b)")).then_inc(freed, 1)

            @block.tensor
            def _(pe):
                for i, (n, a, k) in enumerate(blocks):
                    g = i // 4
                    if i % 4 == 0:
                        pe.wait_ge(ready, n + 1)
                        if g >= 4:
                            pe.wait_ge(freed, g - 3)
                    mm = pe.transpose(ps[:, g % 4, i % 4], view(w, n)[:, k, a * P:(a + 1) * P], ident[:])
                    if i % 4 == 3:
                        mm.then_inc(turned, 1)


def phase_ffn(kit, S):
    nc, ins = kit.nc, kit.ins
    x, rows, cols, ident = S["x0"], S["rows"], S["cols"], S["ident"]
    with Room(nc, "ffn") as r:
        w1T = r.sb("w1T", [P, KD, H])
        w2T = r.sb("w2T", [P, KH, D])
        binarized(kit, r, S, w1T, w2T)
        b1 = r.sb("b1", [P, KH])
        b2 = r.sb("b2", [P, D])
        n1 = r.sb("n1", [P, B, CT, D])
        fT = r.sb("fT", [P, B, KD, CH])
        g = r.sb("g", [P, B, KH, CH])
        o = r.sb("o", [P, B, CT, D])
        norm = Norm(r)
        pT = r.ps("pT", [P, KD, CH])
        pF = r.ps("pF", [P, 4, CH])
        pO = r.ps("pO", [P, 2, 512])
        loads, consts = r.sem("loads"), r.sem("consts")
        n_ready, turned, t_free, f_ready = r.sem("n_ready"), r.sem("turned"), r.sem("t_free"), r.sem("f_ready")
        w1_done, pF_free, g_ready = r.sem("w1_done"), r.sem("pF_free"), r.sem("g_ready")
        w2_done, o_free, steps = r.sem("w2_done"), r.sem("o_free"), r.sem("steps")
        with nc.Block() as block:
            @block.sync
            def _(sp):
                sp.dma_start(b1[:], ins["b1col"]).then_inc(loads, 16)
                sp.dma_start(b2[:], ins["b2"].partition_broadcast(P)).then_inc(loads, 16)

            @block.scalar
            def _(act):
                act.wait_ge(loads, 32)
                act.wait_ge(consts, 1)
                with act.Fori(0, NC) as i:
                    for s in range(B):
                        norm.root(act, s)
                    for s in range(B):
                        take(act, turned)
                        for h in range(KD):
                            last = act.activation(fT[:, s, h], pT[:, h], ACT.Identity,
                                                  scale=cols[:, 0, 1, h, s:s + 1], bias=cols[:, 0, 0, h, s:s + 1])
                        last.then_inc(f_ready, 1)
                    for s in range(B):
                        for m in range(KH):
                            take(act, w1_done)
                            act.activation(g[:, s, m], pF[:, m % 4], ACT.Gelu, bias=b1[:, m:m + 1]).then_inc(pF_free, 1)
                        act.drain().then_inc(g_ready, 1)

            @block.tensor
            def _(pe):
                pe.sem_inc(pF_free, 4)
                with pe.Fori(0, NC) as i:
                    for s in range(B):
                        take(pe, n_ready)
                        if s == 1:
                            take(pe, f_ready)
                        transposes(pe, pT, n1[:, s], ident[:]).then_inc(turned, 1)
                    take(pe, f_ready)
                    for s in range(B):
                        for m in range(KH):
                            take(pe, pF_free)
                            for k in range(KD):
                                mm = pe.matmul(pF[:, m % 4], w1T[:, k, m * P:(m + 1) * P], fT[:, s, k],
                                               start=(k == 0), stop=(k == KD - 1))
                            mm.then_inc(w1_done, 1)
                    for s in range(B):
                        take(pe, g_ready)
                        for j in range(CT):
                            take(pe, o_free)
                            for k in range(KH):
                                mm = pe.matmul(pO[:, j % 2, 0:D], g[:, s, k, j * P:(j + 1) * P], w2T[:, k],
                                               start=(k == 0), stop=(k == KH - 1))
                            mm.then_inc(w2_done, 1)

            @block.vector
            def _(dve):
                dve.wait_ge(loads, 32)
                dve.memset(norm.eps[:], EPS).then_inc(consts, 1)
                dve.sem_inc(o_free, 2)
                c = Chain(dve, steps)
                with dve.Fori(0, NC) as i:
                    for s in range(B):
                        norm.stats_at(dve, c, s, x, i * CT + s * TT)
                    for s in range(B):
                        norm.apply_at(dve, c, s, n1[:, s], x, i * CT + s * TT).then_inc(n_ready, 1)
                    for s in range(B):
                        for j in range(CT):
                            take(dve, w2_done)
                            last = dve.tensor_tensor(o[:, s, j], pO[:, j % 2, 0:D], b2[:], ALU.add)
                            last.then_inc(o_free, 1)
                        dve.drain()
                        c.link(dve.tensor_tensor(o[:, s], o[:, s], row4(rows[:, 0, s, (3 + GATE) * D:(4 + GATE) * D]), ALU.mult))
                        xc = x[:, bass.ds(i * CT + s * TT, CT)]
                        c.link(dve.tensor_tensor(xc, xc, o[:, s], ALU.add))

HA, DA = 16, 16
GH = 4
PAIRS = (0, 0, 0, 1, 1, 2), (0, 1, 2, 0, 1, 0)
KQ = len(PAIRS[0]) * DA
ROWS = KQ + 3


def phase_qkv(kit, S):
    nc, ins = kit.nc, kit.ins
    x, cols, ident, V = S["x0"], S["cols"], S["ident"], S["V"]
    with Room(nc, "qkv") as r:
        W = r.sb("W", [P, 3, KD, D])
        bqk = r.sb("bqk", [P, 2, KD])
        bv = r.sb("bv", [P, D])
        n1 = r.sb("n1", [P, B, CT, D])
        fT = r.sb("fT", [P, B, KD, CH])
        full = r.sb("full", [P, B, 4, CH])
        piece = r.sb("piece", [P, B, 3, 4, CH], BF16)
        norm = Norm(r)
        pT = r.ps("pT", [P, KD, CH])
        pF = r.ps("pF", [P, 4, CH])
        pV = r.ps("pV", [P, CT, D])
        loads, consts = r.sem("loads"), r.sem("consts")
        n_ready, turned, f_ready = r.sem("n_ready"), r.sem("turned"), r.sem("f_ready")
        qk_done, pF_free, v_done, v_free = r.sem("qk_done"), r.sem("pF_free"), r.sem("v_done"), r.sem("v_free")
        p1_ready, r1_ready, p2_ready, p3_ready = r.sem("p1_ready"), r.sem("r1_ready"), r.sem("p2_ready"), r.sem("p3_ready")
        stored, steps = [r.sem("stored0"), r.sem("stored1")], r.sem("steps")
        with nc.Block() as block:
            @block.sync
            def _(sp):
                for n, name in enumerate(("wq", "wk", "wv")):
                    sp.dma_start(W[:, n], ins[name].rearrange("(k p) n -> p k n", p=P)).then_inc(loads, 16)
                sp.dma_start(bqk[:], ins["bqkcol"]).then_inc(loads, 16)
                sp.dma_start(bv[:], ins["bv"].partition_broadcast(P)).then_inc(loads, 16)
                with sp.Fori(0, NC) as i:
                    for s in range(B):
                        take(sp, p3_ready)
                        for n in range(3):
                            for m in range(2):
                                sp.dma_start(S["qk"][m, n, 2 * s:2 * s + 2, :, bass.ds(i * CH, CH)].rearrange("m p t -> p m t"),
                                             piece[:, s, n, 2 * m:2 * m + 2]).then_inc(stored[s], 16)
                for s in range(B):
                    sp.wait_ge(stored[s], 96)

            @block.scalar
            def _(act):
                act.wait_ge(loads, 80)
                act.wait_ge(consts, 2)
                for s in range(B):
                    act.sem_inc(stored[s], 96)
                with act.Fori(0, NC) as i:
                    for s in range(B):
                        norm.root(act, s)
                    for s in range(B):
                        take(act, turned)
                        for h in range(KD):
                            last = act.activation(fT[:, s, h], pT[:, h], ACT.Identity,
                                                  scale=cols[:, 1, 1, h, s:s + 1], bias=cols[:, 1, 0, h, s:s + 1])
                        last.then_inc(f_ready, 1)
                    for s in range(B):
                        take(act, stored[s], 96)
                        for m in range(4):
                            scale = 0.25 if m < 2 else 1.0
                            take(act, qk_done)
                            act.activation(full[:, s, m], pF[:, m], ACT.Identity, scale=scale, bias=bqk[:, m // 2, m % 2:m % 2 + 1])
                            act.activation(piece[:, s, 0, m], pF[:, m], ACT.Identity, scale=scale,
                                           bias=bqk[:, m // 2, m % 2:m % 2 + 1]).then_inc(pF_free, 1)
                        act.drain().then_inc(p1_ready, 1)

            @block.gpsimd
            def _(pool):
                with pool.Fori(0, NC) as i:
                    for s in range(B):
                        take(pool, r1_ready)
                        pool.tensor_copy(piece[:, s, 1], full[:, s]).then_inc(p2_ready, 1)

            @block.tensor
            def _(pe):
                pe.wait_ge(loads, 80)
                pe.sem_inc(pF_free, 4)
                with pe.Fori(0, NC) as i:
                    for s in range(B):
                        take(pe, n_ready)
                        if s == 1:
                            take(pe, f_ready)
                        transposes(pe, pT, n1[:, s], ident[:]).then_inc(turned, 1)
                    take(pe, f_ready)
                    for s in range(B):
                        take(pe, v_free)
                        for j in range(CT):
                            for k in range(KD):
                                mm = pe.matmul(pV[:, j], fT[:, s, k, j * P:(j + 1) * P], W[:, 2, k],
                                               start=(k == 0), stop=(k == KD - 1))
                        mm.then_inc(v_done, 1)
                        for m in range(4):
                            take(pe, pF_free)
                            for k in range(KD):
                                mm = pe.matmul(pF[:, m], W[:, m // 2, k, m % 2 * P:m % 2 * P + P], fT[:, s, k],
                                               start=(k == 0), stop=(k == KD - 1))
                            mm.then_inc(qk_done, 1)

            @block.vector
            def _(dve):
                dve.wait_ge(loads, 80)
                dve.tensor_scalar(bqk[:, 0], bqk[:, 0], 0.25, None, ALU.mult).then_inc(consts, 1)
                dve.memset(norm.eps[:], EPS).then_inc(consts, 1)
                dve.sem_inc(v_free, 1)
                c = Chain(dve, steps)
                with dve.Fori(0, NC) as i:
                    for s in range(B):
                        norm.stats_at(dve, c, s, x, i * CT + s * TT)
                    for s in range(B):
                        norm.apply_at(dve, c, s, n1[:, s], x, i * CT + s * TT).then_inc(n_ready, 1)
                    for s in range(B):
                        take(dve, v_done)
                        for m in range(KD):
                            last = dve.tensor_tensor(V[:, 2 * s + m, bass.ds(i * CT, CT)], pV[:, :, m * P:(m + 1) * P],
                                                     row4(bv[:, m * P:(m + 1) * P]), ALU.add)
                        last.then_inc(v_free, 1)
                        take(dve, p1_ready)
                        dve.tensor_tensor(full[:, s], full[:, s], piece[:, s, 0], ALU.subtract).then_inc(r1_ready, 1)
                        take(dve, p2_ready)
                        dve.tensor_tensor(piece[:, s, 2], full[:, s], piece[:, s, 1], ALU.subtract).then_inc(p3_ready, 1)


def phase_attention(kit, S):
    nc, ins = kit.nc, kit.ins
    ident, identb, V, qk = S["ident"], S["identb"], S["V"], S["qk"]
    with Room(nc, "att") as r:
        Q = r.sb("Q", [P, 2, NC, GH, CH], BF16)
        K = r.sb("K", [P, 2, NC, GH, CH], BF16)
        Vg = r.sb("Vg", [P, 2, TT, GH, 32])
        Pr = r.sb("Pr", [P, 4, 2, CH])
        above = r.sb("above", [P, P], BF16)
        below = r.sb("below", [P, P], BF16)
        mx = r.sb("mx", [P, GH * CT, NC])
        mneg = r.sb("mneg", [P, GH * CT])
        mrest = r.sb("mrest", [P, GH * CT])
        mp = r.sb("mp", [P, 3, GH * CT], BF16)
        mrow = r.sb("mrow", [3 * GH * CT, NC, P], BF16)
        O = r.sb("O", [P, CH])
        rden = r.sb("rden", [P, CT, GH])
        ST = r.ps("ST", [P, 2, 2, CH])
        MX = r.ps("MX", [P, 2, CH])
        OV = r.ps("OV", [P, CH])
        TR = r.ps("TR", [P, CT, P])
        masks, in_q = r.sem("masks"), [[r.sem(f"in{a}{c}") for c in range(NC)] for a in range(2)]
        m_in = [r.sem(f"m_in{c}") for c in range(NC)]
        qk_free, st_done, p_ready = r.sem("qk_free"), r.sem("st_done"), r.sem("p_ready")
        mx_done, mx_free = r.sem("mx_done"), r.sem("mx_free")
        mp_ready, mt_done, mrow_ready = r.sem("mp_ready"), r.sem("mt_done"), r.sem("mrow_ready")
        ov_done, o_ready, tr_done, tr_free = r.sem("ov_done"), r.sem("o_ready"), r.sem("tr_done"), r.sem("tr_free")
        vg_ready, vg_free, steps, consts = r.sem("vg_ready"), r.sem("vg_free"), r.sem("steps"), r.sem("consts")
        chunks = list(range(NC))[::-1]

        def load(sp, i, a, c):
            for t, m in ((Q, 0), (K, 1)):
                for n, x in enumerate(PAIRS[m]):
                    src = qk[m, x, bass.ds(i, 1), 64 * a:64 * a + 64, c * CH:(c + 1) * CH]
                    sp.dma_start(t[DA * n:DA * n + DA, a, c],
                                 src.rearrange("a (h d) t -> d (a h) t", d=DA)).then_inc(in_q[a][c], 16)

        def sp_group(sp, mxg, nxt):
            for c in chunks:
                if mxg is not None:
                    take(sp, mrow_ready)
                    for n in range(3):
                        sp.dma_start(Q[KQ + n:KQ + n + 1, mxg[1], c].rearrange("a h (r p) -> a (h r) p", p=P),
                                     mrow[n * GH * CT:(n + 1) * GH * CT, c]
                                     ).then_inc(m_in[c], 16)
                if nxt is not None:
                    take(sp, qk_free)
                    load(sp, nxt[0], nxt[1], c)

        def pe_group(pe, eg, mxg):
            def scores_t(c, n, e):
                r0 = (n - CT * c) * P if n >= CT * c else 0
                for hh in range(2):
                    h = 2 * (e % 2) + hh
                    mm = pe.matmul(ST[:, e % 2, hh, r0:], K[0:ROWS, eg[1], n // CT, h, n % CT * P:(n % CT + 1) * P],
                                   Q[0:ROWS, eg[1], c, h, r0:], start=True, stop=(n < CT * c))
                    if n >= CT * c:
                        mm = pe.matmul(ST[:, e % 2, hh, r0:r0 + P], identb[:], below[:], start=False, stop=True)
                mm.then_inc(st_done, 1)

            def pv(c, n, e):
                if n == 0 and e % 2 == 0 and c < NC - 1:
                    take(pe, o_ready)
                r0 = (n - CT * c) * P if n >= CT * c else 0
                for hh in range(2):
                    h = 2 * (e % 2) + hh
                    mm = pe.matmul(OV[32 * h:32 * h + 32, r0:], Vg[:, eg[1], n, h], Pr[:, e % 4, hh, r0:],
                                   start=(n == 0), stop=(n == CT * c + CT - 1), tile_position=(0, 32 * h),
                                   skip_group_check=True)
                if n == CT * c + CT - 1 and e % 2:
                    mm.then_inc(ov_done, 1)

            def maxima(c, n, h):
                rr, w = n % CT, c - n // CT
                last = n // CT == 0
                cols = (rr + 1) * P if last else CH
                if h == 0 and rr == 0 and c == NC - 1:
                    take(pe, in_q[mxg[1]][w], 16 * 2 * len(PAIRS[0]))
                take(pe, mx_free)
                mm = pe.matmul(MX[:, h % 2, 0:cols], Q[0:KQ, mxg[1], c, h, rr * P:(rr + 1) * P],
                               K[0:KQ, mxg[1], w, h, 0:cols], start=True, stop=not last)
                if last:
                    mm = pe.matmul(MX[:, h % 2, cols - P:cols], identb[:], above[:], start=False, stop=True)
                mm.then_inc(mx_done, 1)

            def turn_max():
                take(pe, mp_ready)
                take(pe, tr_free)
                pe.transpose(TR[:].rearrange("p a b -> p (a b)").bitcast(BF16)[0:3 * GH * CT, 0:P],
                             mp[:].rearrange("p a b -> p (a b)"), identb[:]).then_inc(mt_done, 1)

            def turn_out():
                take(pe, tr_free)
                for j in range(CT):
                    mm = pe.transpose(TR[:, j], O[:, j * P:(j + 1) * P], ident[:])
                mm.then_inc(tr_done, 1)

            late = []
            if eg is not None:
                take(pe, vg_ready)
            e = 0
            for c in chunks:
                if eg is not None:
                    take(pe, m_in[c], 48)
                lag = []
                for n in range(CT * (c + 1)):
                    for pair in range(2):
                        if eg is not None:
                            if len(lag) == 2:
                                take(pe, p_ready)
                            scores_t(c, n, e)
                            lag.append((c, n, e))
                            e += 1
                        if mxg is not None:
                            maxima(c, n, 2 * pair)
                            maxima(c, n, 2 * pair + 1)
                        if len(lag) == 3:
                            pv(*lag.pop(0))
                    if n == 2:
                        for f in late:
                            f()
                        late = []
                for t in lag:
                    take(pe, p_ready)
                    pv(*t)
                late = ([turn_max] if mxg is not None else []) + ([turn_out] if eg is not None else [])
            if eg is not None:
                take(pe, o_ready)
            for f in late:
                f()

        def act_group(act, eg, c_free):
            e = 0
            for c in chunks:
                for n in range(CT * (c + 1)):
                    r0 = (n - CT * c) * P if n >= CT * c else 0
                    for pair in range(2):
                        take(act, st_done)
                        act.activation(Pr[:, e % 4, :, r0:], ST[:, e % 2, :, r0:], ACT.Exp).then_inc(p_ready, 1)
                        e += 1
                take(act, ov_done)
                act.activation(O[:], OV[:], ACT.Copy).then_inc(o_ready, 1)
                if c_free:
                    act.drain().then_inc(qk_free, 1)

        def dve_group(dve, eg, mxg):
            ch = Chain(dve, steps)

            def maxima(c, n, h):
                rr, w = n % CT, c - n // CT
                cols = (rr + 1) * P if n // CT == 0 else CH
                take(dve, mx_done)
                return dve.tensor_reduce(mx[:, h * CT + rr, w:w + 1], MX[:, h % 2, 0:cols], AX.X, ALU.max)

            def pieces(c):
                dve.drain()
                ch.link(dve.tensor_reduce(mneg[:], mx[:, :, 0:c + 1], AX.X, ALU.max))
                ch.link(dve.tensor_scalar(mneg[:], mneg[:], -1.0, None, ALU.mult))
                ch.link(dve.tensor_copy(mp[:, 0], mneg[:]))
                ch.link(dve.tensor_tensor(mrest[:], mneg[:], mp[:, 0], ALU.subtract))
                ch.link(dve.tensor_copy(mp[:, 1], mrest[:]))
                dve.tensor_tensor(mp[:, 2], mrest[:], mp[:, 1], ALU.subtract).then_inc(mp_ready, 1)

            def row(c):
                take(dve, mt_done)
                dve.tensor_copy(mrow[:, c], TR[:].rearrange("p a b -> p (a b)").bitcast(BF16)[0:3 * GH * CT, 0:P]).then_inc(mrow_ready, 1)
                dve.drain().then_inc(tr_free, 1)

            def out(c):
                take(dve, tr_done)
                ch.link(dve.reciprocal(rden[:], TR[:].rearrange("p r (h d) -> p r h d", h=GH)[:, :, :, DA]))
                for j in range(CT):
                    last = dve.tensor_tensor(
                        V[:, bass.ds(eg[0], 1), c * CT + j, 64 * eg[1]:64 * eg[1] + 64].rearrange("p a (h d) -> p (a h) d", h=GH),
                        TR[:, j].rearrange("p (h d) -> p h d", h=GH)[:, :, 0:DA],
                        rden[:, j].unsqueeze(2).broadcast_to([P, GH, DA]), ALU.mult)
                last.then_inc(tr_free, 1)

            late = []
            for c in chunks:
                for n in range(CT * (c + 1)):
                    if mxg is not None:
                        for h in range(GH):
                            maxima(c, n, h).then_inc(mx_free, 1)
                    if n == 2:
                        for f, k in late:
                            f(k)
                        late = []
                late = []
                if mxg is not None:
                    pieces(c)
                    late.append((row, c))
                if eg is not None:
                    late.append((out, c))
            for f, k in late:
                f(k)
            if eg is not None:
                dve.drain().then_inc(vg_free, 1)

        N2 = 2 * B
        with nc.Block() as block:
            @block.sync
            def _(sp):
                for a in range(2):
                    for c in chunks:
                        load(sp, 0, a, c)
                sp_group(sp, (0, 0), None)
                with sp.Fori(0, N2 - 1) as i:
                    sp_group(sp, (i, 1), (i + 1, 0))
                    sp_group(sp, (i + 1, 0), (i + 1, 1))
                sp_group(sp, (N2 - 1, 1), None)

            @block.gpsimd
            def _(pool):
                pool.memset(above[:], 0.0).then_inc(consts, 1)
                pool.memset(below[:], 0.0).then_inc(consts, 1)
                pool.wait_ge(consts, 2)
                pool.affine_select(out=above[:], in_=above[:], compare_op=ALU.is_ge, fill=NEG, base=0,
                                   pattern=[[-1, P]], channel_multiplier=1).then_inc(masks, 1)
                pool.affine_select(out=below[:], in_=below[:], compare_op=ALU.is_ge, fill=NEG, base=0,
                                   pattern=[[1, P]], channel_multiplier=-1).then_inc(masks, 1)
                pool.memset(Vg[:], 1.0).then_inc(consts, 1)
                pool.wait_ge(consts, 3)
                pool.sem_inc(vg_free, 2)
                with pool.Fori(0, N2) as i:
                    for a in range(2):
                        take(pool, vg_free)
                        src = V[:, bass.ds(i, 1), :, 64 * a:64 * a + 64].rearrange("p a j n -> p (a j) n")
                        for h in range(GH):
                            last = pool.tensor_copy(Vg[:, a, :, h, 0:DA], src[:, :, h * DA:(h + 1) * DA])
                        last.then_inc(vg_ready, 1)

            @block.scalar
            def _(act):
                with act.Fori(0, N2 - 1) as i:
                    act_group(act, (i, 0), True)
                    act_group(act, (i, 1), True)
                act_group(act, (N2 - 1, 0), False)
                act_group(act, (N2 - 1, 1), False)

            @block.tensor
            def _(pe):
                pe.wait_ge(masks, 2)
                pe.wait_ge(S["identb_ready"], 1)
                pe_group(pe, None, (0, 0))
                with pe.Fori(0, N2 - 1) as i:
                    pe_group(pe, (i, 0), (i, 1))
                    pe_group(pe, (i, 1), (i + 1, 0))
                pe_group(pe, (N2 - 1, 0), (N2 - 1, 1))
                pe_group(pe, (N2 - 1, 1), None)

            @block.vector
            def _(dve):
                dve.memset(K[KQ:ROWS], 1.0)
                dve.tensor_copy(identb[:], ident[:]).then_inc(S["identb_ready"], 1)
                dve.sem_inc(mx_free, 2)
                dve.sem_inc(tr_free, 1)
                dve_group(dve, None, (0, 0))
                with dve.Fori(0, N2 - 1) as i:
                    dve_group(dve, (i, 0), (i, 1))
                    dve_group(dve, (i, 1), (i + 1, 0))
                dve_group(dve, (N2 - 1, 0), (N2 - 1, 1))
                dve_group(dve, (N2 - 1, 1), None)


XW = D + 2
NQ, NKV = 256, 512
R4 = 2 * B
FETCH = 9.0 / 8.0
ITERS = 50


def phase_route_scores(kit, S):
    nc, ins = kit.nc, kit.ins
    x, rows, ident, A, xn, sc = S["x0"], S["rows"], S["ident"], S["V"], S["xn"], S["s4"]
    with Room(nc, "rts") as r:
        Wo = r.sb("Wo", [P, KD, D])
        bo = r.sb("bo", [P, D])
        tok = r.sb("tok", [P, 2, D])
        a = r.sb("a", [P, B, CT, D])
        aT = r.sb("aT", [P, B, KD, CH])
        h = r.sb("h", [P, B, CT, D])
        junk = r.sb("junk", [P, D])
        junk2 = r.sb("junk2", [P, B, CT, D])
        dots = r.sb("dots", [P, B, 2, CT])
        ss = r.sb("ss", [P, B, CT])
        norm = Norm(r)
        pT = r.ps("pT", [P, KD, CH])
        pA = r.ps("pA", [P, CT, D])
        loads, consts = r.sem("loads"), r.sem("consts")
        a_ready, turned, aT_ready, a_done, a_free = (r.sem("a_ready"), r.sem("turned"), r.sem("aT_ready"),
                                                     r.sem("a_done"), r.sem("a_free"))
        h_ready, ss_ready, steps, a_read = r.sem("h_ready"), r.sem("ss_ready"), r.sem("steps"), r.sem("a_read")
        with nc.Block() as block:
            @block.sync
            def _(sp):
                sp.dma_start(Wo[:], ins["wo"].rearrange("(k p) n -> p k n", p=P)).then_inc(loads, 16)
                sp.dma_start(bo[:], ins["bo"].partition_broadcast(P)).then_inc(loads, 16)
                for n, name in enumerate(("q_tok", "kv_tok")):
                    sp.dma_start(tok[:, n], ins[name].partition_broadcast(P)).then_inc(loads, 16)

            @block.gpsimd
            def _(pool):
                with pool.Fori(0, NC) as i:
                    for s in range(B):
                        take(pool, a_free)
                        for m in range(KD):
                            last = pool.tensor_copy(a[:, s, :, m * P:(m + 1) * P].unsqueeze(1),
                                                    A[:, 2 * s + m:2 * s + m + 1, bass.ds(i * CT, CT)])
                        last.then_inc(a_ready, 1)

            @block.scalar
            def _(act):
                act.wait_ge(loads, 64)
                act.wait_ge(consts, 1)
                act.sem_inc(a_free, 2)
                with act.Fori(0, NC) as i:
                    for s in range(B):
                        take(act, turned)
                        for k in range(KD):
                            last = act.activation(aT[:, s, k], pT[:, k], ACT.Copy)
                        last.then_inc(aT_ready, 1)
                        act.sem_inc(a_free, 1)
                    for s in range(B):
                        norm.root(act, s)
                    for s in range(B):
                        take(act, h_ready)
                        for j in range(CT):
                            last = act.activation(junk2[:, s, j], h[:, s, j], ACT.Square, accum_out=ss[:, s, j:j + 1])
                        act.drain()
                        act.activation(ss[:, s], ss[:, s], ACT.Sqrt).then_inc(ss_ready, 1)

            @block.tensor
            def _(pe):
                pe.wait_ge(loads, 64)
                with pe.Fori(0, NC) as i:
                    for s in range(B):
                        take(pe, a_ready)
                        if s == 1:
                            take(pe, aT_ready)
                        transposes(pe, pT, a[:, s], ident[:]).then_inc(turned, 1)
                    take(pe, aT_ready)
                    for s in range(B):
                        if s == 1:
                            take(pe, a_read)
                        for j in range(CT):
                            for k in range(KD):
                                mm = pe.matmul(pA[:, j], aT[:, s, k, j * P:(j + 1) * P], Wo[:, k],
                                               start=(k == 0), stop=(k == KD - 1))
                        mm.then_inc(a_done, 1)
                    take(pe, a_read)

            @block.vector
            def _(dve):
                dve.wait_ge(loads, 64)
                dve.memset(norm.eps[:], EPS).then_inc(consts, 1)
                c = Chain(dve, steps)
                with dve.Fori(0, NC) as i:
                    for s in range(B):
                        take(dve, a_done)
                        dve.tensor_tensor(h[:, s], pA[:], row4(bo[:]), ALU.add).then_inc(a_read, 1)
                        dve.drain()
                        c.link(dve.tensor_tensor(h[:, s], h[:, s], row4(rows[:, 1, s, GATE * D:(GATE + 1) * D]), ALU.mult))
                        xc = x[:, bass.ds(i * CT + s * TT, CT)]
                        c.link(dve.tensor_tensor(xc, xc, h[:, s], ALU.add))
                        norm.stats_at(dve, c, s, x, i * CT + s * TT)
                    for s in range(B):
                        c.link(norm.apply_at(dve, c, s, h[:, s], x, i * CT + s * TT))
                        c.link(dve.tensor_tensor(h[:, s], h[:, s], row4(rows[:, 1, s, (3 + SCALE) * D:(4 + SCALE) * D]), ALU.mult))
                        dve.tensor_tensor(h[:, s], h[:, s], row4(rows[:, 1, s, (3 + SHIFT) * D:(4 + SHIFT) * D]), ALU.add).then_inc(h_ready, 1)
                        dve.drain()
                        for n in range(2):
                            for j in range(CT):
                                c.link(dve.tensor_tensor_reduce(junk[:], h[:, s, j], tok[:, n], 1.0, 0.0, ALU.mult,
                                                                ALU.add, dots[:, s, n, j:j + 1]))
                        dve.tensor_copy(sc[:].rearrange("p (n s) t -> p s n t", n=2)[:, s, :, bass.ds(i * CT, CT)], dots[:, s])
                    for s in range(B):
                        take(dve, ss_ready)
                        c.link(dve.tensor_scalar(ss[:, s], ss[:, s], 1e-12, None, ALU.max))
                        c.link(dve.reciprocal(ss[:, s], ss[:, s]))
                        for j in range(CT):
                            dve.tensor_scalar(xn[:, bass.ds(i * CT + s * TT + j, 1), 0:D].rearrange("p a d -> p (a d)"),
                                              h[:, s, j], ss[:, s, j:j + 1], float(D) ** 0.5, ALU.mult, ALU.mult)
                        dve.drain()


def phase_routing(kit, S):
    nc, ins, ident = kit.nc, kit.ins, S["ident"]
    s4, xn, rank = S["s4"], S["xn"], S["rank"]
    with Room(nc, "cdr") as r:
        s17 = r.sb("s17", [P, R4, TT + 1])
        nu = r.sb("nu", [P, R4, TT + 1])
        t = r.sb("t", [P, R4, TT + 1])
        e = r.sb("e", [P, R4, TT])
        es = r.sb("es", [P, R4])
        a = r.sb("a", [P, R4])
        lk = r.sb("lk", [P, R4])
        ln = r.sb("ln", [P, R4])
        m4 = r.sb("m4", [P, R4])
        md = r.sb("md", [R4, R4])
        m1 = r.sb("m1", [R4, 1])
        ones = r.sb("ones", [P, P])
        w = r.sb("w", [P, R4, TT])
        score = r.sb("score", [P, R4, TT])
        R = r.sb("R", [P, 2, T])
        junk = r.sb("junk", [P, 2, T], BF16)
        tie = r.sb("tie", [P, 2, P], BF16)
        lower = r.sb("lower", [P, P])
        cnt = r.sb("cnt", [P, R4, TT, 4])
        pm = r.ps("pm", [P, 512])
        pb = r.ps("pb", [P, NC, 512])
        consts, s_ready, mt, m_ready, mb = r.sem("consts"), r.sem("s_ready"), r.sem("mt"), r.sem("m_ready"), r.sem("mb")
        w_ready, e_ready, es_ready, sum_ready, ln_ready = (r.sem("w_ready"), r.sem("e_ready"), r.sem("es_ready"),
                                                           r.sem("sum_ready"), r.sem("ln_ready"))
        score_in, score_ready, spread, r_ready, steps = (r.sem("score_in"), r.sem("score_ready"), r.sem("spread"),
                                                         r.sem("r_ready"), r.sem("steps"))
        r_free, score_in_order, pb_free = r.sem("r_free"), r.sem("score_in_order"), r.sem("pb_free")
        ks = [min(n * FETCH, T) for n in (NQ, NKV)]
        with nc.Block() as block:
            @block.scalar
            def _(act):
                with act.Fori(0, ITERS) as _i:
                    take(act, w_ready)
                    act.activation(e[:], w[:], ACT.Exp).then_inc(e_ready, 1)
                    take(act, sum_ready)
                    act.activation(ln[:], pm[:, 0:R4], ACT.Ln).then_inc(ln_ready, 1)
                take(act, score_in)
                act.activation(score[:], w[:], ACT.Exp).then_inc(score_ready, 1)
                for n in range(R4):
                    take(act, spread)
                    if n >= 2:
                        take(act, r_free)
                    act.activation(R[:, n % 2], pb[:].rearrange("p a b -> p (a b)"), ACT.Copy).then_inc(r_ready, 1)

            @block.gpsimd
            def _(pool):
                pool.memset(lower[:], 1.0).then_inc(consts, 1)
                pool.wait_ge(consts, 1)
                pool.affine_select(out=lower[:], in_=lower[:], compare_op=ALU.is_ge, fill=0.0, base=-1,
                                   pattern=[[-1, P]], channel_multiplier=1).then_inc(s_ready, 1)

            @block.tensor
            def _(pe):
                pe.wait_ge(mt, 1)
                pe.transpose(pm[0:R4, 0:P], m4[:], ident[:]).then_inc(m_ready, 1)
                pe.wait_ge(mt, 2)
                pe.matmul(pm[:, 0:R4], ones[0:R4], md[:], start=True, stop=True).then_inc(mb, 1)
                with pe.Fori(0, ITERS) as _i:
                    take(pe, es_ready)
                    pe.matmul(pm[:, 0:R4], ones[:], es[:], start=True, stop=True).then_inc(sum_ready, 1)
                pe.wait_ge(score_in_order, 1)
                for n in range(R4):
                    if n:
                        take(pe, pb_free)
                    for j in range(TT):
                        mm = pe.transpose(pb[:, j // CT, j % CT * P:(j % CT + 1) * P],
                                          score[:, n, j:j + 1].broadcast_to([P, P]), ident[:])
                    mm.then_inc(spread, 1)

            @block.vector
            def _(dve):
                c = Chain(dve, steps)
                dve.memset(ones[:], 1.0)
                dve.memset(cnt[:], 0.0)
                for n, k in enumerate(ks):
                    dve.memset(lk[:, n * B:(n + 1) * B], math.log(k))
                dve.memset(nu[:], 0.0)
                dve.tensor_reduce(m4[:], s4[:], AX.X, ALU.max).then_inc(mt, 1)
                dve.wait_ge(m_ready, 1)
                c.link(dve.tensor_reduce(m1[:], pm[0:R4, 0:P], AX.X, ALU.max))
                dve.tensor_scalar(md[:], ident[0:R4, 0:R4], m1[:], None, ALU.mult).then_inc(mt, 1)
                dve.tensor_copy(s17[:, :, 0:TT], s4[:])
                dve.wait_ge(mb, 1)
                c.link(dve.tensor_copy(s17[:, :, TT], pm[:, 0:R4]))
                with dve.Fori(0, ITERS) as _i:
                    dve.tensor_tensor(w[:], nu[:, :, TT:TT + 1].broadcast_to([P, R4, TT]), nu[:, :, 0:TT],
                                      ALU.subtract).then_inc(w_ready, 1)
                    take(dve, e_ready)
                    dve.tensor_reduce(es[:], e[:], AX.X, ALU.add).then_inc(es_ready, 1)
                    take(dve, ln_ready)
                    c.link(dve.tensor_tensor(ln[:], ln[:], nu[:, :, TT], ALU.subtract))
                    c.link(dve.tensor_tensor(a[:], lk[:], ln[:], ALU.subtract))
                    c.link(dve.tensor_tensor(t[:], s17[:], a[:].unsqueeze(2).broadcast_to([P, R4, TT + 1]), ALU.add))
                    c.link(dve.scalar_tensor_tensor(nu[:], t[:], 0.0, s17[:], ALU.max, ALU.subtract))
                dve.tensor_scalar(w[:], t[:, :, 0:TT], 0.0, None, ALU.min).then_inc(score_in, 1)
                dve.wait_ge(score_ready, 1)
                dve.sem_inc(score_in_order, 1)
                c.link(dve.tensor_scalar(e[:], score[:], -1.0, 1.0, ALU.mult, ALU.add))
                for n in range(2):
                    last = dve.tensor_tensor(xn[:, :, D + n].rearrange("p (s t) -> p s t", s=B),
                                             score[:, n * B:(n + 1) * B], e[:, n * B:(n + 1) * B], ALU.add)
                dve.wait_ge(s_ready, 1)
                for n in range(R4):
                    take(dve, r_ready)
                    dve.sem_inc(pb_free, 1)
                    for j in range(TT):
                        Rn, sj = R[:, n % 2], score[:, n, j:j + 1]
                        if j:
                            dve.tensor_scalar(junk[:, j % 2, 0:j * P], Rn[:, 0:j * P], sj, 0.0, ALU.is_ge, ALU.add,
                                              accum_out=cnt[:, n, j, 0:1])
                        dve.tensor_scalar(junk[:, j % 2, j * P:T], Rn[:, j * P:T], sj, 0.0, ALU.is_gt, ALU.add,
                                          accum_out=cnt[:, n, j, 1:2])
                        dve.drain()
                        dve.scalar_tensor_tensor(tie[:, j % 2], Rn[:, j * P:(j + 1) * P], sj, lower[:],
                                                 ALU.is_equal, ALU.mult, accum_out=cnt[:, n, j, 2:3])
                    dve.drain().then_inc(r_free, 1)
                dve.tensor_reduce(rank[:], cnt[:], AX.X, ALU.add)

HB, DH = 8, 64
HID = HB * DH
KG = HID // P


def phase_light(kit, S):
    nc, ins = kit.nc, kit.ins
    x, xn, rows, ident = S["x0"], S["xn"], S["rows"], S["ident"]
    with Room(nc, "lgt") as r:
        Wq = r.sb("Wq", [P, KD, HID])
        Wkv = r.sb("Wkv", [P, KD, 2 * HID])
        Wo = r.sb("Wo", [P, KG, D])
        gamma = r.sb("gamma", [P, KD])
        xc = r.sb("xc", [P, CT, D])
        xT = r.sb("xT", [P, KD, CH])
        qk = S["hT"][:].rearrange("p a b t -> p (a b t)")[:, 0:2 * B * KG * CH].rearrange(
            "p (m s g t) -> p m s g t", m=2, s=B, g=KG)
        v = r.sb("v", [P, B, CT, HID])
        mx = r.sb("mx", [P, 2, HB])
        den = r.sb("den", [P, 2, HB])
        Pr = r.sb("Pr", [P, 2, HB, P])
        PT = r.sb("PT", [P, HB, P])
        OT = r.sb("OT", [P, KG, P])
        y = r.sb("y", [P, 2, D])
        t = r.sb("t", [P, D])
        pu = r.ps("pu", [P, 4, 512])
        pS = r.ps("pS", [P, 2, HB, P])
        loads, x_ready, x_free, full, free = r.sem("loads"), r.sem("x_ready"), r.sem("x_free"), r.sem("full"), r.sem("free")
        s_done, s_free, mx_ready, e_ready, p_ready = (r.sem("s_done"), r.sem("s_free"), r.sem("mx_ready"),
                                                      r.sem("e_ready"), r.sem("p_ready"))
        evac, y_ready, steps = {n: r.sem("evac_" + n) for n in ("xT", "qkv", "PT", "OT")}, r.sem("y_ready"), r.sem("steps")
        p_free, y_free = r.sem("p_free"), r.sem("y_free")
        proj = [("x", h) for h in range(KD)] + [(n, j) for n in ("q", "k", "v") for j in range(CT)]
        share = [(proj[0:2], proj[2:5]), (proj[5:8], proj[8:10]), (proj[10:13], proj[13:14]), ([], [])]

        def slot(h):
            return h % 2 * (HB // 2) + h // 2

        def pe_unit(pe, u, s, kind, j):
            take(pe, free)
            out = pu[:, u % 4]
            if kind == "x":
                if j == 0:
                    take(pe, x_ready)
                for n in range(CT):
                    mm = pe.transpose(out[:, n * P:(n + 1) * P], xc[:, n, j * P:(j + 1) * P], ident[:])
            else:
                if (kind, j) == ("q", 0):
                    take(pe, evac["xT"], 2)
                for k in range(KD):
                    if kind == "q":
                        w, m = Wq[:, k, j * P:(j + 1) * P], xT[:, k]
                    elif kind == "k":
                        w, m = Wkv[:, k, j * P:(j + 1) * P], xT[:, k]
                    else:
                        w, m = xT[:, k, j * P:(j + 1) * P], Wkv[:, k, HID:2 * HID]
                    mm = pe.matmul(out, w, m, start=(k == 0), stop=(k == KD - 1))
            mm.then_inc(full, 1)

        def act_unit(act, u, s, kind, j):
            take(act, full)
            src = pu[:, u % 4]
            if kind == "x":
                act.activation(xT[:, j], src, ACT.Copy, scale=gamma[:, j:j + 1]).then_inc(evac["xT"], 1)
                act.drain().then_inc(free, 1)
                if j == KD - 1:
                    act.sem_inc(x_free, 1)
            else:
                if kind == "q":
                    act.activation(qk[:, 0, s, j], src, ACT.Copy, scale=DH ** -0.5).then_inc(free, 1)
                elif kind == "k":
                    act.activation(qk[:, 1, s, j], src, ACT.Copy).then_inc(free, 1)
                else:
                    act.activation(v[:, s, j], src, ACT.Copy).then_inc(free, 1)
                if (kind, j) == ("v", CT - 1):
                    act.drain().then_inc(evac["qkv"], 1)

        def pe_scores(pe, s, w):
            if w == 0:
                take(pe, evac["qkv"])
            take(pe, s_free)
            for h in range(HB):
                at = slice(DH * (h % 2), DH * (h % 2) + DH)
                mm = pe.matmul(pS[:, w % 2, slot(h)], qk[at, 0, s, h // 2, w * P:(w + 1) * P],
                               qk[at, 1, s, h // 2, w * P:(w + 1) * P], start=True, stop=True)
            mm.then_inc(s_done, 1)

        def act_exp(act, w):
            take(act, mx_ready)
            take(act, p_free)
            for h in range(HB):
                last = act.activation(Pr[:, w % 2, h], pS[:, w % 2, h], ACT.Exp, bias=mx[:, w % 2, h:h + 1],
                                      accum_out=den[:, w % 2, h:h + 1])
            last.then_inc(e_ready, 1)
            act.drain().then_inc(s_free, 1)

        def dve_max(dve, c, w):
            take(dve, s_done)
            c.link(dve.tensor_reduce(mx[:, w % 2], pS[:, w % 2], AX.X, ALU.max))
            dve.tensor_scalar(mx[:, w % 2], mx[:, w % 2], -1.0, None, ALU.mult).then_inc(mx_ready, 1)

        def pe_chunk(pe, s, more, nxt):
            u = 0
            for w in range(CT):
                for half in range(2):
                    take(pe, free)
                    if half == 0:
                        take(pe, p_ready)
                    for h in range(4):
                        mm = pe.transpose(pu[:, u % 4, h * P:(h + 1) * P], Pr[:, w % 2, 4 * half + h], ident[:])
                    mm.then_inc(full, 1)
                    u += 1
                if w < CT - 1:
                    pe_scores(pe, s, w + 1)
                elif nxt:
                    pe_scores(pe, 1 - s, 0)
                take(pe, free)
                take(pe, evac["PT"])
                for h in range(HB):
                    at = DH * (h % 2)
                    mm = pe.matmul(pu[at:at + DH, u % 4, h // 2 * P:(h // 2 + 1) * P], v[:, s, w, h * DH:(h + 1) * DH],
                                   PT[:, slot(h)], start=True, stop=True, tile_position=(0, at), skip_group_check=True)
                mm.then_inc(full, 1)
                u += 1
                if more:
                    for kind, j in share[w][0]:
                        pe_unit(pe, u, 1 - s, kind, j)
                        u += 1
                take(pe, free)
                take(pe, evac["OT"])
                for k in range(KG):
                    mm = pe.matmul(pu[:, u % 4, 0:D], OT[:, k], Wo[:, k], start=(k == 0), stop=(k == KG - 1))
                mm.then_inc(full, 1)
                u += 1
                if more:
                    for kind, j in share[w][1]:
                        pe_unit(pe, u, 1 - s, kind, j)
                        u += 1
            skip = -u % 4

            for _ in range(skip):
                take(pe, free)

        def act_chunk(act, s, more, nxt):
            u = 0
            for w in range(CT):
                for half in range(2):
                    take(act, full)
                    last = act.activation(PT[:, 4 * half:4 * half + 4].rearrange("p a b -> p (a b)"), pu[:, u % 4], ACT.Copy)
                    if half == 0:
                        last.then_inc(free, 1)
                    u += 1
                last.then_inc(evac["PT"], 1)
                act.drain().then_inc(free, 1)
                act.sem_inc(p_free, 1)
                take(act, full)
                act.activation(OT[:].rearrange("p a b -> p (a b)"), pu[:, u % 4], ACT.Copy).then_inc(evac["OT"], 1)
                act.drain().then_inc(free, 1)
                u += 1
                if w < CT - 1 or nxt:
                    act_exp(act, (w + 1) % CT)
                if more:
                    for kind, j in share[w][0]:
                        act_unit(act, u, 1 - s, kind, j)
                        u += 1
                take(act, full)
                take(act, y_free)
                act.activation(y[:, w % 2], pu[:, u % 4, 0:D], ACT.Copy).then_inc(y_ready, 1)
                act.drain().then_inc(free, 1)
                u += 1
                if more:
                    for kind, j in share[w][1]:
                        act_unit(act, u, 1 - s, kind, j)
                        u += 1
            skip = -u % 4
            if skip:
                act.sem_inc(free, skip)

        def dve_chunk(dve, c, s, i, nxt):
            for w in range(CT):
                if w < CT - 1 or nxt:
                    dve_max(dve, c, (w + 1) % CT)
                    dve_normalise(dve, c, (w + 1) % CT)
                take(dve, y_ready)
                c.link(dve.tensor_tensor(t[:], y[:, w % 2], rows[:, 1, s, (3 + GATE) * D:(4 + GATE) * D], ALU.mult))
                xw = flat(x[:, bass.ds(i * CT + (s * TT + w), 1)])
                c.link(dve.tensor_tensor(xw, xw, t[:], ALU.add))
                dve.sem_inc(y_free, 1)

        def dve_normalise(dve, c, w):
            take(dve, e_ready)
            c.link(dve.reciprocal(den[:, w % 2], den[:, w % 2]))
            dve.tensor_tensor(Pr[:, w % 2], Pr[:, w % 2], den[:, w % 2].unsqueeze(2).broadcast_to([P, HB, P]),
                              ALU.mult).then_inc(p_ready, 1)

        def pool_chunk(pool, i, s):
            take(pool, x_free)
            pool.tensor_copy(xc[:], xn[:, bass.ds(i * CT + s * TT, CT), 0:D]).then_inc(x_ready, 1)

        with nc.Block() as block:
            @block.sync
            def _(sp):
                for w, name in ((Wq, "wq_light"), (Wkv, "wkv_light"), (Wo, "wo_light")):
                    sp.dma_start(w[:], ins[name].rearrange("(k p) n -> p k n", p=P)).then_inc(loads, 16)
                sp.dma_start(gamma[:], ins["glcol"]).then_inc(loads, 16)

            @block.gpsimd
            def _(pool):
                pool_chunk(pool, 0, 0)
                with pool.Fori(0, NC - 1) as i:
                    pool_chunk(pool, i, 1)
                    pool_chunk(pool, i + 1, 0)
                pool_chunk(pool, NC - 1, 1)

            @block.tensor
            def _(pe):
                pe.wait_ge(loads, 64)
                pe.sem_inc(s_free, 2)
                pe.sem_inc(free, 4)
                for u, (kind, j) in enumerate(proj):
                    pe_unit(pe, u, 0, kind, j)
                take(pe, free, 2)
                pe_scores(pe, 0, 0)
                with pe.Fori(0, NC - 1) as _i:
                    pe_chunk(pe, 0, True, True)
                    pe_chunk(pe, 1, True, True)
                pe_chunk(pe, 0, True, True)
                pe_chunk(pe, 1, False, False)

            @block.scalar
            def _(act):
                act.wait_ge(loads, 64)
                act.sem_inc(x_free, 1)
                act.sem_inc(p_free, 2)
                for u, (kind, j) in enumerate(proj):
                    act_unit(act, u, 0, kind, j)
                act.sem_inc(free, 2)
                act_exp(act, 0)
                with act.Fori(0, NC - 1) as _i:
                    act_chunk(act, 0, True, True)
                    act_chunk(act, 1, True, True)
                act_chunk(act, 0, True, True)
                act_chunk(act, 1, False, False)

            @block.vector
            def _(dve):
                c = Chain(dve, steps)
                dve.sem_inc(y_free, 2)
                dve_max(dve, c, 0)
                dve_normalise(dve, c, 0)
                with dve.Fori(0, NC - 1) as i:
                    dve_chunk(dve, c, 0, i, True)
                    dve_chunk(dve, c, 1, i, True)
                dve_chunk(dve, c, 0, NC - 1, True)
                dve_chunk(dve, c, 1, NC - 1, False)


def phase_heavy(kit, S, out_d):
    nc, ins = kit.nc, kit.ins
    x, xn, rows, ident, rank = S["x0"], S["xn"], S["rows"], S["ident"], S["rank"]
    TQ, TK = NQ // P, NKV // P
    NG = TQ + TK
    with Room(nc, "hvy") as r:
        Wq = r.sb("Wq", [P, KD, HID])
        Wkv = r.sb("Wkv", [P, KD, 2 * HID])
        Wo = r.sb("Wo", [P, KG, D])
        gamma = r.sb("gamma", [P, KD])
        iota = r.sb("iota", [P, NKV])
        zero = r.sb("zero", [1, XW])
        rc = r.sb("rc", [P, 2, CT])
        gb = r.sb("gb", [P, D])
        G = r.sb("G", [P, 2, NQ + NKV])
        X = r.sb("X", [P, NG, XW])
        xT = r.sb("xT", [P, KD, NQ + NKV])
        flat_h = S["hT"][:].rearrange("p a b t -> p (a b t)")
        qT = flat_h[:, 0:KG * NQ].rearrange("p (g t) -> p g t", g=KG)
        kT = flat_h[:, KG * NQ:KG * (NQ + NKV)].rearrange("p (g t) -> p g t", g=KG)
        v = flat_h[:, KG * (NQ + NKV):KG * (NQ + NKV) + TK * HID].rearrange("p (j n) -> p j n", j=TK)
        mx = r.sb("mx", [P, 4])
        den = r.sb("den", [P, 4])
        Pr = r.sb("Pr", [P, 4, NKV])
        PT = r.sb("PT", [P, 2, TK, NQ])
        OT = r.sb("OT", [P, KG, NQ])
        Y = r.sb("Y", [P, TQ, D])
        Gs = r.sb("Gs", [P, CT, NQ])
        GT = r.sb("GT", [P, TQ, CH])
        o = r.sb("o", [P, CT, D])
        pu = r.ps("pu", [P, 8, 512])
        loads, consts, g_ready, g_free = r.sem("loads"), r.sem("consts"), r.sem("g_ready"), r.sem("g_free")
        gathered, x_ready, full, free = r.sem("gathered"), r.sem("x_ready"), r.sem("full"), r.sem("free")
        xT_ready, qkv_ready, s_done, s_free = r.sem("xT_ready"), r.sem("qkv_ready"), r.sem("s_done"), r.sem("s_free")
        mx_ready, e_ready, p_ready, p_free = r.sem("mx_ready"), r.sem("e_ready"), r.sem("p_ready"), r.sem("p_free")
        PT_ready, OT_ready, y_ready, all_free = r.sem("PT_ready"), r.sem("OT_ready"), r.sem("y_ready"), r.sem("all_free")
        gs_ready, gs_free, turned, GT_ready = r.sem("gs_ready"), r.sem("gs_free"), r.sem("turned"), r.sem("GT_ready")
        back, out_ready, stored, steps = r.sem("back"), r.sem("out_ready"), r.sem("stored"), r.sem("steps")
        added, o_full, o_free = r.sem("added"), r.sem("o_full"), r.sem("o_free")
        ranks = rank[:].rearrange("p (n s) t -> p n (s t)", s=B)
        LOOK = 2
        E = HB * TQ

        def pe_scores(pe, e):
            h, qt = e // TQ, e % TQ
            at = slice(DH * (h % 2), DH * (h % 2) + DH)
            take(pe, s_free)
            pe.matmul(pu[:, 4 + e % 3], qT[at, h // 2, qt * P:(qt + 1) * P], kT[at, h // 2],
                      start=True, stop=True).then_inc(s_done, 1)

        with nc.Block() as block:
            @block.sync
            def _(sp):
                for w, name in ((Wq, "wq_heavy"), (Wkv, "wkv_heavy"), (Wo, "wo_heavy")):
                    sp.dma_start(w[:], ins[name].rearrange("(k p) n -> p k n", p=P)).then_inc(loads, 16)
                sp.dma_start(gamma[:], ins["ghcol"]).then_inc(loads, 16)
                sp.dma_start(iota[:], ins["iota"].partition_broadcast(P)).then_inc(loads, 16)
                o_v = out_d.rearrange("(c j p) d -> c p j d", j=CT, p=P)
                with sp.Fori(0, B) as b:
                    with sp.Fori(0, NC) as c:
                        take(sp, out_ready)
                        sp.dma_start(o_v[bass.ds(b * NC + c, 1)].rearrange("a p j d -> p (a j) d"),
                                     x[:, bass.ds(b * TT + c * CT, CT)]).then_inc(stored, 16)
                        take(sp, stored, 16)

            @block.tensor
            def _(pe):
                pe.wait_ge(loads, 80)
                pe.wait_ge(consts, 1)
                pe.sem_inc(free, 4)
                pe.sem_inc(s_free, 3)
                pe.sem_inc(o_free, 1)
                with pe.Fori(0, B) as b:
                    for j in range(NG):
                        pe.matmul(pu[:, j, 0:XW], zero[:, 0:P], zero[:], start=True, stop=False)
                    with pe.Fori(0, NC) as c:
                        for t in range(CT):
                            take(pe, g_ready)
                            for j in range(NG):
                                mm = pe.matmul(pu[:, j, 0:XW], G[:, t % 2, j * P:(j + 1) * P],
                                               xn[:, bass.ds(b * TT + (c * CT + t), 1)].rearrange("p a d -> p (a d)"),
                                               start=False, stop=False)
                            mm.then_inc(g_free, 1)
                    for j in range(NG):
                        mm = pe.matmul(pu[:, j, 0:XW], zero[:, 0:P], zero[:], start=False, stop=True)
                    mm.then_inc(gathered, 1)
                    take(pe, x_ready)
                    u = 0
                    for h in range(KD):
                        for first, n in ((TQ, TK), (0, TQ)):
                            take(pe, free)
                            for j in range(n):
                                mm = pe.transpose(pu[:, u % 4, j * P:(j + 1) * P], X[:, first + j, h * P:(h + 1) * P], ident[:])
                            mm.then_inc(full, 1)
                            u += 1
                    take(pe, xT_ready)
                    for kind, j in [(n, j) for n in ("q", "k", "v") for j in range(CT)]:
                        take(pe, free)
                        for k in range(KD):
                            if kind == "q":
                                mm = pe.matmul(pu[:, u % 4, 0:NQ], Wq[:, k, j * P:(j + 1) * P], xT[:, k, 0:NQ],
                                               start=(k == 0), stop=(k == KD - 1))
                            elif kind == "k":
                                mm = pe.matmul(pu[:, u % 4], Wkv[:, k, j * P:(j + 1) * P], xT[:, k, NQ:],
                                               start=(k == 0), stop=(k == KD - 1))
                            else:
                                mm = pe.matmul(pu[:, u % 4], xT[:, k, NQ + j * P:NQ + (j + 1) * P], Wkv[:, k, HID:],
                                               start=(k == 0), stop=(k == KD - 1))
                        mm.then_inc(full, 1)
                        u += 1
                    take(pe, qkv_ready)
                    for e in range(LOOK):
                        pe_scores(pe, e)
                    for e in range(E):
                        h, qt = e // TQ, e % TQ
                        take(pe, p_ready)
                        take(pe, free)
                        for j in range(TK):
                            mm = pe.transpose(pu[:, u % 4, j * P:(j + 1) * P], Pr[:, e % 4, j * P:(j + 1) * P], ident[:])
                        mm.then_inc(full, 1)
                        u += 1
                        if e + LOOK < E:
                            pe_scores(pe, e + LOOK)
                        if qt == TQ - 1:
                            if h % 2 == 0:
                                take(pe, o_free)
                            take(pe, PT_ready)
                            at = DH * (h % 2)
                            for j in range(TK):
                                mm = pe.matmul(pu[at:at + DH, 7, 0:NQ], v[:, j, h * DH:(h + 1) * DH], PT[:, h % 2, j],
                                               start=(j == 0), stop=(j == TK - 1), tile_position=(0, at), skip_group_check=True)
                            if h % 2:
                                mm.then_inc(o_full, 1)
                    take(pe, OT_ready)
                    take(pe, free)
                    for j in range(TQ):
                        for k in range(KG):
                            mm = pe.matmul(pu[:, u % 4, j * D:(j + 1) * D], OT[:, k, j * P:(j + 1) * P], Wo[:, k],
                                           start=(k == 0), stop=(k == KG - 1))
                    mm.then_inc(full, 1)
                    take(pe, y_ready)
                    take(pe, free, 4)
                    pe.sem_inc(free, 4)
                    with pe.Fori(0, NC) as c:
                        take(pe, gs_ready)
                        for k in range(TQ):
                            for t in range(CT):
                                mm = pe.transpose(pu[:, k, t * P:(t + 1) * P], Gs[:, t, k * P:(k + 1) * P], ident[:])
                        mm.then_inc(turned, 1)
                        take(pe, GT_ready)
                        for t in range(CT):
                            for k in range(TQ):
                                mm = pe.matmul(pu[:, 4 + t // 2, t % 2 * D:(t % 2 + 1) * D], GT[:, k, t * P:(t + 1) * P], Y[:, k],
                                               start=(k == 0), stop=(k == TQ - 1))
                        mm.then_inc(back, 1)
                        take(pe, added)

            @block.scalar
            def _(act):
                act.wait_ge(loads, 80)
                with act.Fori(0, B) as b:
                    take(act, gathered)
                    act.activation(X[:], pu[:, 0:NG, 0:XW], ACT.Copy).then_inc(x_ready, 1)
                    u = 0
                    for h in range(KD):
                        for lo, hi in ((NQ, NQ + NKV), (0, NQ)):
                            take(act, full)
                            act.activation(xT[:, h, lo:hi], pu[:, u % 4, 0:hi - lo], ACT.Copy,
                                           scale=gamma[:, h:h + 1]).then_inc(free, 1)
                            u += 1
                    act.drain().then_inc(xT_ready, 1)
                    for kind, j in [(n, j) for n in ("q", "k", "v") for j in range(CT)]:
                        take(act, full)
                        if kind == "q":
                            last = act.activation(qT[:, j], pu[:, u % 4, 0:NQ], ACT.Copy, scale=DH ** -0.5)
                        elif kind == "k":
                            last = act.activation(kT[:, j], pu[:, u % 4], ACT.Copy)
                        else:
                            last = act.activation(v[:, j], pu[:, u % 4], ACT.Copy, scale=X[:, TQ + j, D + 1:D + 2])
                        last.then_inc(free, 1)
                        u += 1
                    act.drain().then_inc(qkv_ready, 1)

                    def exp(e):
                        take(act, mx_ready)
                        take(act, p_free)
                        act.activation(Pr[:, e % 4], pu[:, 4 + e % 3], ACT.Exp, bias=mx[:, e % 4:e % 4 + 1],
                                       accum_out=den[:, e % 4:e % 4 + 1]).then_inc(e_ready, 1)
                        act.drain().then_inc(s_free, 1)

                    for e in range(LOOK):
                        exp(e)
                    for e in range(E):
                        h, qt = e // TQ, e % TQ
                        take(act, full)
                        act.activation(PT[:, h % 2, :, qt * P:(qt + 1) * P],
                                       pu[:, u % 4].rearrange("p (j n) -> p j n", j=TK), ACT.Copy).then_inc(free, 1)
                        u += 1
                        act.drain().then_inc(p_free, 1)
                        if qt == TQ - 1:
                            act.sem_inc(PT_ready, 1)
                        if e + LOOK < E:
                            exp(e + LOOK)
                        if qt == TQ - 1 and h % 2:
                            take(act, o_full)
                            act.activation(OT[:, h // 2], pu[:, 7, 0:NQ], ACT.Copy).then_inc(o_free, 1)
                    act.drain().then_inc(OT_ready, 1)
                    take(act, full)
                    for j in range(TQ):
                        last = act.activation(Y[:, j], pu[:, u % 4, j * D:(j + 1) * D], ACT.Copy, scale=X[:, j, D:D + 1])
                    act.drain().then_inc(y_ready, 1)
                    act.sem_inc(free, 1)
                    with act.Fori(0, NC) as c:
                        take(act, turned)
                        act.activation(GT[:], pu[:, 0:TQ], ACT.Copy).then_inc(GT_ready, 1)

            @block.vector
            def _(dve):
                dve.memset(zero[:], 0.0).then_inc(consts, 1)
                dve.wait_ge(loads, 80)
                dve.sem_inc(g_free, 2)
                dve.sem_inc(p_free, 4)
                ch = Chain(dve, steps)
                gates = rows[:, 1, :, (3 + GATE) * D:(4 + GATE) * D]
                with dve.Fori(0, B) as b:
                    dve.tensor_copy(gb[:].unsqueeze(1), gates[:, bass.ds(b, 1)])
                    with dve.Fori(0, NC) as c:
                        ch.link(dve.tensor_copy(rc[:], ranks[:, :, bass.ds(b * TT + c * CT, CT)]))
                        for t in range(CT):
                            take(dve, g_free)
                            dve.tensor_scalar(G[:, t % 2, 0:NQ], iota[:, 0:NQ], rc[:, 0, t:t + 1], None, ALU.is_equal)
                            dve.tensor_scalar(G[:, t % 2, NQ:], iota[:], rc[:, 1, t:t + 1], None, ALU.is_equal)
                            dve.drain().then_inc(g_ready, 1)

                    def max_of(e):
                        take(dve, s_done)
                        ch.link(dve.tensor_reduce(mx[:, e % 4:e % 4 + 1], pu[:, 4 + e % 3], AX.X, ALU.max))
                        dve.tensor_scalar(mx[:, e % 4:e % 4 + 1], mx[:, e % 4:e % 4 + 1], -1.0, None,
                                          ALU.mult).then_inc(mx_ready, 1)

                    for e in range(LOOK):
                        max_of(e)
                    for e in range(E):
                        take(dve, e_ready)
                        d = den[:, e % 4:e % 4 + 1]
                        ch.link(dve.reciprocal(d, d))
                        dve.tensor_scalar(Pr[:, e % 4], Pr[:, e % 4], d, None, ALU.mult).then_inc(p_ready, 1)
                        if e + LOOK < E:
                            max_of(e + LOOK)
                    dve.drain()
                    with dve.Fori(0, NC) as c:
                        ch.link(dve.tensor_copy(rc[:], ranks[:, :, bass.ds(b * TT + c * CT, CT)]))
                        for t in range(CT):
                            last = dve.tensor_scalar(Gs[:, t], iota[:, 0:NQ], rc[:, 0, t:t + 1], None, ALU.is_equal)
                        dve.drain().then_inc(gs_ready, 1)
                        take(dve, back)
                        ch.link(dve.tensor_tensor(o[:], pu[:, 4:6].rearrange("p a (j d) -> p (a j) d", d=D),
                                                  row4(gb[:]), ALU.mult))
                        dve.sem_inc(added, 1)
                        xc = x[:, bass.ds(b * TT + c * CT, CT)]
                        ch.link(dve.tensor_tensor(xc, xc, o[:], ALU.add))
                        dve.sem_inc(out_ready, 1)


def two_layers(nc, ins, out_d):
    with ExitStack() as ctx:
        kit = Kit(nc, ins, ctx)

        def sb(name, shape, dt=F32):
            return ctx.enter_context(nc.sbuf_tensor(name, shape, dt))

        S = {
            "rows": sb("rows", [P, 2, B, 6 * D]),
            "cols": sb("cols", [P, 2, 2, KD, B]),
            "x0": sb("x", [P, NT, D]),
            "hT": sb("hT", [P, KD, B, T + 1]),
            "ident": sb("ident", [P, P]),
            "identb": sb("identb", [P, P], BF16),
            "lncol": sb("lncol", [P, 2, KD]),
            "identb_ready": ctx.enter_context(nc.semaphore("identb_ready")),
            "qk": nc.dram_tensor("qk_pieces", [2, 3, 2 * B, P, T], BF16, kind="Internal").ap(),
        }
        S["V"] = S["hT"][:].rearrange("p a b t -> p (a b t)")[:, 0:NT * D].rearrange("p (i t n) -> p i t n", i=4, t=TT)
        phase_modulation(kit, S)
        phase_norms(kit, S)
        phase_wkv(kit, S)
        phase_channel_mix(kit, S)
        phase_ffn(kit, S)
        phase_qkv(kit, S)
        phase_attention(kit, S)
        S["xn"] = sb("xn", [P, NT, XW])
        S["s4"] = sb("s4", [P, R4, TT])
        S["rank"] = sb("rank", [P, R4, TT])
        phase_route_scores(kit, S)
        phase_routing(kit, S)
        phase_light(kit, S)
        phase_heavy(kit, S, out_d)


def _laid_out(I):
    def rows(a):
        return np.ascontiguousarray(a)

    def col(v):
        return np.asarray(v).reshape(KD, P).T

    def cols(*vs):
        return np.ascontiguousarray(np.stack([col(v) for v in vs], 1))

    a = {"x": rows(I["L0_attn_x"].reshape(B * T, D))}
    for l in (0, 1):
        a[f"cT{l}"] = rows(I[f"L{l}_c"].T)
        a[f"L{l}_wmod"] = rows(I[f"L{l}_wmod"])
    for n in ("ln0_w", "ln0_b"):
        a[n] = rows(I["L0_attn_" + n])
    for n in ("Wk", "Wv", "Wr", "Wo", "Wfk", "Wfv", "Wfr"):
        a[n + "T"] = rows(I["L0_attn_" + n].T)
    a["lncol"] = cols(I["L0_attn_ln1_w"], I["L0_attn_ln1_b"])
    a["ln2col"] = cols(I["L0_attn_ln2_w"], I["L0_attn_ln2_b"])
    a["tmcol"] = cols(I["L0_attn_tmk"], I["L0_attn_tmv"], I["L0_attn_tmr"])
    a["uwcol"] = cols(I["L0_attn_time_first"], I["L0_attn_time_decay"])
    a["cmcol"] = cols(I["L0_attn_cmk"], I["L0_attn_cmr"])
    for n in ("w1", "w2", "b2"):
        a[n] = rows(I["L0_ffn_" + n])
    a["b1col"] = rows(I["L0_ffn_b1"].reshape(KH, P).T)
    for n in ("wq", "wk", "wv", "wo", "bv", "bo"):
        a[n] = rows(I["L1_attn_" + n])
    a["bqkcol"] = cols(I["L1_attn_bq"], I["L1_attn_bk"])
    a["q_tok"] = rows(I["L1_ffn_q_routing_token"])
    a["kv_tok"] = rows(I["L1_ffn_kv_routing_token"])
    for n in ("wq_light", "wkv_light", "wo_light", "wq_heavy", "wo_heavy"):
        a[n] = rows(I["L1_ffn_" + n])
    a["wkv_heavy"] = rows(I["L1_ffn_wkv_heavy"].reshape(HB, 2, DH, D).transpose(3, 1, 0, 2).reshape(D, 2 * HID))
    a["glcol"] = rows(col(I["L1_ffn_gamma_light"]))
    a["ghcol"] = rows(col(I["L1_ffn_gamma_heavy"]))
    a["ident"] = np.eye(P, dtype=np.float32)
    a["iota"] = np.arange(NKV, dtype=np.float32)
    return a


def kernel(**inputs):
    import concourse.bacc as _bacc
    from concourse.bass_utils import run_bass_kernel_spmd as _run

    nc = _bacc.Bacc("TRN2", target_bir_lowering=False, num_devices=1)
    arrays = _laid_out(inputs)
    ins = {n: nc.dram_tensor(f"in_{n}", a.shape, mybir.dt.from_np(a.dtype), kind="ExternalInput").ap()
           for n, a in arrays.items()}
    out = nc.dram_tensor("out", (B * T, D), F32, kind="ExternalOutput").ap()
    two_layers(nc, ins, out)
    r = _run(nc, [{f"in_{n}": a for n, a in arrays.items()}], core_ids=[0])
    return r.results[0]["out"].reshape(B, T, D)
```

```python
import math
from contextlib import ExitStack

import numpy as np
import concourse.bass as bass
from concourse import mybir

F32 = mybir.dt.float32
BF16 = mybir.dt.bfloat16
I32 = mybir.dt.int32
ALU = mybir.AluOpType
ACT = mybir.ActivationFunctionType
AX = mybir.AxisListType

P = 128
B = 2
T = 2048
D = 256
KD = D // P
NT = B * T // P
TT = T // P
CH = 512
CT = CH // P
NC = T // CH
H = 1024
KH = H // P
EPS = 1e-5
SHIFT, SCALE, GATE = 0, 1, 2
NEG = -1.0e30


class Kit:

    def __init__(self, nc, ins, ctx):
        self.nc, self.ins, self.ctx = nc, ins, ctx
        self.begun = ctx.enter_context(nc.semaphore("begun"))


def take(eng, sem, n=1):
    eng.wait_ge(sem, n)
    eng.sem_inc(sem, -n)


class Room:

    def __init__(self, nc, name):
        self.nc, self.name, self.stack, self.sems = nc, name, ExitStack(), []

    def __enter__(self):
        self.stack.__enter__()
        return self

    def __exit__(self, *a):
        if self.sems and a[0] is None:
            self.nc.clear_and_free_semaphores(self.sems)
            self.nc.all_engine_barrier()
        return self.stack.__exit__(*a)

    def sb(self, name, shape, dt=F32):
        return self.stack.enter_context(self.nc.sbuf_tensor(f"{self.name}_{name}", shape, dt))

    def ps(self, name, shape, dt=F32):
        return self.stack.enter_context(self.nc.psum_tensor(f"{self.name}_{name}", shape, dt))

    def sem(self, name):
        self.sems.append(self.nc.alloc_semaphore(name=f"{self.name}_{name}"))
        return self.sems[-1]


class Chain:

    def __init__(self, eng, sem):
        self.eng, self.sem = eng, sem

    def link(self, ins):
        ins.then_inc(self.sem, 1)
        take(self.eng, self.sem)


def sweep(eng, step):
    step(None, (0, 0), None)
    step((0, 0), (0, 1), None)
    with eng.Fori(0, NC - 1) as i:
        step((i, 1), (i + 1, 0), (i, 0))
        step((i + 1, 0), (i + 1, 1), (i, 1))
    step((NC - 1, 1), None, (NC - 1, 0))
    step(None, None, (NC - 1, 1))


def flat(ap):
    return ap.rearrange("p a b -> p (a b)")


def row4(row, n=CT):
    return row.unsqueeze(1).broadcast_to([row.shape[0], n, row.shape[1]])


def phase_modulation(kit, S):
    nc, ins = kit.nc, kit.ins
    with Room(nc, "mod") as r:
        cT = r.sb("cT", [P, 2, KD, B])
        silu_c = r.sb("silu_c", [P, 2, KD, B])
        wmod = r.sb("wmod", [P, 2, KD, 6 * D])
        ones = r.sb("ones", [P, P])
        rep = r.sb("rep", [P, 2 * KD * B, P])
        t1 = r.sb("t1", [P, 4, 2 * D])
        t2 = r.sb("t2", [P, 4, 2 * D])
        ps = r.ps("ps", [P, 4, 512])
        psc = r.ps("psc", [P, 32])
        loaded, silu_done, rep_done = r.sem("loaded"), r.sem("silu_done"), r.sem("rep_done")
        mm_done, evac_done, cols_done, steps = (r.sem("mm_done"), r.sem("evac_done"),
                                                r.sem("cols_done"), r.sem("steps"))
        rows, cols = S["rows"], S["cols"]
        with nc.Block() as block:
            @block.sync
            def _(sp):
                for l in range(2):
                    sp.dma_start(cT[:, l], ins[f"cT{l}"].rearrange("(k p) b -> p k b", p=P)).then_inc(loaded, 16)
                    sp.dma_start(wmod[:, l], ins[f"L{l}_wmod"].rearrange("(k p) n -> p k n", p=P)).then_inc(loaded, 16)

            @block.scalar
            def _(act):
                act.wait_ge(loaded, 64)
                act.activation(silu_c[:], cT[:], ACT.Silu).then_inc(silu_done, 1)

            @block.vector
            def _(dve):
                dve.memset(ones[:], 1.0).then_inc(kit.begun, 1)
                dve.wait_ge(kit.begun, 1)
                dve.wait_ge(silu_done, 1)
                sc = silu_c[:].rearrange("p l k b -> p (l k b)")
                for n in range(2 * KD * B):
                    last = dve.tensor_scalar(rep[:, n], ones[:], sc[:, n:n + 1], None, ALU.mult)
                last.then_inc(rep_done, 1)
                for n in range(12):
                    l, b, m = n // 6, n // 3 % 2, n % 3
                    dve.wait_ge(mm_done, n + 1)
                    dve.tensor_copy(rows[:, l, b, 512 * m:512 * m + 512], ps[:, n % 4]).then_inc(evac_done, 1)
                dve.wait_ge(evac_done, 12)
                n = 0
                for l in range(2):
                    for tr in range(2):
                        sc_row = rows[:, l, :, (3 * tr + SCALE) * D:(3 * tr + SCALE + 1) * D]
                        dve.tensor_scalar(sc_row, sc_row, 1.0, None, ALU.add)
                for l in range(2):
                    for tr in range(2):
                        g = rows[:, l, :, (3 * tr + GATE) * D:(3 * tr + GATE + 1) * D]
                        v = t1[:, 2 * l + tr].rearrange("p (b n) -> p b n", b=2)
                        w = t2[:, 2 * l + tr].rearrange("p (b n) -> p b n", b=2)
                        dve.tensor_scalar(v, g, 0.0, 2.0, ALU.is_ge, ALU.mult).then_inc(steps, 1)
                        dve.scalar_tensor_tensor(w, g, -1.0, g, ALU.mult, ALU.max).then_inc(steps, 1)
                        n += 2
                        dve.wait_ge(steps, n)
                        dve.tensor_scalar(v, v, -1.0, None, ALU.add).then_inc(steps, 1)
                        n += 1
                        dve.wait_ge(steps, n)
                        dve.scalar_tensor_tensor(g, w, 0.25, v, ALU.max, ALU.mult)
                dve.wait_ge(cols_done, 1)
                pc = psc[:, 0:16].rearrange("p (l m k b) -> p l m k b", l=2, m=2, k=2)
                dve.tensor_copy(cols[:, :, 0], pc[:, :, 0])
                dve.tensor_scalar(cols[:, :, 1], pc[:, :, 1], 1.0, None, ALU.add)

            @block.tensor
            def _(pe):
                pe.wait_ge(rep_done, 1)
                n = 0
                for l in range(2):
                    for b in range(B):
                        for m in range(3):
                            if n >= 4:
                                pe.wait_ge(evac_done, n - 3)
                            for k in range(KD):
                                mm = pe.matmul(ps[:, n % 4], rep[:, (l * KD + k) * B + b],
                                               wmod[:, l, k, 512 * m:512 * m + 512],
                                               start=(k == 0), stop=(k == KD - 1))
                            mm.then_inc(mm_done, 1)
                            n += 1
                for l in range(2):
                    for m in range(2):
                        for h in range(KD):
                            at = (3 * (1 - l) + m) * D + h * P
                            o = ((l * 2 + m) * KD + h) * B
                            for k in range(KD):
                                mm = pe.matmul(psc[:, o:o + B], wmod[:, l, k, at:at + P], silu_c[:, l, k],
                                               start=(k == 0), stop=(k == KD - 1))
                mm.then_inc(cols_done, 1)


class Norm:

    def __init__(self, r, name=""):
        self.st = r.sb(name + "st", [P, B, CT, 6])
        self.mv = r.sb(name + "mv", [P, B, CT, 2])
        self.rs = r.sb(name + "rs", [P, B, CT])
        self.eps = r.sb(name + "eps", [P, 1])
        self.mean_ready, self.root_ready = r.sem(name + "mean_ready"), r.sem(name + "root_ready")

    def stats(self, dve, chain, s, src, src_ready=None):
        for j in range(CT):
            last = dve.bn_stats(self.st[:, s, j], src[:, j])
            if j == 0 and src_ready is not None:
                last.then_inc(src_ready, 1)
        chain.link(last)
        for j in range(CT):
            last = dve.bn_aggr(self.mv[:, s, j], self.st[:, s, j])
        last.then_inc(self.mean_ready, 1)

    def stats_at(self, dve, chain, s, x, at):
        for j in range(CT):
            last = dve.bn_stats(self.st[:, s, j], flat(x[:, bass.ds(at + j, 1)]))
        chain.link(last)
        for j in range(CT):
            last = dve.bn_aggr(self.mv[:, s, j], self.st[:, s, j])
        last.then_inc(self.mean_ready, 1)

    def apply_at(self, dve, chain, s, out, x, at):
        take(dve, self.root_ready)
        chain.link(dve.reciprocal(self.rs[:, s], self.rs[:, s]))
        for j in range(CT):
            last = dve.tensor_scalar(out[:, j:j + 1], x[:, bass.ds(at + j, 1)], self.mv[:, s, j, 0:1],
                                     self.rs[:, s, j:j + 1], ALU.subtract, ALU.mult)
        return last

    def root(self, act, s):
        take(act, self.mean_ready)
        act.activation(self.rs[:, s], self.mv[:, s, :, 1], ACT.Sqrt, bias=self.eps[:]).then_inc(self.root_ready, 1)

    def apply(self, dve, chain, s, out, src):
        take(dve, self.root_ready)
        chain.link(dve.reciprocal(self.rs[:, s], self.rs[:, s]))
        for j in range(CT):
            last = dve.tensor_scalar(out[:, j], src[:, j], self.mv[:, s, j, 0:1], self.rs[:, s, j:j + 1],
                                     ALU.subtract, ALU.mult)
        return last


def transposes(pe, out, src, ident):
    for h in range(KD):
        for j in range(CT):
            last = pe.transpose(out[:, h, j * P:(j + 1) * P], src[:, j, h * P:(h + 1) * P], ident)
    return last


def phase_norms(kit, S):
    nc, ins = kit.nc, kit.ins
    x0, hT, rows, ident = S["x0"], S["hT"], S["rows"], S["ident"]
    with Room(nc, "nrm") as r:
        xin = r.sb("xin", [P, B, CT, D])
        w = r.sb("w", [P, B, CT, D])
        n3 = r.sb("n3", [P, B, CT, D])
        ln0 = r.sb("ln0", [P, 2, D])
        lncol = S["lncol"]
        pT = r.ps("pT", [P, B, KD, CH])
        loads, x_in, x_used = r.sem("loads"), [r.sem("x_in0"), r.sem("x_in1")], r.sem("x_used")
        steps, zeroed = r.sem("steps"), r.sem("zeroed")
        n3_free, n3_ready, turned, h_ready = r.sem("n3_free"), r.sem("n3_ready"), r.sem("turned"), r.sem("h_ready")
        norm = Norm(r)
        x_d = ins["x"].rearrange("(s c j p) d -> s c p j d", s=B, c=NC, p=P)
        with nc.Block() as block:
            @block.sync
            def _(sp):
                sp.dma_start(ident[:], ins["ident"]).then_inc(loads, 16)
                for n, name in enumerate(("ln0_w", "ln0_b")):
                    sp.dma_start(ln0[:, n], ins[name].partition_broadcast(P)).then_inc(loads, 16)
                sp.dma_start(lncol[:], ins["lncol"]).then_inc(loads, 16)
                with sp.Fori(0, NC) as i:
                    for s in range(B):
                        take(sp, x_used)
                        sp.dma_start(xin[:, s], x_d[s, bass.ds(i, 1)].rearrange("a p j d -> p (a j) d")).then_inc(x_in[s], 16)

            @block.gpsimd
            def _(pool):
                pool.memset(hT[:, :, :, 0:1], 0.0).then_inc(zeroed, 1)

            @block.vector
            def _(dve):
                dve.wait_ge(loads, 64)
                dve.memset(norm.eps[:], EPS).then_inc(zeroed, 1)
                dve.sem_inc(x_used, 2)
                dve.sem_inc(n3_free, 2)
                with dve.Fori(0, NC) as i:
                    c = Chain(dve, steps)
                    for s in range(B):
                        take(dve, x_in[s], 16)
                        norm.stats(dve, c, s, xin[:, s])
                    for s in range(B):
                        c.link(norm.apply(dve, c, s, w[:, s], xin[:, s]))
                        c.link(dve.tensor_tensor(w[:, s], w[:, s], row4(rows[:, 0, s, SCALE * D:(SCALE + 1) * D]), ALU.mult))
                        c.link(dve.tensor_tensor(w[:, s], w[:, s], row4(rows[:, 0, s, SHIFT * D:(SHIFT + 1) * D]), ALU.add))
                        norm.stats(dve, c, s, w[:, s], x_used)
                    for s in range(B):
                        c.link(norm.apply(dve, c, s, w[:, s], w[:, s]))
                        c.link(dve.tensor_tensor(w[:, s], w[:, s], row4(ln0[:, 0]), ALU.mult))
                        x0c = x0[:, bass.ds(i * CT + s * TT, CT)]
                        c.link(dve.tensor_tensor(x0c, w[:, s], row4(ln0[:, 1]), ALU.add))
                        norm.stats_at(dve, c, s, x0, i * CT + s * TT)
                    for s in range(B):
                        take(dve, n3_free)
                        norm.apply_at(dve, c, s, n3[:, s], x0, i * CT + s * TT).then_inc(n3_ready, 1)

            @block.tensor
            def _(pe):
                pe.wait_ge(loads, 64)
                with pe.Fori(0, NC) as i:
                    for s in range(B):
                        take(pe, h_ready)
                        take(pe, n3_ready)
                        transposes(pe, pT[:, s], n3[:, s], ident[:]).then_inc(turned, 1)

            @block.scalar
            def _(act):
                act.wait_ge(loads, 64)
                act.wait_ge(zeroed, 2)
                act.sem_inc(h_ready, 2)
                with act.Fori(0, NC) as i:
                    for n in range(3):
                        for s in range(B):
                            norm.root(act, s)
                    for s in range(B):
                        take(act, turned)
                        for h in range(KD):
                            last = act.activation(hT[:, h, s, bass.ds(i * CH + 1, CH)], pT[:, s, h], ACT.Identity,
                                                  scale=lncol[:, 0, h:h + 1], bias=lncol[:, 1, h:h + 1])
                            if h == 0:
                                last.then_inc(n3_free, 1)
                        last.then_inc(h_ready, 1)


def phase_wkv(kit, S):
    nc, ins = kit.nc, kit.ins
    hT, yT = S["hT"], S["hT"]
    with Room(nc, "wkv") as r:
        W = r.sb("W", [P, 3, KD, D])
        tm = r.sb("tm", [P, 3, KD])
        omt = r.sb("omt", [P, 3, KD])
        uw = r.sb("uw", [P, 2, KD])
        xm = r.sb("xm", [P, B, 3, KD, CH])
        kv = r.sb("kv", [P, B, 2, KD, CH])
        sr = r.sb("sr", [P, B, KD, CH])
        pp = r.sb("pp", [P, B, KD, CH + 1])
        aa = r.sb("aa", [P, B, KD, CH + 1])
        bb = r.sb("bb", [P, B, KD, CH + 1])
        pm = r.sb("pm", [P, KD, CH])
        ex = r.sb("ex", [P, B, 4, KD, CH])
        ps = r.ps("ps", [P, 3, KD, CH])
        loads, consts, a_ready, xm_ready = r.sem("loads"), r.sem("consts"), r.sem("a_ready"), r.sem("xm_ready")
        proj_done, kv_ready, ex_ready, e_ready = r.sem("proj_done"), r.sem("kv_ready"), r.sem("ex_ready"), r.sem("e_ready")
        y_ready, steps, ps_free = r.sem("y_ready"), r.sem("steps"), r.sem("ps_free")

        def halves(t):
            return t.rearrange("p h n -> p (h n)")

        with nc.Block() as block:
            @block.sync
            def _(sp):
                for n, name in enumerate(("WkT", "WvT", "WrT")):
                    sp.dma_start(W[:, n], ins[name].rearrange("(k p) n -> p k n", p=P)).then_inc(loads, 16)
                sp.dma_start(tm[:], ins["tmcol"]).then_inc(loads, 16)
                sp.dma_start(uw[:], ins["uwcol"]).then_inc(loads, 16)

            @block.scalar
            def _(act):
                act.wait_ge(loads, 80)
                act.activation(uw[:, 1], uw[:, 1], ACT.Exp).then_inc(consts, 1)
                act.wait_ge(consts, 5)

                def step(now, following, before):
                    if following:
                        i, s = following
                        for n in range(3):
                            for h in range(KD):
                                last = act.activation(xm[:, s, n, h], hT[:, h, s, bass.ds(i * CH, CH)],
                                                      ACT.Copy, scale=omt[:, n, h:h + 1])
                        last.then_inc(a_ready, 1)
                    if now:
                        s = now[1]
                        take(act, ex_ready)
                        ee = ex[:, s].rearrange("p a h n -> p (a h n)")
                        act.activation(ee, ee, ACT.Exp).then_inc(e_ready, 1)
                    if following:
                        s = following[1]
                        take(act, proj_done)
                        take(act, y_ready)
                        for n in range(2):
                            for h in range(KD):
                                act.activation(kv[:, s, n, h], ps[:, n, h], ACT.Copy)
                        for h in range(KD):
                            last = act.activation(sr[:, s, h], ps[:, 2, h], ACT.Sigmoid)
                        last.then_inc(kv_ready, 1)

                sweep(act, step)

            @block.tensor
            def _(pe):
                pe.wait_ge(loads, 80)
                pe.wait_ge(consts, 5)

                def step(now, following, before):
                    if following:
                        s = following[1]
                        take(pe, xm_ready)
                        take(pe, ps_free)
                        for n in range(3):
                            for o in range(KD):
                                for k in range(KD):
                                    mm = pe.matmul(ps[:, n, o], W[:, n, k, o * P:(o + 1) * P], xm[:, s, n, k],
                                                   start=(k == 0), stop=(k == KD - 1))
                        mm.then_inc(proj_done, 1)

                sweep(pe, step)

            @block.vector
            def _(dve):
                dve.wait_ge(consts, 1)
                dve.tensor_scalar(uw[:, 1], uw[:, 1], -1.0, None, ALU.mult).then_inc(consts, 1)
                dve.tensor_scalar(omt[:], tm[:], -1.0, 1.0, ALU.mult, ALU.add).then_inc(consts, 1)
                dve.memset(pp[:, :, :, 0:1], -1e38)
                dve.memset(aa[:, :, :, 0:1], 0.0)
                dve.memset(bb[:, :, :, 0:1], 0.0).then_inc(consts, 1)
                dve.sem_inc(y_ready, 2)
                dve.sem_inc(ps_free, 1)
                dve.wait_ge(consts, 4)
                dve.sem_inc(consts, 1)
                c = Chain(dve, steps)

                def step(now, following, before):
                    if now:
                        s = now[1]
                        take(dve, kv_ready)
                        k_t, v_t = kv[:, s, 0], kv[:, s, 1]
                        cur, old = pp[:, s, :, 1:CH + 1], pp[:, s, :, 0:CH]
                        for h in range(KD):
                            last = dve.tensor_tensor_scan(pp[:, s, h, 1:CH + 1], uw[:, 1, h:h + 1].broadcast_to([P, CH]),
                                                          kv[:, s, 0, h], pp[:, s, h, 0:1], ALU.add, ALU.max)
                            if h == 0:
                                last.then_inc(ps_free, 1)
                        c.link(last)
                        for h in range(KD):
                            dve.scalar_tensor_tensor(ex[:, s, 0, h], pp[:, s, h, 0:CH], uw[:, 1, h:h + 1],
                                                     pp[:, s, h, 1:CH + 1], ALU.add, ALU.subtract)
                            last = dve.scalar_tensor_tensor(pm[:, h], kv[:, s, 0, h], uw[:, 0, h:h + 1],
                                                            pp[:, s, h, 0:CH], ALU.add, ALU.max)
                        c.link(last)
                        dve.tensor_tensor(ex[:, s, 1], k_t, cur, ALU.subtract)
                        dve.tensor_tensor(ex[:, s, 2], old, pm[:], ALU.subtract)
                        for h in range(KD):
                            last = dve.scalar_tensor_tensor(ex[:, s, 3, h], kv[:, s, 0, h], uw[:, 0, h:h + 1],
                                                            pm[:, h], ALU.add, ALU.subtract)
                        last.then_inc(ex_ready, 1)
                    if following:
                        i, s = following
                        take(dve, a_ready)
                        for n in range(3):
                            for h in range(KD):
                                last = dve.scalar_tensor_tensor(xm[:, s, n, h], hT[:, h, s, bass.ds(i * CH + 1, CH)],
                                                                tm[:, n, h:h + 1], xm[:, s, n, h], ALU.mult, ALU.add)
                        last.then_inc(xm_ready, 1)
                    if now:
                        i, s = now
                        v_t = kv[:, s, 1]
                        take(dve, e_ready)
                        k_v = kv[:, s, 0]
                        c.link(dve.tensor_tensor(k_v, ex[:, s, 1], v_t, ALU.mult))
                        for h in range(KD):
                            dve.tensor_tensor_scan(aa[:, s, h, 1:CH + 1], ex[:, s, 0, h], kv[:, s, 0, h],
                                                   aa[:, s, h, 0:1], ALU.mult, ALU.add)
                            last = dve.tensor_tensor_scan(bb[:, s, h, 1:CH + 1], ex[:, s, 0, h], ex[:, s, 1, h],
                                                          bb[:, s, h, 0:1], ALU.mult, ALU.add)
                        c.link(last)
                        f = ex[:, s, 3]
                        dve.tensor_tensor(k_v, ex[:, s, 2], aa[:, s, :, 0:CH], ALU.mult)
                        dve.tensor_tensor(v_t, f, v_t, ALU.mult)
                        c.link(dve.tensor_tensor(ex[:, s, 1], ex[:, s, 2], bb[:, s, :, 0:CH], ALU.mult))
                        dve.tensor_tensor(k_v, k_v, v_t, ALU.add)
                        c.link(dve.tensor_tensor(ex[:, s, 1], ex[:, s, 1], f, ALU.add))
                        dve.tensor_tensor(k_v, k_v, sr[:, s], ALU.mult)
                        c.link(dve.reciprocal(ex[:, s, 1], ex[:, s, 1]))
                        c.link(dve.tensor_tensor(yT[:, :, s, bass.ds(i * CH, CH)], k_v, ex[:, s, 1], ALU.mult))
                        for t in (pp, aa, bb):
                            last = dve.tensor_copy(t[:, s, :, 0:1], t[:, s, :, CH:CH + 1])
                        dve.drain().then_inc(y_ready, 1)

                sweep(dve, step)


def phase_channel_mix(kit, S):
    nc, ins = kit.nc, kit.ins
    x0, hT, rows, ident = S["x0"], S["hT"], S["rows"], S["ident"]
    with Room(nc, "cmx") as r:
        Wo = r.sb("Wo", [P, KD, D])
        Wfk = r.sb("Wfk", [P, KD, H])
        Wfv = r.sb("Wfv", [P, KH, D])
        Wfr = r.sb("Wfr", [P, KD, D])
        ln2 = r.sb("ln2", [P, 2, KD])
        cm = r.sb("cm", [P, 2, KD])
        omc = r.sb("omc", [P, 2, KD])
        xin = r.sb("xin", [P, B, CT, D])
        yc = r.sb("yc", [P, B, KD, CH])
        x1 = r.sb("x1", [P, B, CT, D])
        n2 = r.sb("n2", [P, B, CT, D])
        h2T = r.sb("h2T", [P, B, KD, CH + 1])
        xm = r.sb("xm", [P, B, 2, KD, CH])
        kf = r.sb("kf", [P, B, KH, CH])
        sg = r.sb("sg", [P, B, CT, D])
        norm = Norm(r)
        pA = r.ps("pA", [P, CT, D])
        pT = r.ps("pT", [P, KD, CH])
        pF = r.ps("pF", [P, 2, CH])
        pO = r.ps("pO", [P, 2, 512])
        loads, consts, x_in, x_free = r.sem("loads"), r.sem("consts"), [r.sem("x_in0"), r.sem("x_in1")], r.sem("x_free")
        y_ready, wo_done, pA_free = r.sem("y_ready"), r.sem("wo_done"), r.sem("pA_free")
        n_ready, turned, t_free = r.sem("n_ready"), r.sem("turned"), r.sem("t_free")
        a_steps, a_ready, xm_ready = r.sem("a_steps"), r.sem("a_ready"), r.sem("xm_ready")
        fk_done, relu_ready, fk_free, kf_ready = r.sem("fk_done"), r.sem("relu_ready"), r.sem("fk_free"), r.sem("kf_ready")
        r_done, kv_done, o_free, sg_ready = r.sem("r_done"), r.sem("kv_done"), r.sem("o_free"), r.sem("sg_ready")
        steps = r.sem("steps")
        x_d = ins["x"].rearrange("(s c j p) d -> s c p j d", s=B, c=NC, p=P)
        EARLY = 6
        with nc.Block() as block:
            @block.sync
            def _(sp):
                for w, name in ((Wo, "WoT"), (Wfk, "WfkT"), (Wfv, "WfvT"), (Wfr, "WfrT")):
                    sp.dma_start(w[:], ins[name].rearrange("(k p) n -> p k n", p=P)).then_inc(loads, 16)
                sp.dma_start(ln2[:], ins["ln2col"]).then_inc(loads, 16)
                sp.dma_start(cm[:], ins["cmcol"]).then_inc(loads, 16)
                with sp.Fori(0, NC) as i:
                    for s in range(B):
                        take(sp, x_free)
                        sp.dma_start(xin[:, s], x_d[s, bass.ds(i, 1)].rearrange("a p j d -> p (a j) d")).then_inc(x_in[s], 16)

            @block.scalar
            def _(act):
                act.wait_ge(loads, 96)
                act.wait_ge(consts, 1)
                c = Chain(act, a_steps)

                def step(now, following, before):
                    if following:
                        i, s = following
                        for h in range(KD):
                            last = act.activation(yc[:, s, h], hT[:, h, s, bass.ds(i * CH, CH)], ACT.Copy)
                        last.then_inc(y_ready, 1)
                    if now:
                        s = now[1]
                        for o in range(KH):
                            take(act, fk_done)
                            act.activation(kf[:, s, o], pF[:, o % 2], ACT.Relu).then_inc(relu_ready, 1)
                    if following:
                        norm.root(act, following[1])
                    if now:
                        take(act, r_done)
                        act.activation(sg[:, s], pA[:], ACT.Sigmoid).then_inc(sg_ready, 1)
                    if following:
                        s = following[1]
                        take(act, turned)
                        c.link(act.activation(h2T[:, s, :, 0:1], h2T[:, s, :, CH:CH + 1], ACT.Copy))
                        for h in range(KD):
                            last = act.activation(h2T[:, s, h, 1:CH + 1], pT[:, h], ACT.Identity,
                                                  scale=ln2[:, 0, h:h + 1], bias=ln2[:, 1, h:h + 1])
                        c.link(last)
                        for n in range(2):
                            for h in range(KD):
                                last = act.activation(xm[:, s, n, h], h2T[:, s, h, 0:CH], ACT.Copy, scale=omc[:, n, h:h + 1])
                                if n == h == 0:
                                    last.then_inc(t_free, 1)
                        last.then_inc(a_ready, 1)

                sweep(act, step)

            @block.tensor
            def _(pe):
                pe.wait_ge(loads, 96)
                pe.sem_inc(x_free, 2)

                def step(now, following, before):
                    if now:
                        s = now[1]
                        take(pe, xm_ready)
                        for o in range(EARLY):
                            hidden(s, o)
                    if following:
                        s = following[1]
                        take(pe, pA_free)
                        take(pe, y_ready)
                        for j in range(CT):
                            for k in range(KD):
                                mm = pe.matmul(pA[:, j], yc[:, s, k, j * P:(j + 1) * P], Wo[:, k],
                                               start=(k == 0), stop=(k == KD - 1))
                        mm.then_inc(wo_done, 1)
                    if now:
                        s = now[1]
                        for o in range(EARLY, KH):
                            hidden(s, o)
                        take(pe, pA_free)
                        for j in range(CT):
                            for k in range(KD):
                                mm = pe.matmul(pA[:, j], xm[:, s, 1, k, j * P:(j + 1) * P], Wfr[:, k],
                                               start=(k == 0), stop=(k == KD - 1))
                        mm.then_inc(r_done, 1)
                        take(pe, kf_ready)
                        back(s, 0)
                    if following:
                        s = following[1]
                        take(pe, n_ready)
                        take(pe, t_free)
                        transposes(pe, pT, n2[:, s], ident[:]).then_inc(turned, 1)
                    if now:
                        for j in range(1, CT):
                            back(now[1], j)

                def hidden(s, o):
                    take(pe, fk_free)
                    for k in range(KD):
                        mm = pe.matmul(pF[:, o % 2], Wfk[:, k, o * P:(o + 1) * P], xm[:, s, 0, k],
                                       start=(k == 0), stop=(k == KD - 1))
                    mm.then_inc(fk_done, 1)

                def back(s, j):
                    take(pe, o_free)
                    for k in range(KH):
                        mm = pe.matmul(pO[:, j % 2, 0:D], kf[:, s, k, j * P:(j + 1) * P], Wfv[:, k],
                                       start=(k == 0), stop=(k == KH - 1))
                    mm.then_inc(kv_done, 1)

                sweep(pe, step)

            @block.vector
            def _(dve):
                dve.wait_ge(loads, 96)
                dve.tensor_scalar(omc[:], cm[:], -1.0, 1.0, ALU.mult, ALU.add)
                dve.memset(h2T[:, :, :, CH:CH + 1], 0.0)
                dve.memset(norm.eps[:], EPS).then_inc(consts, 1)
                dve.sem_inc(pA_free, 1)
                dve.sem_inc(t_free, 1)
                dve.sem_inc(fk_free, 2)
                dve.sem_inc(o_free, 2)
                c = Chain(dve, steps)

                def square(s, o):
                    take(dve, relu_ready)
                    dve.tensor_tensor(kf[:, s, o], kf[:, s, o], kf[:, s, o], ALU.mult).then_inc(fk_free, 1)

                def gated(s, j):
                    take(dve, kv_done)
                    dve.tensor_tensor(sg[:, s, j], sg[:, s, j], pO[:, j % 2, 0:D], ALU.mult).then_inc(o_free, 1)

                def step(now, following, before):
                    if now:
                        for o in range(EARLY):
                            square(now[1], o)
                    if following:
                        i, s = following
                        take(dve, wo_done)
                        c.link(dve.tensor_tensor(x1[:, s], x0[:, bass.ds(i * CT + s * TT, CT)], pA[:], ALU.add))
                        norm.stats(dve, c, s, x1[:, s], pA_free)
                    if now:
                        for o in range(EARLY, KH):
                            square(now[1], o)
                        dve.drain().then_inc(kf_ready, 1)
                    if following:
                        s = following[1]
                        norm.apply(dve, c, s, n2[:, s], x1[:, s]).then_inc(n_ready, 1)
                    if now:
                        take(dve, sg_ready)
                        dve.sem_inc(pA_free, 1)
                        gated(now[1], 0)
                    if following:
                        s = following[1]
                        take(dve, a_ready)
                        for n in range(2):
                            for h in range(KD):
                                last = dve.scalar_tensor_tensor(xm[:, s, n, h], h2T[:, s, h, 1:CH + 1], cm[:, n, h:h + 1],
                                                                xm[:, s, n, h], ALU.mult, ALU.add)
                        last.then_inc(xm_ready, 1)
                    if now:
                        i, s = now
                        for j in range(1, CT):
                            gated(s, j)
                        dve.drain()
                        take(dve, x_in[s], 16)
                        c.link(dve.tensor_tensor(sg[:, s], sg[:, s], x1[:, s], ALU.add))
                        c.link(dve.tensor_tensor(sg[:, s], sg[:, s], row4(rows[:, 0, s, GATE * D:(GATE + 1) * D]), ALU.mult))
                        dve.tensor_tensor(x0[:, bass.ds(i * CT + s * TT, CT)], sg[:, s], xin[:, s], ALU.add).then_inc(x_free, 1)

                sweep(dve, step)


def binarized(kit, r, S, w1T, w2T):
    nc, ins, ident = kit.nc, kit.ins, S["ident"]
    with Room(nc, "bin") as q:
        w = [q.sb(f"w{n}", [P, H // P * D]) for n in range(2)]
        sgn = [q.sb(f"s{n}", [P, H // P * D]) for n in range(2)]
        al = [q.sb("al0", [P, KH]), q.sb("al1", [P, KD])]
        ps = q.ps("ps", [P, 4, 4, P])
        loaded, signed, ready, turned, freed, steps = (q.sem("loaded"), q.sem("signed"), q.sem("ready"),
                                                       q.sem("turned"), q.sem("freed"), q.sem("steps"))
        shape = [(KH, D), (KD, H)]
        blocks = [(n, a, k) for n in range(2) for a in range(shape[n][1] // P) for k in range(shape[n][0])]

        def view(t, n):
            return t[n][:].rearrange("p (k m) -> p k m", k=shape[n][0])

        with nc.Block() as block:
            @block.sync
            def _(sp):
                for n, name in enumerate(("w1", "w2")):
                    sp.dma_start(view(w, n), ins[name].rearrange("(k p) m -> p k m", p=P)).then_inc(loaded, 16)

            @block.scalar
            def _(act):
                act.wait_ge(loaded, 32)
                for n in range(2):
                    act.activation(sgn[n][:], w[n][:], ACT.Sign).then_inc(signed, 1)

            @block.vector
            def _(dve):
                dve.wait_ge(loaded, 32)
                dve.wait_ge(signed, 2)
                c = Chain(dve, steps)
                for n in range(2):
                    k, m = shape[n]
                    c.link(dve.tensor_reduce(al[n][:], view(w, n), AX.X, ALU.add, apply_absolute_value=True))
                    c.link(dve.tensor_scalar(al[n][:], al[n][:], 1.0 / m, None, ALU.mult))
                    for j in range(k):
                        last = dve.scalar_tensor_tensor(view(sgn, n)[:, j], view(sgn, n)[:, j], al[n][:, j:j + 1],
                                                        view(w, n)[:, j], ALU.mult, ALU.subtract)
                    c.link(last)
                    dve.tensor_tensor(w[n][:], w[n][:], sgn[n][:], ALU.add).then_inc(ready, 1)
                for g in range(len(blocks) // 4):
                    dve.wait_ge(turned, g + 1)
                    n, a, k = blocks[4 * g]
                    out = (w1T, w2T)[n]
                    if n == 0:
                        dve.tensor_copy(out[:, a, k * P:(k + 4) * P], ps[:, g % 4].rearrange("p a b -> p (a b)")).then_inc(freed, 1)
                    else:
                        dve.tensor_copy(out[:, a:a + 2].rearrange("p a b -> p (a b)"), ps[:, g % 4].rearrange("p a b -> p (a b)")).then_inc(freed, 1)

            @block.tensor
            def _(pe):
                for i, (n, a, k) in enumerate(blocks):
                    g = i // 4
                    if i % 4 == 0:
                        pe.wait_ge(ready, n + 1)
                        if g >= 4:
                            pe.wait_ge(freed, g - 3)
                    mm = pe.transpose(ps[:, g % 4, i % 4], view(w, n)[:, k, a * P:(a + 1) * P], ident[:])
                    if i % 4 == 3:
                        mm.then_inc(turned, 1)


def phase_ffn(kit, S):
    nc, ins = kit.nc, kit.ins
    x, rows, cols, ident = S["x0"], S["rows"], S["cols"], S["ident"]
    with Room(nc, "ffn") as r:
        w1T = r.sb("w1T", [P, KD, H])
        w2T = r.sb("w2T", [P, KH, D])
        binarized(kit, r, S, w1T, w2T)
        b1 = r.sb("b1", [P, KH])
        b2 = r.sb("b2", [P, D])
        n1 = r.sb("n1", [P, B, CT, D])
        fT = r.sb("fT", [P, B, KD, CH])
        g = r.sb("g", [P, B, KH, CH])
        o = r.sb("o", [P, B, CT, D])
        norm = Norm(r)
        pT = r.ps("pT", [P, KD, CH])
        pF = r.ps("pF", [P, 4, CH])
        pO = r.ps("pO", [P, 2, 512])
        loads, consts = r.sem("loads"), r.sem("consts")
        n_ready, turned, t_free, f_ready = r.sem("n_ready"), r.sem("turned"), r.sem("t_free"), r.sem("f_ready")
        w1_done, pF_free, g_ready = r.sem("w1_done"), r.sem("pF_free"), r.sem("g_ready")
        w2_done, o_free, steps = r.sem("w2_done"), r.sem("o_free"), r.sem("steps")
        with nc.Block() as block:
            @block.sync
            def _(sp):
                sp.dma_start(b1[:], ins["b1col"]).then_inc(loads, 16)
                sp.dma_start(b2[:], ins["b2"].partition_broadcast(P)).then_inc(loads, 16)

            @block.scalar
            def _(act):
                act.wait_ge(loads, 32)
                act.wait_ge(consts, 1)

                def step(now, following, before):
                    if following:
                        norm.root(act, following[1])
                    if now:
                        s = now[1]
                        for m in range(KH):
                            take(act, w1_done)
                            act.activation(g[:, s, m], pF[:, m % 4], ACT.Gelu, bias=b1[:, m:m + 1]).then_inc(pF_free, 1)
                        act.drain().then_inc(g_ready, 1)
                    if following:
                        s = following[1]
                        take(act, turned)
                        for h in range(KD):
                            last = act.activation(fT[:, s, h], pT[:, h], ACT.Identity,
                                                  scale=cols[:, 0, 1, h, s:s + 1], bias=cols[:, 0, 0, h, s:s + 1])
                        last.then_inc(f_ready, 1)

                sweep(act, step)

            @block.tensor
            def _(pe):
                pe.sem_inc(pF_free, 4)

                def step(now, following, before):
                    if now:
                        s = now[1]
                        take(pe, f_ready)
                        for m in range(KH):
                            take(pe, pF_free)
                            for k in range(KD):
                                mm = pe.matmul(pF[:, m % 4], w1T[:, k, m * P:(m + 1) * P], fT[:, s, k],
                                               start=(k == 0), stop=(k == KD - 1))
                            mm.then_inc(w1_done, 1)
                    if following:
                        take(pe, n_ready)
                        transposes(pe, pT, n1[:, following[1]], ident[:]).then_inc(turned, 1)
                    if before:
                        s = before[1]
                        take(pe, g_ready)
                        for j in range(CT):
                            take(pe, o_free)
                            for k in range(KH):
                                mm = pe.matmul(pO[:, j % 2, 0:D], g[:, s, k, j * P:(j + 1) * P], w2T[:, k],
                                               start=(k == 0), stop=(k == KH - 1))
                            mm.then_inc(w2_done, 1)

                sweep(pe, step)

            @block.vector
            def _(dve):
                dve.wait_ge(loads, 32)
                dve.memset(norm.eps[:], EPS).then_inc(consts, 1)
                dve.sem_inc(o_free, 2)
                c = Chain(dve, steps)

                def step(now, following, before):
                    if following:
                        i, s = following
                        norm.stats_at(dve, c, s, x, i * CT + s * TT)
                        norm.apply_at(dve, c, s, n1[:, s], x, i * CT + s * TT).then_inc(n_ready, 1)
                    if before:
                        i, s = before
                        for j in range(CT):
                            take(dve, w2_done)
                            dve.tensor_tensor(o[:, s, j], pO[:, j % 2, 0:D], b2[:], ALU.add).then_inc(o_free, 1)
                        dve.drain()
                        c.link(dve.tensor_tensor(o[:, s], o[:, s], row4(rows[:, 0, s, (3 + GATE) * D:(4 + GATE) * D]), ALU.mult))
                        xc = x[:, bass.ds(i * CT + s * TT, CT)]
                        c.link(dve.tensor_tensor(xc, xc, o[:, s], ALU.add))

                sweep(dve, step)

HA, DA = 16, 16
GH = 4
PAIRS = (0, 0, 0, 1, 1, 2), (0, 1, 2, 0, 1, 0)
KQ = len(PAIRS[0]) * DA
ROWS = KQ + 3


def phase_qkv(kit, S):
    nc, ins = kit.nc, kit.ins
    x, cols, ident, V = S["x0"], S["cols"], S["ident"], S["V"]
    with Room(nc, "qkv") as r:
        W = r.sb("W", [P, 3, KD, D])
        bqk = r.sb("bqk", [P, 2, KD])
        bv = r.sb("bv", [P, D])
        n1 = r.sb("n1", [P, B, CT, D])
        fT = r.sb("fT", [P, B, KD, CH])
        full = r.sb("full", [P, B, 4, CH])
        piece = r.sb("piece", [P, B, 3, 4, CH], BF16)
        norm = Norm(r)
        pT = r.ps("pT", [P, KD, CH])
        pF = r.ps("pF", [P, 4, CH])
        pV = r.ps("pV", [P, CT, D])
        loads, consts = r.sem("loads"), r.sem("consts")
        n_ready, turned, f_ready = r.sem("n_ready"), r.sem("turned"), r.sem("f_ready")
        qk_done, pF_free, v_done, v_free = r.sem("qk_done"), r.sem("pF_free"), r.sem("v_done"), r.sem("v_free")
        p1_ready, r1_ready, p2_ready, p3_ready = r.sem("p1_ready"), r.sem("r1_ready"), r.sem("p2_ready"), r.sem("p3_ready")
        stored, steps = [r.sem("stored0"), r.sem("stored1")], r.sem("steps")
        with nc.Block() as block:
            @block.sync
            def _(sp):
                for n, name in enumerate(("wq", "wk", "wv")):
                    sp.dma_start(W[:, n], ins[name].rearrange("(k p) n -> p k n", p=P)).then_inc(loads, 16)
                sp.dma_start(bqk[:], ins["bqkcol"]).then_inc(loads, 16)
                sp.dma_start(bv[:], ins["bv"].partition_broadcast(P)).then_inc(loads, 16)

                def step(now, following, before):
                    if before:
                        i, s = before
                        take(sp, p3_ready)
                        for n in range(3):
                            for m in range(2):
                                sp.dma_start(S["qk"][m, n, 2 * s:2 * s + 2, :, bass.ds(i * CH, CH)].rearrange("m p t -> p m t"),
                                             piece[:, s, n, 2 * m:2 * m + 2]).then_inc(stored[s], 16)

                sweep(sp, step)
                for s in range(B):
                    sp.wait_ge(stored[s], 96)

            @block.scalar
            def _(act):
                act.wait_ge(loads, 80)
                act.wait_ge(consts, 2)
                for s in range(B):
                    act.sem_inc(stored[s], 96)

                def split(s, m):
                    scale = 0.25 if m < 2 else 1.0
                    take(act, qk_done)
                    act.activation(full[:, s, m], pF[:, m], ACT.Identity, scale=scale, bias=bqk[:, m // 2, m % 2:m % 2 + 1])
                    act.activation(piece[:, s, 0, m], pF[:, m], ACT.Identity, scale=scale,
                                   bias=bqk[:, m // 2, m % 2:m % 2 + 1]).then_inc(pF_free, 1)

                def step(now, following, before):
                    if following:
                        norm.root(act, following[1])
                    if now:
                        take(act, stored[now[1]], 96)
                        split(now[1], 0)
                        split(now[1], 1)
                    if following:
                        s = following[1]
                        take(act, turned)
                        for h in range(KD):
                            last = act.activation(fT[:, s, h], pT[:, h], ACT.Identity,
                                                  scale=cols[:, 1, 1, h, s:s + 1], bias=cols[:, 1, 0, h, s:s + 1])
                        last.then_inc(f_ready, 1)
                    if now:
                        split(now[1], 2)
                        split(now[1], 3)
                        act.drain().then_inc(p1_ready, 1)

                act.preload_act_table_set("sqrt_and_others")
                sweep(act, step)

            @block.gpsimd
            def _(pool):

                def step(now, following, before):
                    if now:
                        s = now[1]
                        take(pool, r1_ready)
                        pool.tensor_copy(piece[:, s, 1], full[:, s]).then_inc(p2_ready, 1)

                sweep(pool, step)

            @block.tensor
            def _(pe):
                pe.wait_ge(loads, 80)
                pe.sem_inc(pF_free, 4)

                def project(s, m):
                    take(pe, pF_free)
                    for k in range(KD):
                        mm = pe.matmul(pF[:, m], W[:, m // 2, k, m % 2 * P:m % 2 * P + P], fT[:, s, k],
                                       start=(k == 0), stop=(k == KD - 1))
                    mm.then_inc(qk_done, 1)

                def step(now, following, before):
                    if now:
                        s = now[1]
                        take(pe, f_ready)
                        take(pe, v_free)
                        for j in range(CT):
                            for k in range(KD):
                                mm = pe.matmul(pV[:, j], fT[:, s, k, j * P:(j + 1) * P], W[:, 2, k],
                                               start=(k == 0), stop=(k == KD - 1))
                        mm.then_inc(v_done, 1)
                        project(s, 0)
                        project(s, 1)
                    if following:
                        take(pe, n_ready)
                        transposes(pe, pT, n1[:, following[1]], ident[:]).then_inc(turned, 1)
                    if now:
                        project(s, 2)
                        project(s, 3)

                sweep(pe, step)

            @block.vector
            def _(dve):
                dve.wait_ge(loads, 80)
                dve.tensor_scalar(bqk[:, 0], bqk[:, 0], 0.25, None, ALU.mult).then_inc(consts, 1)
                dve.memset(norm.eps[:], EPS).then_inc(consts, 1)
                dve.sem_inc(v_free, 1)
                c = Chain(dve, steps)

                def step(now, following, before):
                    if following:
                        i, s = following
                        norm.stats_at(dve, c, s, x, i * CT + s * TT)
                        norm.apply_at(dve, c, s, n1[:, s], x, i * CT + s * TT).then_inc(n_ready, 1)
                    if now:
                        i, s = now
                        take(dve, v_done)
                        for m in range(KD):
                            last = dve.tensor_tensor(V[:, 2 * s + m, bass.ds(i * CT, CT)], pV[:, :, m * P:(m + 1) * P],
                                                     row4(bv[:, m * P:(m + 1) * P]), ALU.add)
                        last.then_inc(v_free, 1)
                        take(dve, p1_ready)
                        dve.tensor_tensor(full[:, s], full[:, s], piece[:, s, 0], ALU.subtract).then_inc(r1_ready, 1)
                    if before:
                        s = before[1]
                        take(dve, p2_ready)
                        dve.tensor_tensor(piece[:, s, 2], full[:, s], piece[:, s, 1], ALU.subtract).then_inc(p3_ready, 1)

                sweep(dve, step)


def phase_attention(kit, S):
    nc, ins = kit.nc, kit.ins
    ident, identb, V, qk = S["ident"], S["identb"], S["V"], S["qk"]
    with Room(nc, "att") as r:
        Q = r.sb("Q", [P, 2, NC, GH, CH], BF16)
        K = r.sb("K", [P, 2, NC, GH, CH], BF16)
        Vg = r.sb("Vg", [P, 2, TT, GH, 32])
        Pr = r.sb("Pr", [P, 4, 2, CH])
        above = r.sb("above", [P, P], BF16)
        below = r.sb("below", [P, P], BF16)
        mx = r.sb("mx", [P, 2, GH * CT, NC])
        mneg = r.sb("mneg", [P, GH * CT])
        mrest = r.sb("mrest", [P, GH * CT])
        mp = r.sb("mp", [P, 3, GH * CT], BF16)
        mrow = r.sb("mrow", [3 * GH * CT, NC, P], BF16)
        O = r.sb("O", [P, CH])
        rden = r.sb("rden", [P, 2, CT, GH])
        ST = r.ps("ST", [P, 2, 2, CH])
        MX = r.ps("MX", [P, 3, CH])
        OV = r.ps("OV", [P, CH])
        masks, in_q = r.sem("masks"), [[r.sem(f"in{a}{c}") for c in range(NC)] for a in range(2)]
        m_in = [r.sem(f"m_in{c}") for c in range(NC)]
        qk_free, st_done, p_ready = r.sem("qk_free"), r.sem("st_done"), r.sem("p_ready")
        mx_done, mx_free = r.sem("mx_done"), r.sem("mx_free")
        mp_ready, mt_done, mrow_ready = r.sem("mp_ready"), r.sem("mt_done"), r.sem("mrow_ready")
        ov_done, o_ready, tr_done = r.sem("ov_done"), r.sem("o_ready"), r.sem("tr_done")
        vg_ready, vg_free, steps, consts = r.sem("vg_ready"), r.sem("vg_free"), r.sem("steps"), r.sem("consts")
        chunks = list(range(NC))[::-1]

        def load(sp, i, a, c):
            for t, m in ((Q, 0), (K, 1)):
                for n, x in enumerate(PAIRS[m]):
                    src = qk[m, x, bass.ds(i, 1), 64 * a:64 * a + 64, c * CH:(c + 1) * CH]
                    sp.dma_start(t[DA * n:DA * n + DA, a, c],
                                 src.rearrange("a (h d) t -> d (a h) t", d=DA)).then_inc(in_q[a][c], 16)

        def sp_group(sp, mxg, nxt):
            for c in chunks:
                if mxg is not None:
                    take(sp, mrow_ready)
                    for n in range(3):
                        sp.dma_start(Q[KQ + n:KQ + n + 1, mxg[1], c].rearrange("a h (r p) -> a (h r) p", p=P),
                                     mrow[n * GH * CT:(n + 1) * GH * CT, c]
                                     ).then_inc(m_in[c], 16)
                if nxt is not None:
                    take(sp, qk_free)
                    load(sp, nxt[0], nxt[1], c)

        LAST = 2 * sum(CT * (c + 1) for c in range(NC))

        def pe_group(pe, eg, mxg, before=None, first=False):
            def scores_t(c, n, e, hh):
                r0 = (n - CT * c) * P if n >= CT * c else 0
                h = 2 * (e % 2) + hh
                mm = pe.matmul(ST[:, e % 2, hh, r0:], K[0:ROWS, eg[1], n // CT, h, n % CT * P:(n % CT + 1) * P],
                               Q[0:ROWS, eg[1], c, h, r0:], start=True, stop=(n < CT * c))
                if n >= CT * c:
                    mm = pe.matmul(ST[:, e % 2, hh, r0:r0 + P], identb[:], below[:], start=False, stop=True)
                if hh:
                    mm.then_inc(st_done, 1)

            def pv(c, n, e, a):
                if n == 0 and (c < NC - 1 or before is not None):
                    take(pe, o_ready)
                r0 = (n - CT * c) * P if n >= CT * c else 0
                for h in range(GH):
                    mm = pe.matmul(OV[32 * h:32 * h + 32, r0:], Vg[:, a, n, h], Pr[:, (e + h // 2) % 4, h % 2, r0:],
                                   start=(n == 0), stop=(n == CT * c + CT - 1), tile_position=(0, 32 * h),
                                   skip_group_check=True)
                if n == CT * c + CT - 1:
                    mm.then_inc(ov_done, 1)

            def maxima(c, n, h):
                rr, w = n % CT, c - n // CT
                last = n // CT == 0
                cols = (rr + 1) * P if last else CH
                if h == 0 and rr == 0 and c == NC - 1:
                    take(pe, in_q[mxg[1]][w], 16 * 2 * len(PAIRS[0]))
                take(pe, mx_free)
                bank = MX[:, u[0] % 3]
                u[0] += 1
                mm = pe.matmul(bank[:, 0:cols], Q[0:KQ, mxg[1], c, h, rr * P:(rr + 1) * P],
                               K[0:KQ, mxg[1], w, h, 0:cols], start=True, stop=not last)
                if last:
                    mm = pe.matmul(bank[:, cols - P:cols], identb[:], above[:], start=False, stop=True)
                mm.then_inc(mx_done, 1)

            def turn_max():
                take(pe, mp_ready)
                take(pe, mx_free)
                u[0] += 1
                pe.transpose(MX[:, (u[0] - 1) % 3].bitcast(BF16)[0:3 * GH * CT, 0:P],
                             mp[:].rearrange("p a b -> p (a b)"), identb[:]).then_inc(mt_done, 1)

            def turn_out():
                take(pe, mx_free)
                u[0] += 1
                for j in range(CT):
                    mm = pe.transpose(MX[:, (u[0] - 1) % 3, j * P:(j + 1) * P], O[:, j * P:(j + 1) * P], ident[:])
                mm.then_inc(tr_done, 1)

            u = [0]
            late = [] if first else [turn_max]
            lag = []
            if before is not None:
                late.append(turn_out)
                lag = [(0, CT - 1, LAST - 2, before[1])]
            if eg is not None:
                take(pe, vg_ready)
            e = 0
            for c in chunks:
                if eg is not None:
                    take(pe, m_in[c], 48)
                for n in range(CT * (c + 1)):
                    for pair in range(2):
                        if eg is not None and lag:
                            take(pe, p_ready)
                        for hh in range(2):
                            if eg is not None:
                                scores_t(c, n, e, hh)
                            if mxg is not None:
                                maxima(c, n, 2 * pair + hh)
                        e += 1
                    if eg is not None:
                        if lag:
                            pv(*lag.pop(0))
                        lag.append((c, n, e - 2, eg[1]))
                    if n == 2:
                        for f in late:
                            f()
                        late = []
                if c:
                    late = ([turn_max] if mxg is not None else []) + ([turn_out] if eg is not None else [])
            if u[0] % 3 and mxg is not None:
                take(pe, mx_free, -u[0] % 3)
            if mxg is None:
                take(pe, p_ready, 2)
                pv(*lag[0])
                take(pe, o_ready)
                turn_out()

        def act_out(act, c_free):
            take(act, ov_done)
            act.activation(O[:], OV[:], ACT.Copy).then_inc(o_ready, 1)
            if c_free:
                act.drain().then_inc(qk_free, 1)

        def act_group(act, c_free, before, before_free, last=False):
            e = 0
            owed, owed_free = before, before_free
            for c in chunks:
                for n in range(CT * (c + 1)):
                    r0 = (n - CT * c) * P if n >= CT * c else 0
                    for pair in range(2):
                        take(act, st_done)
                        act.activation(Pr[:, e % 4, :, r0:], ST[:, e % 2, :, r0:], ACT.Exp).then_inc(p_ready, 1)
                        e += 1
                    if n == 0 and owed:
                        act_out(act, owed_free)
                owed, owed_free = True, c_free
            if last:
                act_out(act, c_free)

        def dve_group(dve, eg, mxg, before=None, first=False):
            ch = Chain(dve, steps)

            def maxima(c, n, h):
                rr, w = n % CT, c - n // CT
                cols = (rr + 1) * P if n // CT == 0 else CH
                take(dve, mx_done)
                u[0] += 1
                return dve.tensor_reduce(mx[:, c % 2, h * CT + rr, w:w + 1], MX[:, (u[0] - 1) % 3, 0:cols], AX.X, ALU.max)

            def piece_step(c, k):
                take(dve, steps)
                if k == 0:
                    last = dve.tensor_reduce(mneg[:], mx[:, c % 2, :, 0:c + 1], AX.X, ALU.max)
                elif k == 1:
                    last = dve.tensor_scalar(mneg[:], mneg[:], -1.0, None, ALU.mult)
                elif k == 2:
                    last = dve.tensor_copy(mp[:, 0], mneg[:])
                elif k == 3:
                    last = dve.tensor_tensor(mrest[:], mneg[:], mp[:, 0], ALU.subtract)
                elif k == 4:
                    last = dve.tensor_copy(mp[:, 1], mrest[:])
                else:
                    last = dve.tensor_tensor(mp[:, 2], mrest[:], mp[:, 1], ALU.subtract)
                last.then_inc(mp_ready if k == 5 else steps, 1)

            def row(c):
                take(dve, mt_done)
                dve.tensor_copy(mrow[:, c], MX[:, u[0] % 3].bitcast(BF16)[0:3 * GH * CT, 0:P]).then_inc(mrow_ready, 1)
                dve.drain().then_inc(mx_free, 1)
                u[0] += 1

            def out(c, eg):
                take(dve, tr_done)
                turned = MX[:, u[0] % 3].rearrange("p (r h d) -> p r h d", r=CT, h=GH)
                u[0] += 1
                ch.link(dve.reciprocal(rden[:, c % 2], turned[:, :, :, DA]))
                for j in range(CT):
                    last = dve.tensor_tensor(
                        V[:, bass.ds(eg[0], 1), c * CT + j, 64 * eg[1]:64 * eg[1] + 64].rearrange("p a (h d) -> p (a h) d", h=GH),
                        turned[:, j, :, 0:DA],
                        rden[:, c % 2, j].unsqueeze(2).broadcast_to([P, GH, DA]), ALU.mult)
                last.then_inc(mx_free, 1)
                if c == 0:
                    dve.drain().then_inc(vg_free, 1)

            u = [0]
            owed = [] if first else [(0, k) for k in range(6)]
            late = [] if first else [(row, (0,))]
            if mxg is None:
                for t in owed:
                    piece_step(*t)
            if before is not None:
                late.append((out, (0, before)))
            for c in chunks:
                for n in range(CT * (c + 1)):
                    if mxg is not None:
                        for h in range(GH):
                            maxima(c, n, h).then_inc(mx_free, 1)
                            if owed:
                                piece_step(*owed.pop(0))
                    if n == 2:
                        for f, k in late:
                            f(*k)
                        late = []
                if mxg is not None:
                    dve.drain().then_inc(steps, 1)
                    owed = [(c, k) for k in range(6)]
                    late.append((row, (c,)))
                if eg is not None:
                    late.append((out, (c, eg)))
            if u[0] % 3 and mxg is not None:
                dve.sem_inc(mx_free, -u[0] % 3)
            if mxg is None:
                out(0, eg)

        N2 = 2 * B
        with nc.Block() as block:
            @block.sync
            def _(sp):
                for a in range(2):
                    for c in chunks:
                        load(sp, 0, a, c)
                sp_group(sp, (0, 0), None)
                with sp.Fori(0, N2 - 1) as i:
                    sp_group(sp, (i, 1), (i + 1, 0))
                    sp_group(sp, (i + 1, 0), (i + 1, 1))
                sp_group(sp, (N2 - 1, 1), None)

            @block.gpsimd
            def _(pool):
                pool.memset(above[:], 0.0).then_inc(consts, 1)
                pool.memset(below[:], 0.0).then_inc(consts, 1)
                pool.wait_ge(consts, 2)
                pool.affine_select(out=above[:], in_=above[:], compare_op=ALU.is_ge, fill=NEG, base=0,
                                   pattern=[[-1, P]], channel_multiplier=1).then_inc(masks, 1)
                pool.affine_select(out=below[:], in_=below[:], compare_op=ALU.is_ge, fill=NEG, base=0,
                                   pattern=[[1, P]], channel_multiplier=-1).then_inc(masks, 1)
                pool.memset(Vg[:], 1.0).then_inc(consts, 1)
                pool.wait_ge(consts, 3)
                pool.sem_inc(vg_free, 2)
                with pool.Fori(0, N2) as i:
                    for a in range(2):
                        take(pool, vg_free)
                        src = V[:, bass.ds(i, 1), :, 64 * a:64 * a + 64].rearrange("p a j n -> p (a j) n")
                        for h in range(GH):
                            last = pool.tensor_copy(Vg[:, a, :, h, 0:DA], src[:, :, h * DA:(h + 1) * DA])
                        last.then_inc(vg_ready, 1)

            @block.scalar
            def _(act):
                act_group(act, True, False, False)
                with act.Fori(0, N2 - 2) as _i:
                    act_group(act, True, True, True)
                    act_group(act, True, True, True)
                act_group(act, True, True, True)
                act_group(act, False, True, True)
                act_group(act, False, True, False, last=True)

            @block.tensor
            def _(pe):
                pe.wait_ge(masks, 2)
                pe.wait_ge(S["identb_ready"], 1)
                pe_group(pe, None, (0, 0), first=True)
                pe_group(pe, (0, 0), (0, 1))
                with pe.Fori(0, N2 - 1) as i:
                    pe_group(pe, (i, 1), (i + 1, 0), before=(i, 0))
                    pe_group(pe, (i + 1, 0), (i + 1, 1), before=(i, 1))
                pe_group(pe, (N2 - 1, 1), None, before=(N2 - 1, 0))

            @block.vector
            def _(dve):
                dve.memset(K[KQ:ROWS], 1.0)
                dve.tensor_copy(identb[:], ident[:]).then_inc(S["identb_ready"], 1)
                dve.sem_inc(mx_free, 3)
                dve_group(dve, None, (0, 0), first=True)
                dve_group(dve, (0, 0), (0, 1))
                with dve.Fori(0, N2 - 1) as i:
                    dve_group(dve, (i, 1), (i + 1, 0), before=(i, 0))
                    dve_group(dve, (i + 1, 0), (i + 1, 1), before=(i, 1))
                dve_group(dve, (N2 - 1, 1), None, before=(N2 - 1, 0))


XW = D + 2
NQ, NKV = 256, 512
R4 = 2 * B
FETCH = 9.0 / 8.0
ITERS = 50


def phase_route_scores(kit, S):
    nc, ins = kit.nc, kit.ins
    x, rows, ident, A, xn, sc = S["x0"], S["rows"], S["ident"], S["V"], S["xn"], S["s4"]
    with Room(nc, "rts") as r:
        Wo = r.sb("Wo", [P, KD, D])
        bo = r.sb("bo", [P, D])
        tok = r.sb("tok", [P, 2, D])
        a = r.sb("a", [P, B, CT, D])
        aT = r.sb("aT", [P, B, KD, CH])
        h = r.sb("h", [P, B, CT, D])
        junk = r.sb("junk", [P, 2, CT, D])
        junk2 = r.sb("junk2", [P, B, CT, D])
        dots = r.sb("dots", [P, B, 2, CT])
        ss = r.sb("ss", [P, B, CT])
        norm = Norm(r)
        pT = r.ps("pT", [P, KD, CH])
        pA = r.ps("pA", [P, CT, D])
        loads, consts = r.sem("loads"), r.sem("consts")
        a_ready, turned, aT_ready, a_done, a_free = (r.sem("a_ready"), r.sem("turned"), r.sem("aT_ready"),
                                                     r.sem("a_done"), r.sem("a_free"))
        h_ready, ss_ready, steps, a_read = r.sem("h_ready"), r.sem("ss_ready"), r.sem("steps"), r.sem("a_read")
        with nc.Block() as block:
            @block.sync
            def _(sp):
                sp.dma_start(Wo[:], ins["wo"].rearrange("(k p) n -> p k n", p=P)).then_inc(loads, 16)
                sp.dma_start(bo[:], ins["bo"].partition_broadcast(P)).then_inc(loads, 16)
                for n, name in enumerate(("q_tok", "kv_tok")):
                    sp.dma_start(tok[:, n], ins[name].partition_broadcast(P)).then_inc(loads, 16)

            @block.gpsimd
            def _(pool):

                def step(now, following, before):
                    if following:
                        i, s = following
                        take(pool, a_free)
                        for m in range(KD):
                            last = pool.tensor_copy(a[:, s, :, m * P:(m + 1) * P].unsqueeze(1),
                                                    A[:, 2 * s + m:2 * s + m + 1, bass.ds(i * CT, CT)])
                        last.then_inc(a_ready, 1)

                sweep(pool, step)

            @block.scalar
            def _(act):
                act.wait_ge(loads, 64)
                act.wait_ge(consts, 1)
                act.sem_inc(a_free, 2)

                def step(now, following, before):
                    if following:
                        s = following[1]
                        take(act, turned)
                        for k in range(KD):
                            last = act.activation(aT[:, s, k], pT[:, k], ACT.Copy)
                        last.then_inc(aT_ready, 1)
                        act.sem_inc(a_free, 1)
                    if now:
                        s = now[1]
                        take(act, h_ready)
                        for j in range(CT):
                            last = act.activation(junk2[:, s, j], h[:, s, j], ACT.Square, accum_out=ss[:, s, j:j + 1])
                        act.drain()
                        act.activation(ss[:, s], ss[:, s], ACT.Sqrt).then_inc(ss_ready, 1)
                    if following:
                        norm.root(act, following[1])

                act.preload_act_table_set("sqrt_and_others")
                sweep(act, step)

            @block.tensor
            def _(pe):
                pe.wait_ge(loads, 64)

                def step(now, following, before):
                    if following:
                        take(pe, a_ready)
                        transposes(pe, pT, a[:, following[1]], ident[:]).then_inc(turned, 1)
                        take(pe, aT_ready)
                        take(pe, a_read)
                        s = following[1]
                        for j in range(CT):
                            for k in range(KD):
                                mm = pe.matmul(pA[:, j], aT[:, s, k, j * P:(j + 1) * P], Wo[:, k],
                                               start=(k == 0), stop=(k == KD - 1))
                        mm.then_inc(a_done, 1)

                sweep(pe, step)

            @block.vector
            def _(dve):
                dve.wait_ge(loads, 64)
                dve.memset(norm.eps[:], EPS).then_inc(consts, 1)
                c = Chain(dve, steps)

                def step(now, following, before):
                    if now:
                        i, s = now
                        c.link(norm.apply_at(dve, c, s, h[:, s], x, i * CT + s * TT))
                        c.link(dve.tensor_tensor(h[:, s], h[:, s], row4(rows[:, 1, s, (3 + SCALE) * D:(4 + SCALE) * D]), ALU.mult))
                        dve.tensor_tensor(h[:, s], h[:, s], row4(rows[:, 1, s, (3 + SHIFT) * D:(4 + SHIFT) * D]), ALU.add).then_inc(h_ready, 1)
                        dve.drain()
                        for n in range(2):
                            for j in range(CT):
                                last = dve.tensor_tensor_reduce(junk[:, n, j], h[:, s, j], tok[:, n], 1.0, 0.0, ALU.mult,
                                                                ALU.add, dots[:, s, n, j:j + 1])
                        dve.drain()
                        dve.tensor_copy(sc[:].rearrange("p (n s) t -> p s n t", n=2)[:, s, :, bass.ds(i * CT, CT)], dots[:, s])
                    if following:
                        i, s = following
                        take(dve, a_done)
                        dve.tensor_tensor(h[:, s], pA[:], row4(bo[:]), ALU.add).then_inc(a_read, 1)
                        dve.drain()
                        c.link(dve.tensor_tensor(h[:, s], h[:, s], row4(rows[:, 1, s, GATE * D:(GATE + 1) * D]), ALU.mult))
                        xc = x[:, bass.ds(i * CT + s * TT, CT)]
                        c.link(dve.tensor_tensor(xc, xc, h[:, s], ALU.add))
                        norm.stats_at(dve, c, s, x, i * CT + s * TT)
                    if now:
                        i, s = now
                        take(dve, ss_ready)
                        c.link(dve.tensor_scalar(ss[:, s], ss[:, s], 1e-12, None, ALU.max))
                        c.link(dve.reciprocal(ss[:, s], ss[:, s]))
                        for j in range(CT):
                            dve.tensor_scalar(xn[:, bass.ds(i * CT + s * TT + j, 1), 0:D].rearrange("p a d -> p (a d)"),
                                              h[:, s, j], ss[:, s, j:j + 1], float(D) ** 0.5, ALU.mult, ALU.mult)
                        dve.drain()

                dve.sem_inc(a_read, 1)
                sweep(dve, step)


class Descent:

    def __init__(self, r, S):
        self.ident, self.s4, self.xn, self.rank = S["ident"], S["s4"], S["xn"], S["rank"]
        self.s17 = r.sb("s17", [P, R4, TT + 1])
        self.nu = r.sb("nu", [P, R4, TT + 1])
        self.t = r.sb("t17", [P, R4, TT + 1])
        self.e = r.sb("e", [P, R4, TT])
        self.es = r.sb("es", [P, R4])
        self.a = r.sb("a", [P, R4])
        self.lk = r.sb("lk", [P, R4])
        self.ln = r.sb("ln", [P, R4])
        self.m4 = r.sb("m4", [P, R4])
        self.md = r.sb("md", [R4, R4])
        self.m1 = r.sb("m1", [R4, 1])
        self.ones = r.sb("ones", [P, P])
        self.w = r.sb("w", [P, R4, TT])
        self.score = r.sb("score", [P, R4, TT])
        self.R = r.sb("R", [P, 2, T])
        self.junk = r.sb("junk", [P, T], BF16)
        self.tie = r.sb("tie", [P, P], BF16)
        self.lower = r.sb("lower", [P, P])
        self.cnt = r.sb("cnt", [P, R4, TT, 4])
        self.consts, self.mt, self.m_ready, self.mb = r.sem("consts"), r.sem("mt"), r.sem("m_ready"), r.sem("mb")
        self.w_ready, self.e_ready, self.es_ready = r.sem("w_ready"), r.sem("ce_ready"), r.sem("es_ready")
        self.ln_ready, self.score_in, self.score_ready = r.sem("ln_ready"), r.sem("score_in"), r.sem("score_ready")
        self.scores_final, self.r_ready, self.r_free = r.sem("scores_final"), r.sem("r_ready"), r.sem("r_free")

    def pool_start(self, pool):
        pool.memset(self.lower[:], 1.0).then_inc(self.consts, 1)
        pool.wait_ge(self.consts, 1)
        pool.affine_select(out=self.lower[:], in_=self.lower[:], compare_op=ALU.is_ge, fill=0.0, base=-1,
                           pattern=[[-1, P]], channel_multiplier=1).then_inc(self.consts, 1)

    def pe_start(self, pe, bank):
        pe.wait_ge(self.mt, 1)
        pe.transpose(bank[0:R4, 0:P], self.m4[:], self.ident[:]).then_inc(self.m_ready, 1)
        pe.wait_ge(self.mt, 2)
        pe.matmul(bank[:, 0:R4], self.ones[0:R4], self.md[:], start=True, stop=True).then_inc(self.mb, 1)
        pe.wait_ge(self.mt, 3)

    def dve_start(self, dve, c, bank):
        dve.memset(self.ones[:], 1.0)
        dve.memset(self.cnt[:], 0.0)
        for n, k in enumerate(min(n * FETCH, T) for n in (NQ, NKV)):
            dve.memset(self.lk[:, n * B:(n + 1) * B], math.log(k))
        dve.memset(self.nu[:], 0.0)
        dve.tensor_reduce(self.m4[:], self.s4[:], AX.X, ALU.max).then_inc(self.mt, 1)
        dve.wait_ge(self.m_ready, 1)
        c.link(dve.tensor_reduce(self.m1[:], bank[0:R4, 0:P], AX.X, ALU.max))
        dve.tensor_scalar(self.md[:], self.ident[0:R4, 0:R4], self.m1[:], None, ALU.mult).then_inc(self.mt, 1)
        dve.tensor_copy(self.s17[:, :, 0:TT], self.s4[:])
        dve.wait_ge(self.mb, 1)
        c.link(dve.tensor_copy(self.s17[:, :, TT], bank[:, 0:R4]))
        dve.sem_inc(self.mt, 1)
        self.dve_weights(dve)

    def act_exp(self, act):
        take(act, self.w_ready)
        act.activation(self.e[:], self.w[:], ACT.Exp).then_inc(self.e_ready, 1)

    def dve_sum(self, dve):
        take(dve, self.e_ready)
        dve.tensor_reduce(self.es[:], self.e[:], AX.X, ALU.add).then_inc(self.es_ready, 1)

    def pe_sum(self, pe, bank):
        take(pe, self.es_ready)
        return pe.matmul(bank[:, 0:R4], self.ones[:], self.es[:], start=True, stop=True)

    def act_log(self, act, bank):
        act.activation(self.ln[:], bank[:, 0:R4], ACT.Ln).then_inc(self.ln_ready, 1)

    def dve_weights(self, dve):
        dve.tensor_tensor(self.w[:], self.nu[:, :, TT:TT + 1].broadcast_to([P, R4, TT]), self.nu[:, :, 0:TT],
                          ALU.subtract).then_inc(self.w_ready, 1)

    def dve_step(self, dve, c):
        take(dve, self.ln_ready)
        c.link(dve.tensor_tensor(self.ln[:], self.ln[:], self.nu[:, :, TT], ALU.subtract))
        c.link(dve.tensor_tensor(self.a[:], self.lk[:], self.ln[:], ALU.subtract))
        c.link(dve.tensor_tensor(self.t[:], self.s17[:], self.a[:].unsqueeze(2).broadcast_to([P, R4, TT + 1]), ALU.add))
        c.link(dve.scalar_tensor_tensor(self.nu[:], self.t[:], 0.0, self.s17[:], ALU.max, ALU.subtract))
        self.dve_weights(dve)

    def dve_scores(self, dve, c):
        take(dve, self.w_ready)
        c.link(dve.tensor_scalar(self.w[:], self.t[:, :, 0:TT], 0.0, None, ALU.min))
        dve.sem_inc(self.score_in, 1)
        dve.wait_ge(self.score_ready, 1)
        dve.sem_inc(self.scores_final, 1)
        c.link(dve.tensor_scalar(self.e[:], self.score[:], -1.0, 1.0, ALU.mult, ALU.add))
        for n in range(2):
            dve.tensor_tensor(self.xn[:, :, D + n].rearrange("p (s t) -> p s t", s=B),
                              self.score[:, n * B:(n + 1) * B], self.e[:, n * B:(n + 1) * B], ALU.add)
        dve.wait_ge(self.consts, 2)
        dve.sem_inc(self.r_free, 2)

    def act_scores(self, act):
        take(act, self.score_in)
        act.activation(self.score[:], self.w[:], ACT.Exp).then_inc(self.score_ready, 1)

    def pe_row(self, pe, bank, n, q):
        for j in range(CT):
            mm = pe.transpose(bank[:, j * P:(j + 1) * P], self.score[:, n, q * CT + j:q * CT + j + 1].broadcast_to([P, P]),
                              self.ident[:])
        return mm

    def act_row(self, act, bank, n, q):
        if q == 0:
            take(act, self.r_free)
        return act.activation(self.R[:, n % 2, q * CH:(q + 1) * CH], bank, ACT.Copy)

    def dve_rank(self, dve, n, j):
        Rn, sj = self.R[:, n % 2], self.score[:, n, j:j + 1]
        if j == 0:
            take(dve, self.r_ready)
        dve.drain()
        if j:
            dve.tensor_scalar(self.junk[:, 0:j * P], Rn[:, 0:j * P], sj, 0.0, ALU.is_ge, ALU.add,
                              accum_out=self.cnt[:, n, j, 0:1])
        dve.tensor_scalar(self.junk[:, j * P:T], Rn[:, j * P:T], sj, 0.0, ALU.is_gt, ALU.add,
                          accum_out=self.cnt[:, n, j, 1:2])
        dve.scalar_tensor_tensor(self.tie[:], Rn[:, j * P:(j + 1) * P], sj, self.lower[:],
                                 ALU.is_equal, ALU.mult, accum_out=self.cnt[:, n, j, 2:3])
        if j == TT - 1:
            dve.drain().then_inc(self.r_free, 1)

HB, DH = 8, 64
HID = HB * DH
KG = HID // P


def phase_light(kit, S):
    nc, ins = kit.nc, kit.ins
    x, xn, rows, ident = S["x0"], S["xn"], S["rows"], S["ident"]
    with Room(nc, "lgt") as r:
        Wq = r.sb("Wq", [P, KD, HID])
        Wkv = r.sb("Wkv", [P, KD, 2 * HID])
        Wo = r.sb("Wo", [P, KG, D])
        gamma = r.sb("gamma", [P, KD])
        xc = r.sb("xc", [P, CT, D])
        xT = r.sb("xT", [P, KD, CH])
        qk = S["hT"][:].rearrange("p a b t -> p (a b t)")[:, 0:2 * B * KG * CH].rearrange(
            "p (m s g t) -> p m s g t", m=2, s=B, g=KG)
        v = r.sb("v", [P, B, CT, HID])
        mx = r.sb("mx", [P, 2, HB])
        den = r.sb("den", [P, 2, HB])
        Pr = r.sb("Pr", [P, 2, HB, P])
        PT = r.sb("PT", [P, HB, P])
        OT = r.sb("OT", [P, KG, P])
        y = r.sb("y", [P, 2, D])
        t = r.sb("t", [P, D])
        pu = r.ps("pu", [P, 4, 512])
        pS = r.ps("pS", [P, 2, HB, P])
        loads, x_ready, x_free, full, free = r.sem("loads"), r.sem("x_ready"), r.sem("x_free"), r.sem("full"), r.sem("free")
        s_done, s_free, mx_ready, e_ready, p_ready = (r.sem("s_done"), r.sem("s_free"), r.sem("mx_ready"),
                                                      r.sem("e_ready"), r.sem("p_ready"))
        evac, y_ready, steps = {n: r.sem("evac_" + n) for n in ("xT", "qkv", "PT", "OT")}, r.sem("y_ready"), r.sem("steps")
        p_free, y_free = r.sem("p_free"), r.sem("y_free")
        rt = Descent(r, S)
        UP = NC // 2
        PER = 3
        AHEAD = ITERS - UP * B * CT * PER
        proj = [("x", h) for h in range(KD)] + [(n, j) for n in ("q", "k", "v") for j in range(CT)]
        SKIP = -(len(proj) + AHEAD) % 4
        share = [(proj[0:2], proj[2:5]), (proj[5:8], proj[8:10]), (proj[10:13], proj[13:14]), ([], [])]

        def slot(h):
            return h % 2 * (HB // 2) + h // 2

        def pe_unit(pe, u, s, kind, j):
            take(pe, free)
            out = pu[:, u % 4]
            if kind == "x":
                if j == 0:
                    take(pe, x_ready)
                for n in range(CT):
                    mm = pe.transpose(out[:, n * P:(n + 1) * P], xc[:, n, j * P:(j + 1) * P], ident[:])
            else:
                if (kind, j) == ("q", 0):
                    take(pe, evac["xT"], 2)
                for k in range(KD):
                    if kind == "q":
                        w, m = Wq[:, k, j * P:(j + 1) * P], xT[:, k]
                    elif kind == "k":
                        w, m = Wkv[:, k, j * P:(j + 1) * P], xT[:, k]
                    else:
                        w, m = xT[:, k, j * P:(j + 1) * P], Wkv[:, k, HID:2 * HID]
                    mm = pe.matmul(out, w, m, start=(k == 0), stop=(k == KD - 1))
            mm.then_inc(full, 1)

        def act_unit(act, u, s, kind, j):
            take(act, full)
            src = pu[:, u % 4]
            if kind == "x":
                act.activation(xT[:, j], src, ACT.Copy, scale=gamma[:, j:j + 1]).then_inc(evac["xT"], 1)
                act.drain().then_inc(free, 1)
                if j == KD - 1:
                    act.sem_inc(x_free, 1)
            else:
                if kind == "q":
                    act.activation(qk[:, 0, s, j], src, ACT.Copy, scale=DH ** -0.5).then_inc(free, 1)
                elif kind == "k":
                    act.activation(qk[:, 1, s, j], src, ACT.Copy).then_inc(free, 1)
                else:
                    act.activation(v[:, s, j], src, ACT.Copy).then_inc(free, 1)
                if (kind, j) == ("v", CT - 1):
                    act.drain().then_inc(evac["qkv"], 1)

        def pe_scores(pe, s, w):
            if w == 0:
                take(pe, evac["qkv"])
            take(pe, s_free)
            for h in range(HB):
                at = slice(DH * (h % 2), DH * (h % 2) + DH)
                mm = pe.matmul(pS[:, w % 2, slot(h)], qk[at, 0, s, h // 2, w * P:(w + 1) * P],
                               qk[at, 1, s, h // 2, w * P:(w + 1) * P], start=True, stop=True)
            mm.then_inc(s_done, 1)

        def act_exp(act, w):
            take(act, mx_ready)
            take(act, p_free)
            for h in range(HB):
                last = act.activation(Pr[:, w % 2, h], pS[:, w % 2, h], ACT.Exp, bias=mx[:, w % 2, h:h + 1],
                                      accum_out=den[:, w % 2, h:h + 1])
            last.then_inc(e_ready, 1)
            act.drain().then_inc(s_free, 1)

        def dve_max(dve, c, w):
            take(dve, s_done)
            c.link(dve.tensor_reduce(mx[:, w % 2], pS[:, w % 2], AX.X, ALU.max))
            dve.tensor_scalar(mx[:, w % 2], mx[:, w % 2], -1.0, None, ALU.mult).then_inc(mx_ready, 1)

        def pe_sum(pe, u):
            take(pe, free)
            rt.pe_sum(pe, pu[:, u % 4]).then_inc(full, 1)

        def act_log(act, u):
            take(act, full)
            rt.act_log(act, pu[:, u % 4])
            act.drain().then_inc(free, 1)

        def pe_row(pe, u, n, q):
            take(pe, free)
            rt.pe_row(pe, pu[:, u % 4], n, q).then_inc(full, 1)

        def act_row(act, u, n, q):
            take(act, full)
            rt.act_row(act, pu[:, u % 4], n, q)
            act.drain().then_inc(free, 1)
            if q == CT - 1:
                act.sem_inc(rt.r_ready, 1)

        def pe_chunk(pe, s, more, nxt, descend, row=None):
            u = 0
            for w in range(CT):
                for half in range(2):
                    take(pe, free)
                    if half == 0:
                        take(pe, p_ready)
                    for h in range(4):
                        mm = pe.transpose(pu[:, u % 4, h * P:(h + 1) * P], Pr[:, w % 2, 4 * half + h], ident[:])
                    mm.then_inc(full, 1)
                    u += 1
                if w < CT - 1:
                    pe_scores(pe, s, w + 1)
                elif nxt:
                    pe_scores(pe, 1 - s, 0)
                if descend:
                    pe_sum(pe, u)
                    u += 1
                take(pe, free)
                take(pe, evac["PT"])
                for h in range(HB):
                    at = DH * (h % 2)
                    mm = pe.matmul(pu[at:at + DH, u % 4, h // 2 * P:(h // 2 + 1) * P], v[:, s, w, h * DH:(h + 1) * DH],
                                   PT[:, slot(h)], start=True, stop=True, tile_position=(0, at), skip_group_check=True)
                mm.then_inc(full, 1)
                u += 1
                if more:
                    for kind, j in share[w][0]:
                        pe_unit(pe, u, 1 - s, kind, j)
                        u += 1
                if descend:
                    pe_sum(pe, u)
                    u += 1
                take(pe, free)
                take(pe, evac["OT"])
                for k in range(KG):
                    mm = pe.matmul(pu[:, u % 4, 0:D], OT[:, k], Wo[:, k], start=(k == 0), stop=(k == KG - 1))
                mm.then_inc(full, 1)
                u += 1
                if more:
                    for kind, j in share[w][1]:
                        pe_unit(pe, u, 1 - s, kind, j)
                        u += 1
                if descend:
                    pe_sum(pe, u)
                    u += 1
                if row is not None:
                    pe_row(pe, u, row, w)
                    u += 1
            skip = -u % 4
            for _ in range(skip):
                take(pe, free)

        def act_chunk(act, s, more, nxt, descend, row=None):
            u = 0
            for w in range(CT):
                if descend:
                    rt.act_exp(act)
                for half in range(2):
                    take(act, full)
                    last = act.activation(PT[:, 4 * half:4 * half + 4].rearrange("p a b -> p (a b)"), pu[:, u % 4], ACT.Copy)
                    if half == 0:
                        last.then_inc(free, 1)
                    u += 1
                last.then_inc(evac["PT"], 1)
                act.drain().then_inc(free, 1)
                act.sem_inc(p_free, 1)
                if descend:
                    act_log(act, u)
                    u += 1
                take(act, full)
                act.activation(OT[:].rearrange("p a b -> p (a b)"), pu[:, u % 4], ACT.Copy).then_inc(evac["OT"], 1)
                act.drain().then_inc(free, 1)
                u += 1
                if descend:
                    rt.act_exp(act)
                if w < CT - 1 or nxt:
                    act_exp(act, (w + 1) % CT)
                if more:
                    for kind, j in share[w][0]:
                        act_unit(act, u, 1 - s, kind, j)
                        u += 1
                if descend:
                    act_log(act, u)
                    u += 1
                take(act, full)
                take(act, y_free)
                act.activation(y[:, w % 2], pu[:, u % 4, 0:D], ACT.Copy).then_inc(y_ready, 1)
                act.drain().then_inc(free, 1)
                u += 1
                if descend:
                    rt.act_exp(act)
                if more:
                    for kind, j in share[w][1]:
                        act_unit(act, u, 1 - s, kind, j)
                        u += 1
                if descend:
                    act_log(act, u)
                    u += 1
                if row is not None:
                    act_row(act, u, row, w)
                    u += 1
            skip = -u % 4
            if skip:
                act.sem_inc(free, skip)

        def dve_chunk(dve, c, s, i, nxt, descend, ranks=None):
            for w in range(CT):
                if descend:
                    rt.dve_sum(dve)
                if w < CT - 1 or nxt:
                    dve_max(dve, c, (w + 1) % CT)
                if descend:
                    rt.dve_step(dve, c)
                    rt.dve_sum(dve)
                if ranks is not None:
                    for j in range(2):
                        rt.dve_rank(dve, ranks, w * CT + j)
                if w < CT - 1 or nxt:
                    dve_normalise(dve, c, (w + 1) % CT)
                if descend:
                    rt.dve_step(dve, c)
                    rt.dve_sum(dve)
                if ranks is not None:
                    for j in range(2, CT):
                        rt.dve_rank(dve, ranks, w * CT + j)
                take(dve, y_ready)
                c.link(dve.tensor_tensor(t[:], y[:, w % 2], rows[:, 1, s, (3 + GATE) * D:(4 + GATE) * D], ALU.mult))
                xw = flat(x[:, bass.ds(i * CT + (s * TT + w), 1)])
                c.link(dve.tensor_tensor(xw, xw, t[:], ALU.add))
                dve.sem_inc(y_free, 1)
                if descend:
                    rt.dve_step(dve, c)

        def dve_normalise(dve, c, w):
            take(dve, e_ready)
            c.link(dve.reciprocal(den[:, w % 2], den[:, w % 2]))
            dve.tensor_tensor(Pr[:, w % 2], Pr[:, w % 2], den[:, w % 2].unsqueeze(2).broadcast_to([P, HB, P]),
                              ALU.mult).then_inc(p_ready, 1)

        def pool_chunk(pool, i, s):
            take(pool, x_free)
            pool.tensor_copy(xc[:], xn[:, bass.ds(i * CT + s * TT, CT), 0:D]).then_inc(x_ready, 1)

        with nc.Block() as block:
            @block.sync
            def _(sp):
                for w, name in ((Wq, "wq_light"), (Wkv, "wkv_light"), (Wo, "wo_light")):
                    sp.dma_start(w[:], ins[name].rearrange("(k p) n -> p k n", p=P)).then_inc(loads, 16)
                sp.dma_start(gamma[:], ins["glcol"]).then_inc(loads, 16)

            @block.gpsimd
            def _(pool):
                rt.pool_start(pool)
                pool_chunk(pool, 0, 0)
                with pool.Fori(0, NC - 1) as i:
                    pool_chunk(pool, i, 1)
                    pool_chunk(pool, i + 1, 0)
                pool_chunk(pool, NC - 1, 1)

            @block.tensor
            def _(pe):
                pe.wait_ge(loads, 64)
                pe.sem_inc(s_free, 2)
                pe.sem_inc(free, 4)
                rt.pe_start(pe, pS[:, 1, 0])
                for u, (kind, j) in enumerate(proj):
                    pe_unit(pe, u, 0, kind, j)
                pe_scores(pe, 0, 0)
                for u in range(len(proj), len(proj) + AHEAD):
                    pe_sum(pe, u)
                if SKIP:
                    take(pe, free, SKIP)
                with pe.Fori(0, UP) as _i:
                    pe_chunk(pe, 0, True, True, True)
                    pe_chunk(pe, 1, True, True, True)
                pe.wait_ge(rt.scores_final, 1)
                for q in range(CT):
                    pe_row(pe, q, 0, q)
                for n in range(R4):
                    pe_chunk(pe, n % 2, n < R4 - 1, n < R4 - 1, False, n + 1 if n < R4 - 1 else None)

            @block.scalar
            def _(act):
                act.wait_ge(loads, 64)
                act.preload_act_table_set("natural_log_exp_and_others")
                act.sem_inc(x_free, 1)
                act.sem_inc(p_free, 2)
                for u, (kind, j) in enumerate(proj):
                    act_unit(act, u, 0, kind, j)
                act_exp(act, 0)
                for u in range(len(proj), len(proj) + AHEAD):
                    rt.act_exp(act)
                    act_log(act, u)
                if SKIP:
                    act.sem_inc(free, SKIP)
                with act.Fori(0, UP) as _i:
                    act_chunk(act, 0, True, True, True)
                    act_chunk(act, 1, True, True, True)
                rt.act_scores(act)
                for q in range(CT):
                    act_row(act, q, 0, q)
                for n in range(R4):
                    act_chunk(act, n % 2, n < R4 - 1, n < R4 - 1, False, n + 1 if n < R4 - 1 else None)

            @block.vector
            def _(dve):
                c = Chain(dve, steps)
                dve.sem_inc(y_free, 2)
                rt.dve_start(dve, c, pS[:, 1, 0])
                dve_max(dve, c, 0)
                dve_normalise(dve, c, 0)
                for _ in range(AHEAD):
                    rt.dve_sum(dve)
                    rt.dve_step(dve, c)
                with dve.Fori(0, UP) as i:
                    dve_chunk(dve, c, 0, i, True, True)
                    dve_chunk(dve, c, 1, i, True, True)
                rt.dve_scores(dve, c)
                for n in range(R4):
                    dve_chunk(dve, c, n % 2, UP + n // 2, n < R4 - 1, False, n)
                dve.tensor_reduce(S["rank"][:], rt.cnt[:], AX.X, ALU.add)


def phase_heavy(kit, S, out_d):
    nc, ins = kit.nc, kit.ins
    x, xn, rows, ident, rank = S["x0"], S["xn"], S["rows"], S["ident"], S["rank"]
    TQ, TK = NQ // P, NKV // P
    NG = TQ + TK
    with Room(nc, "hvy") as r:
        Wq = r.sb("Wq", [P, KD, HID])
        Wkv = r.sb("Wkv", [P, KD, 2 * HID])
        Wo = r.sb("Wo", [P, KG, D])
        gamma = r.sb("gamma", [P, KD])
        iota = r.sb("iota", [P, NKV])
        zero = r.sb("zero", [1, XW])
        rc = r.sb("rc", [P, 2, CT])
        gb = r.sb("gb", [P, D])
        G = r.sb("G", [P, 2, NQ + NKV])
        X = r.sb("X", [P, NG, XW])
        xT = r.sb("xT", [P, KD, NQ + NKV])
        flat_h = S["hT"][:].rearrange("p a b t -> p (a b t)")
        qT = flat_h[:, 0:KG * NQ].rearrange("p (g t) -> p g t", g=KG)
        kT = flat_h[:, KG * NQ:KG * (NQ + NKV)].rearrange("p (g t) -> p g t", g=KG)
        v = flat_h[:, KG * (NQ + NKV):KG * (NQ + NKV) + TK * HID].rearrange("p (j n) -> p j n", j=TK)
        mx = r.sb("mx", [P, 4])
        den = r.sb("den", [P, 4])
        Pr = r.sb("Pr", [P, 4, NKV])
        PT = r.sb("PT", [P, 2, TK, NQ])
        OT = r.sb("OT", [P, KG, NQ])
        Y = r.sb("Y", [P, TQ, D])
        Gs = r.sb("Gs", [P, 2, CT, NQ])
        GT = r.sb("GT", [P, 2, TQ, CH])
        o = r.sb("o", [P, 2, CT, D])
        pu = r.ps("pu", [P, 8, 512])
        loads, consts, g_ready, g_free = r.sem("loads"), r.sem("consts"), r.sem("g_ready"), r.sem("g_free")
        gathered, x_ready, full, free = r.sem("gathered"), r.sem("x_ready"), r.sem("full"), r.sem("free")
        xT_ready, qkv_ready, s_done, s_free = r.sem("xT_ready"), r.sem("qkv_ready"), r.sem("s_done"), r.sem("s_free")
        mx_ready, e_ready, p_ready, p_free = r.sem("mx_ready"), r.sem("e_ready"), r.sem("p_ready"), r.sem("p_free")
        PT_ready, OT_ready, y_ready, all_free = r.sem("PT_ready"), r.sem("OT_ready"), r.sem("y_ready"), r.sem("all_free")
        gs_ready, gs_free, turned, GT_ready = r.sem("gs_ready"), r.sem("gs_free"), r.sem("turned"), r.sem("GT_ready")
        back, out_ready, stored, steps = r.sem("back"), r.sem("out_ready"), r.sem("stored"), r.sem("steps")
        added, o_full, o_free = r.sem("added"), r.sem("o_full"), r.sem("o_free")
        ranks = rank[:].rearrange("p (n s) t -> p n (s t)", s=B)
        LOOK = 3
        E = HB * TQ
        NU, NS = 3, 4

        def pe_scores(pe, e):
            h, qt = e // TQ, e % TQ
            at = slice(DH * (h % 2), DH * (h % 2) + DH)
            take(pe, s_free)
            pe.matmul(pu[:, NU + e % NS], qT[at, h // 2, qt * P:(qt + 1) * P], kT[at, h // 2],
                      start=True, stop=True).then_inc(s_done, 1)

        with nc.Block() as block:
            @block.sync
            def _(sp):
                for w, name in ((Wq, "wq_heavy"), (Wkv, "wkv_heavy"), (Wo, "wo_heavy")):
                    sp.dma_start(w[:], ins[name].rearrange("(k p) n -> p k n", p=P)).then_inc(loads, 16)
                sp.dma_start(gamma[:], ins["ghcol"]).then_inc(loads, 16)
                sp.dma_start(iota[:], ins["iota"].partition_broadcast(P)).then_inc(loads, 16)
                o_v = out_d.rearrange("(c j p) d -> c p j d", j=CT, p=P)
                with sp.Fori(0, B) as b:
                    with sp.Fori(0, NC) as c:
                        take(sp, out_ready)
                        sp.dma_start(o_v[bass.ds(b * NC + c, 1)].rearrange("a p j d -> p (a j) d"),
                                     x[:, bass.ds(b * TT + c * CT, CT)]).then_inc(stored, 16)
                        take(sp, stored, 16)

            @block.tensor
            def _(pe):
                pe.wait_ge(loads, 80)
                pe.wait_ge(consts, 1)
                pe.sem_inc(free, NU)
                pe.sem_inc(s_free, NS)
                pe.sem_inc(o_free, 1)
                with pe.Fori(0, B) as b:
                    for j in range(NG):
                        pe.matmul(pu[:, j, 0:XW], zero[:, 0:P], zero[:], start=True, stop=False)
                    with pe.Fori(0, NC) as c:
                        for t in range(CT):
                            take(pe, g_ready)
                            for j in range(NG):
                                mm = pe.matmul(pu[:, j, 0:XW], G[:, t % 2, j * P:(j + 1) * P],
                                               xn[:, bass.ds(b * TT + (c * CT + t), 1)].rearrange("p a d -> p (a d)"),
                                               start=False, stop=False)
                            mm.then_inc(g_free, 1)
                    for j in range(NG):
                        mm = pe.matmul(pu[:, j, 0:XW], zero[:, 0:P], zero[:], start=False, stop=True)
                    mm.then_inc(gathered, 1)
                    take(pe, x_ready)
                    u = 0
                    for h in range(KD):
                        for first, n in ((TQ, TK), (0, TQ)):
                            take(pe, free)
                            for j in range(n):
                                mm = pe.transpose(pu[:, u % NU, j * P:(j + 1) * P], X[:, first + j, h * P:(h + 1) * P], ident[:])
                            mm.then_inc(full, 1)
                            u += 1
                    take(pe, xT_ready)
                    for kind, j in [(n, j) for n in ("q", "k", "v") for j in range(CT)]:
                        take(pe, free)
                        for k in range(KD):
                            if kind == "q":
                                mm = pe.matmul(pu[:, u % NU, 0:NQ], Wq[:, k, j * P:(j + 1) * P], xT[:, k, 0:NQ],
                                               start=(k == 0), stop=(k == KD - 1))
                            elif kind == "k":
                                mm = pe.matmul(pu[:, u % NU], Wkv[:, k, j * P:(j + 1) * P], xT[:, k, NQ:],
                                               start=(k == 0), stop=(k == KD - 1))
                            else:
                                mm = pe.matmul(pu[:, u % NU], xT[:, k, NQ + j * P:NQ + (j + 1) * P], Wkv[:, k, HID:],
                                               start=(k == 0), stop=(k == KD - 1))
                        mm.then_inc(full, 1)
                        u += 1
                    take(pe, qkv_ready)
                    for e in range(LOOK):
                        pe_scores(pe, e)
                    for e in range(E):
                        h, qt = e // TQ, e % TQ
                        take(pe, p_ready)
                        take(pe, free)
                        for j in range(TK):
                            mm = pe.transpose(pu[:, u % NU, j * P:(j + 1) * P], Pr[:, e % 4, j * P:(j + 1) * P], ident[:])
                        mm.then_inc(full, 1)
                        u += 1
                        if e + LOOK < E:
                            pe_scores(pe, e + LOOK)
                        if qt == TQ - 1:
                            if h % 2 == 0:
                                take(pe, o_free)
                            take(pe, PT_ready)
                            at = DH * (h % 2)
                            for j in range(TK):
                                mm = pe.matmul(pu[at:at + DH, 7, 0:NQ], v[:, j, h * DH:(h + 1) * DH], PT[:, h % 2, j],
                                               start=(j == 0), stop=(j == TK - 1), tile_position=(0, at), skip_group_check=True)
                            if h % 2:
                                mm.then_inc(o_full, 1)
                    take(pe, OT_ready)
                    take(pe, free)
                    for j in range(TQ):
                        for k in range(KG):
                            mm = pe.matmul(pu[:, u % NU, j * D:(j + 1) * D], OT[:, k, j * P:(j + 1) * P], Wo[:, k],
                                           start=(k == 0), stop=(k == KG - 1))
                    mm.then_inc(full, 1)
                    take(pe, y_ready)
                    take(pe, free, NU)
                    pe.sem_inc(free, NU)

                    def turn(c):
                        take(pe, gs_ready)
                        for k in range(TQ):
                            for t in range(CT):
                                mm = pe.transpose(pu[:, k, t * P:(t + 1) * P], Gs[:, c % 2, t, k * P:(k + 1) * P], ident[:])
                        mm.then_inc(turned, 1)

                    turn(0)
                    for c in range(NC):
                        take(pe, GT_ready)
                        if c < NC - 1:
                            turn(c + 1)
                        if c >= 2:
                            take(pe, added)
                        for t in range(CT):
                            for k in range(TQ):
                                mm = pe.matmul(pu[:, 4 + 2 * (c % 2) + t // 2, t % 2 * D:(t % 2 + 1) * D],
                                               GT[:, c % 2, k, t * P:(t + 1) * P], Y[:, k],
                                               start=(k == 0), stop=(k == TQ - 1))
                        mm.then_inc(back, 1)
                    take(pe, added, 2)

            @block.scalar
            def _(act):
                act.wait_ge(loads, 80)
                with act.Fori(0, B) as b:
                    take(act, gathered)
                    act.activation(X[:], pu[:, 0:NG, 0:XW], ACT.Copy).then_inc(x_ready, 1)
                    u = 0
                    for h in range(KD):
                        for lo, hi in ((NQ, NQ + NKV), (0, NQ)):
                            take(act, full)
                            act.activation(xT[:, h, lo:hi], pu[:, u % NU, 0:hi - lo], ACT.Copy,
                                           scale=gamma[:, h:h + 1]).then_inc(free, 1)
                            u += 1
                    act.drain().then_inc(xT_ready, 1)
                    for kind, j in [(n, j) for n in ("q", "k", "v") for j in range(CT)]:
                        take(act, full)
                        if kind == "q":
                            last = act.activation(qT[:, j], pu[:, u % NU, 0:NQ], ACT.Copy, scale=DH ** -0.5)
                        elif kind == "k":
                            last = act.activation(kT[:, j], pu[:, u % NU], ACT.Copy)
                        else:
                            last = act.activation(v[:, j], pu[:, u % NU], ACT.Copy, scale=X[:, TQ + j, D + 1:D + 2])
                        last.then_inc(free, 1)
                        u += 1
                    act.drain().then_inc(qkv_ready, 1)

                    def exp(e):
                        take(act, mx_ready)
                        take(act, p_free)
                        act.activation(Pr[:, e % 4], pu[:, NU + e % NS], ACT.Exp, bias=mx[:, e % 4:e % 4 + 1],
                                       accum_out=den[:, e % 4:e % 4 + 1]).then_inc(e_ready, 1)
                        act.drain().then_inc(s_free, 1)

                    for e in range(LOOK - 1):
                        exp(e)
                    for e in range(E):
                        h, qt = e // TQ, e % TQ
                        if e + LOOK - 1 < E:
                            exp(e + LOOK - 1)
                        take(act, full)
                        act.activation(PT[:, h % 2, :, qt * P:(qt + 1) * P],
                                       pu[:, u % NU].rearrange("p (j n) -> p j n", j=TK), ACT.Copy).then_inc(free, 1)
                        u += 1
                        act.drain().then_inc(p_free, 1)
                        if qt == TQ - 1:
                            act.sem_inc(PT_ready, 1)
                        if qt == TQ - 1 and h % 2:
                            take(act, o_full)
                            act.activation(OT[:, h // 2], pu[:, 7, 0:NQ], ACT.Copy).then_inc(o_free, 1)
                    act.drain().then_inc(OT_ready, 1)
                    take(act, full)
                    for j in range(TQ):
                        last = act.activation(Y[:, j], pu[:, u % NU, j * D:(j + 1) * D], ACT.Copy, scale=X[:, j, D:D + 1])
                    act.drain().then_inc(y_ready, 1)
                    act.sem_inc(free, 1)
                    for c in range(NC):
                        take(act, turned)
                        act.activation(GT[:, c % 2], pu[:, 0:TQ], ACT.Copy).then_inc(GT_ready, 1)

            @block.vector
            def _(dve):
                dve.memset(zero[:], 0.0).then_inc(consts, 1)
                dve.wait_ge(loads, 80)
                dve.sem_inc(g_free, 2)
                dve.sem_inc(p_free, 4)
                ch = Chain(dve, steps)
                gates = rows[:, 1, :, (3 + GATE) * D:(4 + GATE) * D]
                with dve.Fori(0, B) as b:
                    dve.tensor_copy(gb[:].unsqueeze(1), gates[:, bass.ds(b, 1)])
                    with dve.Fori(0, NC) as c:
                        ch.link(dve.tensor_copy(rc[:], ranks[:, :, bass.ds(b * TT + c * CT, CT)]))
                        for t in range(CT):
                            take(dve, g_free)
                            dve.tensor_scalar(G[:, t % 2, 0:NQ], iota[:, 0:NQ], rc[:, 0, t:t + 1], None, ALU.is_equal)
                            dve.tensor_scalar(G[:, t % 2, NQ:], iota[:], rc[:, 1, t:t + 1], None, ALU.is_equal)
                            dve.drain().then_inc(g_ready, 1)

                    def max_of(e):
                        take(dve, s_done)
                        ch.link(dve.tensor_reduce(mx[:, e % 4:e % 4 + 1], pu[:, NU + e % NS], AX.X, ALU.max))
                        dve.tensor_scalar(mx[:, e % 4:e % 4 + 1], mx[:, e % 4:e % 4 + 1], -1.0, None,
                                          ALU.mult).then_inc(mx_ready, 1)

                    def normalise(e):
                        take(dve, e_ready)
                        d = den[:, e % 4:e % 4 + 1]
                        ch.link(dve.reciprocal(d, d))
                        dve.tensor_scalar(Pr[:, e % 4], Pr[:, e % 4], d, None, ALU.mult).then_inc(p_ready, 1)

                    for e in range(LOOK):
                        max_of(e)
                    normalise(0)
                    for e in range(E):
                        if e + 1 < E:
                            normalise(e + 1)
                        if e + LOOK < E:
                            max_of(e + LOOK)
                    dve.drain()

                    def one_hot(c):
                        ch.link(dve.tensor_copy(rc[:], ranks[:, :, bass.ds(b * TT + c * CT, CT)]))
                        for t in range(CT):
                            dve.tensor_scalar(Gs[:, c % 2, t], iota[:, 0:NQ], rc[:, 0, t:t + 1], None, ALU.is_equal)
                        dve.drain().then_inc(gs_ready, 1)

                    one_hot(0)
                    one_hot(1)
                    for c in range(NC):
                        take(dve, back)
                        if c + 2 < NC:
                            one_hot(c + 2)
                        ch.link(dve.tensor_tensor(o[:, c % 2], pu[:, 4 + 2 * (c % 2):6 + 2 * (c % 2)].rearrange("p a (j d) -> p (a j) d", d=D),
                                                  row4(gb[:]), ALU.mult))
                        dve.sem_inc(added, 1)
                        xc = x[:, bass.ds(b * TT + c * CT, CT)]
                        ch.link(dve.tensor_tensor(xc, xc, o[:, c % 2], ALU.add))
                        dve.sem_inc(out_ready, 1)


def two_layers(nc, ins, out_d):
    with ExitStack() as ctx:
        kit = Kit(nc, ins, ctx)

        def sb(name, shape, dt=F32):
            return ctx.enter_context(nc.sbuf_tensor(name, shape, dt))

        S = {
            "rows": sb("rows", [P, 2, B, 6 * D]),
            "cols": sb("cols", [P, 2, 2, KD, B]),
            "x0": sb("x", [P, NT, D]),
            "hT": sb("hT", [P, KD, B, T + 1]),
            "ident": sb("ident", [P, P]),
            "identb": sb("identb", [P, P], BF16),
            "lncol": sb("lncol", [P, 2, KD]),
            "identb_ready": ctx.enter_context(nc.semaphore("identb_ready")),
            "qk": nc.dram_tensor("qk_pieces", [2, 3, 2 * B, P, T], BF16, kind="Internal").ap(),
        }
        S["V"] = S["hT"][:].rearrange("p a b t -> p (a b t)")[:, 0:NT * D].rearrange("p (i t n) -> p i t n", i=4, t=TT)
        phase_modulation(kit, S)
        phase_norms(kit, S)
        phase_wkv(kit, S)
        phase_channel_mix(kit, S)
        phase_ffn(kit, S)
        phase_qkv(kit, S)
        phase_attention(kit, S)
        S["xn"] = sb("xn", [P, NT, XW])
        S["s4"] = sb("s4", [P, R4, TT])
        S["rank"] = sb("rank", [P, R4, TT])
        phase_route_scores(kit, S)
        phase_light(kit, S)
        phase_heavy(kit, S, out_d)


def _laid_out(I):
    def rows(a):
        return np.ascontiguousarray(a)

    def col(v):
        return np.asarray(v).reshape(KD, P).T

    def cols(*vs):
        return np.ascontiguousarray(np.stack([col(v) for v in vs], 1))

    a = {"x": rows(I["L0_attn_x"].reshape(B * T, D))}
    for l in (0, 1):
        a[f"cT{l}"] = rows(I[f"L{l}_c"].T)
        a[f"L{l}_wmod"] = rows(I[f"L{l}_wmod"])
    for n in ("ln0_w", "ln0_b"):
        a[n] = rows(I["L0_attn_" + n])
    for n in ("Wk", "Wv", "Wr", "Wo", "Wfk", "Wfv", "Wfr"):
        a[n + "T"] = rows(I["L0_attn_" + n].T)
    a["lncol"] = cols(I["L0_attn_ln1_w"], I["L0_attn_ln1_b"])
    a["ln2col"] = cols(I["L0_attn_ln2_w"], I["L0_attn_ln2_b"])
    a["tmcol"] = cols(I["L0_attn_tmk"], I["L0_attn_tmv"], I["L0_attn_tmr"])
    a["uwcol"] = cols(I["L0_attn_time_first"], I["L0_attn_time_decay"])
    a["cmcol"] = cols(I["L0_attn_cmk"], I["L0_attn_cmr"])
    for n in ("w1", "w2", "b2"):
        a[n] = rows(I["L0_ffn_" + n])
    a["b1col"] = rows(I["L0_ffn_b1"].reshape(KH, P).T)
    for n in ("wq", "wk", "wv", "wo", "bv", "bo"):
        a[n] = rows(I["L1_attn_" + n])
    a["bqkcol"] = cols(I["L1_attn_bq"], I["L1_attn_bk"])
    a["q_tok"] = rows(I["L1_ffn_q_routing_token"])
    a["kv_tok"] = rows(I["L1_ffn_kv_routing_token"])
    for n in ("wq_light", "wkv_light", "wo_light", "wq_heavy", "wo_heavy"):
        a[n] = rows(I["L1_ffn_" + n])
    a["wkv_heavy"] = rows(I["L1_ffn_wkv_heavy"].reshape(HB, 2, DH, D).transpose(3, 1, 0, 2).reshape(D, 2 * HID))
    a["glcol"] = rows(col(I["L1_ffn_gamma_light"]))
    a["ghcol"] = rows(col(I["L1_ffn_gamma_heavy"]))
    a["ident"] = np.eye(P, dtype=np.float32)
    a["iota"] = np.arange(NKV, dtype=np.float32)
    return a


def kernel(**inputs):
    import concourse.bacc as _bacc
    from concourse.bass_utils import run_bass_kernel_spmd as _run

    nc = _bacc.Bacc("TRN2", target_bir_lowering=False, num_devices=1)
    arrays = _laid_out(inputs)
    ins = {n: nc.dram_tensor(f"in_{n}", a.shape, mybir.dt.from_np(a.dtype), kind="ExternalInput").ap()
           for n, a in arrays.items()}
    out = nc.dram_tensor("out", (B * T, D), F32, kind="ExternalOutput").ap()
    two_layers(nc, ins, out)
    r = _run(nc, [{f"in_{n}": a for n, a in arrays.items()}], core_ids=[0])
    return r.results[0]["out"].reshape(B, T, D)
```

```python
import math
from contextlib import ExitStack

import numpy as np
import concourse.bass as bass
from concourse import mybir

F32 = mybir.dt.float32
BF16 = mybir.dt.bfloat16
I32 = mybir.dt.int32
ALU = mybir.AluOpType
ACT = mybir.ActivationFunctionType
AX = mybir.AxisListType

P = 128
B = 2
T = 2048
D = 256
KD = D // P
NT = B * T // P
TT = T // P
CH = 512
CT = CH // P
NC = T // CH
H = 1024
KH = H // P
EPS = 1e-5
SHIFT, SCALE, GATE = 0, 1, 2
NEG = -1.0e30


class Kit:

    def __init__(self, nc, ins, ctx):
        self.nc, self.ins, self.ctx = nc, ins, ctx



class Room:

    def __init__(self, nc, name):
        self.nc, self.name, self.stack, self.sems = nc, name, ExitStack(), []

    def __enter__(self):
        self.stack.__enter__()
        return self

    def __exit__(self, *a):
        if self.sems and a[0] is None:
            self.nc.clear_and_free_semaphores(self.sems)
            self.nc.all_engine_barrier()
        return self.stack.__exit__(*a)

    def sb(self, name, shape, dt=F32):
        return self.stack.enter_context(self.nc.sbuf_tensor(f"{self.name}_{name}", shape, dt))

    def ps(self, name, shape, dt=F32):
        return self.stack.enter_context(self.nc.psum_tensor(f"{self.name}_{name}", shape, dt))

    def sem(self, name):
        self.sems.append(self.nc.alloc_semaphore(name=f"{self.name}_{name}"))
        return self.sems[-1]


class Early(Room):

    def __init__(self, nc, name, sources):
        Room.__init__(self, nc, name)
        self.sources = sources

    def __enter__(self):
        Room.__enter__(self)
        self.at = {n: self.sb(n, shape) for n, (shape, _) in self.sources.items()}
        self.loaded = self.sem("loaded")
        return self

    def issue(self, sp):
        for n, (_, source) in self.sources.items():
            sp.dma_start(self.at[n][:], source).then_inc(self.loaded, 16)

    def wait(self, eng):
        eng.wait_ge(self.loaded, 16 * len(self.sources))


def blocks(w):
    return w.rearrange("(k p) n -> p k n", p=P)


class Chain:

    def __init__(self, eng, sem):
        self.eng, self.sem = eng, sem

    def link(self, ins):
        ins.then_inc(self.sem, 1)
        self.eng.wait_ge(self.sem, 1)
        self.eng.sem_inc(self.sem, -1)


def sweep(eng, step):
    step(None, (0, 0), None)
    step((0, 0), (0, 1), None)
    with eng.Fori(0, NC - 1) as i:
        step((i, 1), (i + 1, 0), (i, 0))
        step((i + 1, 0), (i + 1, 1), (i, 1))
    step((NC - 1, 1), None, (NC - 1, 0))
    step(None, None, (NC - 1, 1))


def flat(ap):
    return ap.rearrange("p a b -> p (a b)")


def row4(row, n=CT):
    return row.unsqueeze(1).broadcast_to([row.shape[0], n, row.shape[1]])


class Norm:

    def __init__(self, r, name=""):
        self.st = r.sb(name + "st", [P, B, CT, 6])
        self.mv = r.sb(name + "mv", [P, B, CT, 2])
        self.rs = r.sb(name + "rs", [P, B, CT])
        self.eps = r.sb(name + "eps", [P, 1])
        self.mean_ready, self.root_ready = r.sem(name + "mean_ready"), r.sem(name + "root_ready")

    def stats(self, dve, chain, s, src, src_ready=None):
        for j in range(CT):
            last = dve.bn_stats(self.st[:, s, j], src[:, j])
            if j == 0 and src_ready is not None:
                last.then_inc(src_ready, 1)
        chain.link(last)
        for j in range(CT):
            last = dve.bn_aggr(self.mv[:, s, j], self.st[:, s, j])
        last.then_inc(self.mean_ready, 1)
        dve.drain()

    def stats_at(self, dve, chain, s, x, at):
        for j in range(CT):
            last = dve.bn_stats(self.st[:, s, j], flat(x[:, bass.ds(at + j, 1)]))
        chain.link(last)
        for j in range(CT):
            last = dve.bn_aggr(self.mv[:, s, j], self.st[:, s, j])
        last.then_inc(self.mean_ready, 1)
        dve.drain()

    def apply_at(self, dve, chain, s, out, x, at):
        dve.wait_ge(self.root_ready, 1)
        dve.sem_inc(self.root_ready, -1)
        chain.link(dve.reciprocal(self.rs[:, s], self.rs[:, s]))
        for j in range(CT):
            last = dve.tensor_scalar(out[:, j:j + 1], x[:, bass.ds(at + j, 1)], self.mv[:, s, j, 0:1],
                                     self.rs[:, s, j:j + 1], ALU.subtract, ALU.mult)
        return last

    def scaled(self, dve, chain, s, out, src, scale, shift):
        for j in range(CT):
            last = dve.scalar_tensor_tensor(out(j), src(j), self.mv[:, s, j, 0:1], scale, ALU.subtract, ALU.mult)
        chain.link(last)
        dve.wait_ge(self.root_ready, 1)
        dve.sem_inc(self.root_ready, -1)
        chain.link(dve.reciprocal(self.rs[:, s], self.rs[:, s]))
        for j in range(CT):
            last = dve.scalar_tensor_tensor(out(j), out(j), self.rs[:, s, j:j + 1], shift, ALU.mult, ALU.add)
        return last

    def root(self, act, s):
        act.wait_ge(self.mean_ready, 1)
        act.sem_inc(self.mean_ready, -1)
        act.activation(self.rs[:, s], self.mv[:, s, :, 1], ACT.Sqrt, bias=self.eps[:]).then_inc(self.root_ready, 1)

    def apply(self, dve, chain, s, out, src):
        dve.wait_ge(self.root_ready, 1)
        dve.sem_inc(self.root_ready, -1)
        chain.link(dve.reciprocal(self.rs[:, s], self.rs[:, s]))
        for j in range(CT):
            last = dve.tensor_scalar(out[:, j], src[:, j], self.mv[:, s, j, 0:1], self.rs[:, s, j:j + 1],
                                     ALU.subtract, ALU.mult)
        return last


def transposes(pe, out, src, ident):
    for h in range(KD):
        for j in range(CT):
            last = pe.transpose(out[:, h, j * P:(j + 1) * P], src[:, j, h * P:(h + 1) * P], ident)
    return last


def phase_norms(kit, S, soon):
    nc, ins = kit.nc, kit.ins
    cols = S["cols"]
    x0, hT, rows, ident = S["x0"], S["hT"], S["rows"], S["ident"]
    with Room(nc, "nrm") as r:
        xin = r.sb("xin", [P, B, CT, D])
        w = r.sb("w", [P, B, CT, D])
        n3 = r.sb("n3", [P, B, CT, D])
        ln0 = r.sb("ln0", [P, 2, D])
        lncol = S["lncol"]
        pT = r.ps("pT", [P, B, KD, CH])
        cT = r.sb("cT", [P, 2, KD, B])
        silu_c = r.sb("silu_c", [P, 2, KD, B])
        wmod = r.sb("wmod", [P, 2, KD, 6 * D])
        ones = r.sb("ones", [P, P])
        rep = r.sb("rep", [P, 2 * KD * B, P])
        gate_a = r.sb("gate_a", [P, 4, 2 * D])
        gate_b = r.sb("gate_b", [P, 4, 2 * D])
        pR = r.ps("pR", [P, 3, 512])
        pC = r.ps("pC", [P, 32])
        c_in, w_in = r.sem("c_in"), [r.sem("w_in0"), r.sem("w_in1")]
        rep_done, rows_done, rows_free, rows_ready = r.sem("rep_done"), r.sem("rows_done"), r.sem("rows_free"), r.sem("rows_ready")
        cols_done, silu_done = r.sem("cols_done"), r.sem("silu_done")
        loads, x_in, x_used = r.sem("loads"), [r.sem("x_in0"), r.sem("x_in1")], r.sem("x_used")
        steps, zeroed = r.sem("steps"), r.sem("zeroed")
        n3_free, n3_ready, turned, h_ready = r.sem("n3_free"), r.sem("n3_ready"), r.sem("turned"), r.sem("h_ready")
        norm = Norm(r)
        x_d = ins["x"].rearrange("(s c j p) d -> s c p j d", s=B, c=NC, p=P)
        with nc.Block() as block:
            @block.sync
            def _(sp):
                for l in range(2):
                    sp.dma_start(cT[:, l], blocks(ins[f"cT{l}"])).then_inc(c_in, 16)
                sp.dma_start(wmod[:, 0], blocks(ins["L0_wmod"])).then_inc(w_in[0], 16)
                sp.dma_start(ident[:], ins["ident"]).then_inc(loads, 16)
                for n, name in enumerate(("ln0_w", "ln0_b")):
                    sp.dma_start(ln0[:, n], ins[name].partition_broadcast(P)).then_inc(loads, 16)
                sp.dma_start(lncol[:], ins["lncol"]).then_inc(loads, 16)
                for s in range(B):
                    sp.wait_ge(x_used, 1)
                    sp.sem_inc(x_used, -1)
                    sp.dma_start(xin[:, s], x_d[s, 0]).then_inc(x_in[s], 16)
                sp.dma_start(wmod[:, 1], blocks(ins["L1_wmod"])).then_inc(w_in[1], 16)
                with sp.Fori(1, NC) as i:
                    for s in range(B):
                        sp.wait_ge(x_used, 1)
                        sp.sem_inc(x_used, -1)
                        sp.dma_start(xin[:, s], x_d[s, bass.ds(i, 1)].rearrange("a p j d -> p (a j) d")).then_inc(x_in[s], 16)
                for e in soon:
                    e.issue(sp)

            @block.gpsimd
            def _(pool):
                pool.memset(hT[:, :, :, 0:1], 0.0).then_inc(zeroed, 1)

            @block.vector
            def _(dve):
                dve.memset(ones[:], 1.0).then_inc(rep_done, 1)
                dve.memset(norm.eps[:], EPS).then_inc(zeroed, 1)
                dve.sem_inc(x_used, 2)
                dve.sem_inc(n3_free, 2)
                with dve.Fori(0, NC) as i:
                    c = Chain(dve, steps)
                    for s in range(B):
                        dve.wait_ge(x_in[s], 16)
                        dve.sem_inc(x_in[s], -16)
                        norm.stats(dve, c, s, xin[:, s])
                    for s in range(B):
                        dve.wait_ge(rows_ready, 12)
                        c.link(norm.scaled(dve, c, s, lambda j: w[:, s, j], lambda j: xin[:, s, j],
                                           rows[:, 0, s, SCALE * D:(SCALE + 1) * D], rows[:, 0, s, SHIFT * D:(SHIFT + 1) * D]))
                        norm.stats(dve, c, s, w[:, s], x_used)
                    for s in range(B):
                        dve.wait_ge(loads, 64)
                        c.link(norm.scaled(dve, c, s, lambda j: flat(x0[:, bass.ds(i * CT + s * TT + j, 1)]),
                                           lambda j: w[:, s, j], ln0[:, 0], ln0[:, 1]))
                        norm.stats_at(dve, c, s, x0, i * CT + s * TT)
                    for s in range(B):
                        dve.wait_ge(n3_free, 1)
                        dve.sem_inc(n3_free, -1)
                        norm.apply_at(dve, c, s, n3[:, s], x0, i * CT + s * TT).then_inc(n3_ready, 1)
                dve.wait_ge(rows_ready, 24)
                all_gates = [(l, tr, rows[:, l, :, (3 * tr + GATE) * D:(3 * tr + GATE + 1) * D])
                             for l in range(2) for tr in range(2)]
                for l, tr, g in all_gates:
                    sign, size = (t[:, 2 * l + tr].rearrange("p (b n) -> p b n", b=2) for t in (gate_a, gate_b))
                    dve.tensor_scalar(sign, g, 0.0, 2.0, ALU.is_ge, ALU.mult)
                    dve.scalar_tensor_tensor(size, g, -1.0, g, ALU.mult, ALU.max)
                dve.drain()
                dve.tensor_scalar(gate_a[:], gate_a[:], -1.0, None, ALU.add)
                dve.drain()
                for l, tr, g in all_gates:
                    sign, size = (t[:, 2 * l + tr].rearrange("p (b n) -> p b n", b=2) for t in (gate_a, gate_b))
                    dve.scalar_tensor_tensor(g, size, 0.25, sign, ALU.max, ALU.mult)

            @block.tensor
            def _(pe):
                def modulation(l):
                    pe.wait_ge(rep_done, 2)
                    pe.wait_ge(w_in[l], 16)
                    for n in range(2 * 3):
                        b, m = n // 3, n % 3
                        pe.wait_ge(rows_free, 1)
                        pe.sem_inc(rows_free, -1)
                        for k in range(KD):
                            mm = pe.matmul(pR[:, n % 3], rep[:, (l * KD + k) * B + b], wmod[:, l, k, 512 * m:512 * m + 512],
                                           start=(k == 0), stop=(k == KD - 1))
                        mm.then_inc(rows_done, 1)
                    for m in range(2):
                        for h in range(KD):
                            at = (3 * (1 - l) + m) * D + h * P
                            o = ((l * 2 + m) * KD + h) * B
                            for k in range(KD):
                                mm = pe.matmul(pC[:, o:o + B], wmod[:, l, k, at:at + P], silu_c[:, l, k],
                                               start=(k == 0), stop=(k == KD - 1))
                    mm.then_inc(cols_done, 1)

                modulation(0)
                modulation(1)
                pe.wait_ge(loads, 64)
                with pe.Fori(0, NC) as i:
                    for s in range(B):
                        pe.wait_ge(h_ready, 1)
                        pe.sem_inc(h_ready, -1)
                        pe.wait_ge(n3_ready, 1)
                        pe.sem_inc(n3_ready, -1)
                        transposes(pe, pT[:, s], n3[:, s], ident[:]).then_inc(turned, 1)

            @block.scalar
            def _(act):
                def modulation(l):
                    for n in range(2 * 3):
                        b, m = n // 3, n % 3
                        act.wait_ge(rows_done, 1)
                        act.sem_inc(rows_done, -1)
                        for half in range(2):
                            at = 512 * m + half * D
                            plus = {"bias": ones[:, 0:1]} if at // D % 3 == SCALE else {}
                            act.activation(rows[:, l, b, at:at + D], pR[:, n % 3, half * D:half * D + D],
                                           ACT.Identity, **plus).then_inc(rows_ready, 1)
                        act.drain().then_inc(rows_free, 1)

                act.wait_ge(rep_done, 1)
                act.sem_inc(rows_free, 3)
                act.wait_ge(c_in, 32)
                act.activation(silu_c[:], cT[:], ACT.Silu).then_inc(silu_done, 1)
                act.wait_ge(silu_done, 1)
                for n in range(2 * KD * B):
                    act.activation(rep[:, n], ones[:], ACT.Copy,
                                   scale=silu_c[:].rearrange("p l k b -> p (l k b)")[:, n:n + 1])
                act.drain().then_inc(rep_done, 1)
                modulation(0)
                act.wait_ge(zeroed, 2)
                act.sem_inc(h_ready, 2)

                def second_layer():
                    modulation(1)
                    act.wait_ge(loads, 64)
                    act.wait_ge(cols_done, 2)
                    pc = pC[:, 0:16].rearrange("p (l m k b) -> p l m k b", l=2, m=2, k=2)
                    act.activation(cols[:, :, 0], pc[:, :, 0], ACT.Copy)
                    act.activation(cols[:, :, 1], pc[:, :, 1], ACT.Identity, bias=ones[:, 0:1])

                def chunk(i, beside=None):
                    for n in range(3):
                        for s in range(B):
                            norm.root(act, s)
                    if beside:
                        beside()
                    for s in range(B):
                        act.wait_ge(turned, 1)
                        act.sem_inc(turned, -1)
                        for h in range(KD):
                            last = act.activation(hT[:, h, s, bass.ds(i * CH + 1, CH)], pT[:, s, h], ACT.Identity,
                                                  scale=lncol[:, 0, h:h + 1], bias=lncol[:, 1, h:h + 1])
                            if h == 0:
                                last.then_inc(n3_free, 1)
                        last.then_inc(h_ready, 1)

                chunk(0, second_layer)
                with act.Fori(1, NC) as i:
                    chunk(i)


def phase_wkv(kit, S, early):
    nc, ins = kit.nc, kit.ins
    hT, yT = S["hT"], S["hT"]
    with Room(nc, "wkv") as r:
        raw = [early.at[n] for n in ("Wk", "Wv", "Wr")]
        tm, uw = early.at["tm"], early.at["uw"]
        Wb = r.sb("Wb", [P, 3, KD, D])
        W = raw, [Wb[:, n] for n in range(3)]
        omt = r.sb("omt", [P, 3, KD])
        kv = r.sb("kv", [P, B, 2, KD, CH])
        sr = r.sb("sr", [P, B, KD, CH])
        pp = r.sb("pp", [P, B, KD, CH + 1])
        aa = r.sb("aa", [P, B, KD, CH + 1])
        bb = r.sb("bb", [P, B, KD, CH + 1])
        pm = r.sb("pm", [P, KD, CH])
        ex = r.sb("ex", [P, B, 4, KD, CH])
        ps = r.ps("ps", [P, 3, KD, CH])
        consts, mixed = r.sem("consts"), r.sem("mixed")
        proj_done, kv_ready, ex_ready, e_ready = r.sem("proj_done"), r.sem("kv_ready"), r.sem("ex_ready"), r.sem("e_ready")
        y_ready, steps, ps_free = r.sem("y_ready"), r.sem("steps"), r.sem("ps_free")
        den_ready, ln_done, inv_ready = r.sem("den_ready"), r.sem("ln_done"), r.sem("inv_ready")

        def halves(t):
            return t.rearrange("p h n -> p (h n)")

        with nc.Block() as block:
            @block.scalar
            def _(act):
                early.wait(act)
                act.activation(uw[:, 1], uw[:, 1], ACT.Exp).then_inc(consts, 1)
                act.wait_ge(consts, 5)

                def step(now, following, before):
                    if now:
                        s = now[1]
                        act.wait_ge(ex_ready, 1)
                        act.sem_inc(ex_ready, -1)
                        ee = ex[:, s].rearrange("p a h n -> p (a h n)")
                        act.preload_act_table_set("natural_log_exp_and_others")
                        act.activation(ee, ee, ACT.Exp).then_inc(e_ready, 1)
                    if before:
                        s = before[1]
                        act.wait_ge(den_ready, 1)
                        act.sem_inc(den_ready, -1)
                        act.activation(ex[:, s, 3], ex[:, s, 1], ACT.Ln).then_inc(ln_done, 1)
                        act.wait_ge(ln_done, 1)
                        act.sem_inc(ln_done, -1)
                        act.activation(ex[:, s, 3], ex[:, s, 3], ACT.Exp, scale=-1.0).then_inc(inv_ready, 1)
                    if following:
                        s = following[1]
                        act.wait_ge(y_ready, 1)
                        act.sem_inc(y_ready, -1)
                        for n in range(2):
                            act.wait_ge(proj_done, 1)
                            act.sem_inc(proj_done, -1)
                            for h in range(KD):
                                last = act.activation(kv[:, s, n, h], ps[:, n, h], ACT.Copy)
                            last.then_inc(ps_free, 1)
                        act.wait_ge(proj_done, 1)
                        act.sem_inc(proj_done, -1)
                        for h in range(KD):
                            last = act.activation(sr[:, s, h], ps[:, 2, h], ACT.Sigmoid)
                        last.then_inc(ps_free, 1)
                        act.drain().then_inc(kv_ready, 1)

                sweep(act, step)

            @block.tensor
            def _(pe):
                pe.wait_ge(mixed, 1)

                def step(now, following, before):
                    if following:
                        i, s = following
                        for n in range(3):
                            pe.wait_ge(ps_free, 1)
                            pe.sem_inc(ps_free, -1)
                            for o in range(KD):
                                for k in range(KD):
                                    for shift in range(2):
                                        mm = pe.matmul(ps[:, n, o], W[shift][n][:, k, o * P:(o + 1) * P],
                                                       hT[:, k, s, bass.ds(i * CH + 1 - shift, CH)],
                                                       start=(k == shift == 0), stop=(k == KD - 1 and shift == 1))
                            mm.then_inc(proj_done, 1)

                sweep(pe, step)

            @block.vector
            def _(dve):
                dve.wait_ge(consts, 1)
                dve.tensor_scalar(uw[:, 1], uw[:, 1], -1.0, None, ALU.mult).then_inc(consts, 1)
                dve.tensor_scalar(omt[:], tm[:], -1.0, 1.0, ALU.mult, ALU.add).then_inc(consts, 1)
                dve.memset(pp[:, :, :, 0:1], -1e38)
                dve.memset(aa[:, :, :, 0:1], 0.0)
                dve.memset(bb[:, :, :, 0:1], 0.0).then_inc(consts, 1)
                dve.sem_inc(y_ready, 2)
                dve.sem_inc(ps_free, 3)
                dve.wait_ge(consts, 4)
                dve.sem_inc(consts, 1)
                for t, share in ((1, omt), (0, tm)):
                    for n in range(3):
                        for k in range(KD):
                            dve.tensor_scalar(W[t][n][:, k], raw[n][:, k], share[:, n, k:k + 1], None, ALU.mult)
                    dve.drain()
                dve.sem_inc(mixed, 1)
                c = Chain(dve, steps)

                def step(now, following, before):
                    if now:
                        s = now[1]
                        dve.wait_ge(kv_ready, 1)
                        dve.sem_inc(kv_ready, -1)
                        k_t, v_t = kv[:, s, 0], kv[:, s, 1]
                        cur, old = pp[:, s, :, 1:CH + 1], pp[:, s, :, 0:CH]
                        for h in range(KD):
                            last = dve.tensor_tensor_scan(pp[:, s, h, 1:CH + 1], uw[:, 1, h:h + 1].broadcast_to([P, CH]),
                                                          kv[:, s, 0, h], pp[:, s, h, 0:1], ALU.add, ALU.max)
                        c.link(last)
                        for h in range(KD):
                            dve.scalar_tensor_tensor(ex[:, s, 0, h], pp[:, s, h, 0:CH], uw[:, 1, h:h + 1],
                                                     pp[:, s, h, 1:CH + 1], ALU.add, ALU.subtract)
                            last = dve.scalar_tensor_tensor(pm[:, h], kv[:, s, 0, h], uw[:, 0, h:h + 1],
                                                            pp[:, s, h, 0:CH], ALU.add, ALU.max)
                        c.link(last)
                        dve.tensor_tensor(ex[:, s, 1], k_t, cur, ALU.subtract)
                        dve.tensor_tensor(ex[:, s, 2], old, pm[:], ALU.subtract)
                        for h in range(KD):
                            last = dve.scalar_tensor_tensor(ex[:, s, 3, h], kv[:, s, 0, h], uw[:, 0, h:h + 1],
                                                            pm[:, h], ALU.add, ALU.subtract)
                        last.then_inc(ex_ready, 1)
                    if before:
                        i, s = before
                        dve.wait_ge(e_ready, 1)
                        dve.sem_inc(e_ready, -1)
                        k_v, v_t, num = kv[:, s, 0], kv[:, s, 1], ex[:, s, 0]
                        c.link(dve.tensor_tensor(k_v, ex[:, s, 1], v_t, ALU.mult))
                        for h in range(KD):
                            dve.tensor_tensor_scan(aa[:, s, h, 1:CH + 1], ex[:, s, 0, h], kv[:, s, 0, h],
                                                   aa[:, s, h, 0:1], ALU.mult, ALU.add)
                            last = dve.tensor_tensor_scan(bb[:, s, h, 1:CH + 1], ex[:, s, 0, h], ex[:, s, 1, h],
                                                          bb[:, s, h, 0:1], ALU.mult, ALU.add)
                        c.link(last)
                        f = ex[:, s, 3]
                        dve.tensor_tensor(num, ex[:, s, 2], aa[:, s, :, 0:CH], ALU.mult)
                        dve.tensor_tensor(v_t, f, v_t, ALU.mult)
                        c.link(dve.tensor_tensor(ex[:, s, 1], ex[:, s, 2], bb[:, s, :, 0:CH], ALU.mult))
                        dve.tensor_tensor(ex[:, s, 1], ex[:, s, 1], f, ALU.add).then_inc(den_ready, 1)
                        c.link(dve.tensor_tensor(num, num, v_t, ALU.add))
                        c.link(dve.tensor_tensor(num, num, sr[:, s], ALU.mult))
                        dve.sem_inc(y_ready, 1)
                        for t in (pp, aa, bb):
                            dve.tensor_copy(t[:, s, :, 0:1], t[:, s, :, CH:CH + 1])
                        dve.wait_ge(inv_ready, 1)
                        dve.sem_inc(inv_ready, -1)
                        inv, step = ex[:, s, 3], ex[:, s, 2]
                        c.link(dve.tensor_tensor(step, ex[:, s, 1], inv, ALU.mult))
                        c.link(dve.scalar_tensor_tensor(step, step, 2.0, inv, ALU.subtract, ALU.mult))
                        dve.scalar_tensor_tensor(yT[:, :, s, bass.ds(i * CH, CH)], step, -1.0, num, ALU.mult, ALU.mult)
                        dve.drain()

                sweep(dve, step)


def phase_channel_mix(kit, S, early, soon):
    nc, ins = kit.nc, kit.ins
    x0, hT, rows, ident = S["x0"], S["hT"], S["rows"], S["ident"]
    with Room(nc, "cmx") as r:
        Wo, Wfk, Wfv, Wfr, ln2, cm = (early.at[n] for n in ("Wo", "Wfk", "Wfv", "Wfr", "ln2", "cm"))
        omc = r.sb("omc", [P, 2, KD])
        xin = r.sb("xin", [P, B, CT, D])
        yc = r.sb("yc", [P, B, KD, CH])
        x1 = r.sb("x1", [P, B, CT, D])
        n2 = r.sb("n2", [P, B, CT, D])
        h2T = r.sb("h2T", [P, B, KD, CH + 1])
        xm = r.sb("xm", [P, B, 2, KD, CH])
        kf = r.sb("kf", [P, KH, CH])
        sg = r.sb("sg", [P, B, CT, D])
        norm = Norm(r)
        pA = r.ps("pA", [P, CT, D])
        pT = r.ps("pT", [P, KD, CH])
        pF = r.ps("pF", [P, 2, CH])
        pO = r.ps("pO", [P, 2, 512])
        consts, x_in, x_free = r.sem("consts"), [r.sem("x_in0"), r.sem("x_in1")], r.sem("x_free")
        y_ready, wo_done, pA_free = r.sem("y_ready"), r.sem("wo_done"), r.sem("pA_free")
        n_ready, turned, t_free = r.sem("n_ready"), r.sem("turned"), r.sem("t_free")
        a_steps, a_ready, xm_ready = r.sem("a_steps"), r.sem("a_ready"), r.sem("xm_ready")
        fk_done, relu_ready, fk_free, kf_ready = r.sem("fk_done"), r.sem("relu_ready"), r.sem("fk_free"), r.sem("kf_ready")
        r_done, kv_done, o_free, sg_ready = r.sem("r_done"), r.sem("kv_done"), r.sem("o_free"), r.sem("sg_ready")
        steps = r.sem("steps")
        x_d = ins["x"].rearrange("(s c j p) d -> s c p j d", s=B, c=NC, p=P)
        EARLY = 6
        with nc.Block() as block:
            @block.sync
            def _(sp):
                soon.issue(sp)
                with sp.Fori(0, NC) as i:
                    for s in range(B):
                        sp.wait_ge(x_free, 1)
                        sp.sem_inc(x_free, -1)
                        sp.dma_start(xin[:, s], x_d[s, bass.ds(i, 1)].rearrange("a p j d -> p (a j) d")).then_inc(x_in[s], 16)

            @block.scalar
            def _(act):
                early.wait(act)
                act.wait_ge(consts, 1)
                c = Chain(act, a_steps)

                def step(now, following, before):
                    if following:
                        i, s = following
                        for h in range(KD):
                            last = act.activation(yc[:, s, h], hT[:, h, s, bass.ds(i * CH, CH)], ACT.Copy)
                        last.then_inc(y_ready, 1)
                    if now:
                        s = now[1]
                        for o in range(KH):
                            act.wait_ge(fk_done, 1)
                            act.sem_inc(fk_done, -1)
                            act.activation(kf[:, o], pF[:, o % 2], ACT.Relu).then_inc(relu_ready, 1)
                    if following:
                        norm.root(act, following[1])
                    if now:
                        act.wait_ge(r_done, 1)
                        act.sem_inc(r_done, -1)
                        act.activation(sg[:, s], pA[:], ACT.Sigmoid).then_inc(sg_ready, 1)
                    if following:
                        s = following[1]
                        act.wait_ge(turned, 1)
                        act.sem_inc(turned, -1)
                        c.link(act.activation(h2T[:, s, :, 0:1], h2T[:, s, :, CH:CH + 1], ACT.Copy))
                        for h in range(KD):
                            last = act.activation(h2T[:, s, h, 1:CH + 1], pT[:, h], ACT.Identity,
                                                  scale=ln2[:, 0, h:h + 1], bias=ln2[:, 1, h:h + 1])
                        c.link(last)
                        for n in range(2):
                            for h in range(KD):
                                last = act.activation(xm[:, s, n, h], h2T[:, s, h, 0:CH], ACT.Copy, scale=omc[:, n, h:h + 1])
                                if n == h == 0:
                                    last.then_inc(t_free, 1)
                        last.then_inc(a_ready, 1)

                sweep(act, step)

            @block.tensor
            def _(pe):
                early.wait(pe)
                pe.sem_inc(x_free, 2)

                def step(now, following, before):
                    if now:
                        s = now[1]
                        pe.wait_ge(xm_ready, 1)
                        pe.sem_inc(xm_ready, -1)
                        for o in range(EARLY):
                            hidden(s, o)
                    if following:
                        s = following[1]
                        pe.wait_ge(pA_free, 1)
                        pe.sem_inc(pA_free, -1)
                        pe.wait_ge(y_ready, 1)
                        pe.sem_inc(y_ready, -1)
                        for j in range(CT):
                            for k in range(KD):
                                mm = pe.matmul(pA[:, j], yc[:, s, k, j * P:(j + 1) * P], Wo[:, k],
                                               start=(k == 0), stop=(k == KD - 1))
                        mm.then_inc(wo_done, 1)
                    if now:
                        s = now[1]
                        for o in range(EARLY, KH):
                            hidden(s, o)
                        pe.wait_ge(pA_free, 1)
                        pe.sem_inc(pA_free, -1)
                        for j in range(CT):
                            for k in range(KD):
                                mm = pe.matmul(pA[:, j], xm[:, s, 1, k, j * P:(j + 1) * P], Wfr[:, k],
                                               start=(k == 0), stop=(k == KD - 1))
                        mm.then_inc(r_done, 1)
                        pe.wait_ge(kf_ready, 1)
                        pe.sem_inc(kf_ready, -1)
                        back(s, 0)
                    if following:
                        s = following[1]
                        pe.wait_ge(n_ready, 1)
                        pe.sem_inc(n_ready, -1)
                        pe.wait_ge(t_free, 1)
                        pe.sem_inc(t_free, -1)
                        transposes(pe, pT, n2[:, s], ident[:]).then_inc(turned, 1)
                    if now:
                        for j in range(1, CT):
                            back(now[1], j)

                def hidden(s, o):
                    pe.wait_ge(fk_free, 1)
                    pe.sem_inc(fk_free, -1)
                    for k in range(KD):
                        mm = pe.matmul(pF[:, o % 2], Wfk[:, k, o * P:(o + 1) * P], xm[:, s, 0, k],
                                       start=(k == 0), stop=(k == KD - 1))
                    mm.then_inc(fk_done, 1)

                def back(s, j):
                    pe.wait_ge(o_free, 1)
                    pe.sem_inc(o_free, -1)
                    for k in range(KH):
                        mm = pe.matmul(pO[:, j % 2, 0:D], kf[:, k, j * P:(j + 1) * P], Wfv[:, k],
                                       start=(k == 0), stop=(k == KH - 1))
                    mm.then_inc(kv_done, 1)

                sweep(pe, step)

            @block.vector
            def _(dve):
                early.wait(dve)
                dve.tensor_scalar(omc[:], cm[:], -1.0, 1.0, ALU.mult, ALU.add)
                dve.memset(h2T[:, :, :, CH:CH + 1], 0.0)
                dve.memset(norm.eps[:], EPS).then_inc(consts, 1)
                dve.sem_inc(pA_free, 1)
                dve.sem_inc(t_free, 1)
                dve.sem_inc(fk_free, 2)
                dve.sem_inc(o_free, 2)
                c = Chain(dve, steps)

                def square(s, o):
                    dve.wait_ge(relu_ready, 1)
                    dve.sem_inc(relu_ready, -1)
                    dve.tensor_tensor(kf[:, o], kf[:, o], kf[:, o], ALU.mult).then_inc(fk_free, 1)

                def gated(s, j):
                    dve.wait_ge(kv_done, 1)
                    dve.sem_inc(kv_done, -1)
                    dve.tensor_tensor(sg[:, s, j], sg[:, s, j], pO[:, j % 2, 0:D], ALU.mult).then_inc(o_free, 1)

                def step(now, following, before):
                    if now:
                        for o in range(EARLY):
                            square(now[1], o)
                    if following:
                        i, s = following
                        dve.wait_ge(wo_done, 1)
                        dve.sem_inc(wo_done, -1)
                        c.link(dve.tensor_tensor(x1[:, s], x0[:, bass.ds(i * CT + s * TT, CT)], pA[:], ALU.add))
                        norm.stats(dve, c, s, x1[:, s], pA_free)
                    if now:
                        for o in range(EARLY, KH):
                            square(now[1], o)
                        dve.drain().then_inc(kf_ready, 1)
                    if following:
                        s = following[1]
                        norm.apply(dve, c, s, n2[:, s], x1[:, s]).then_inc(n_ready, 1)
                    if now:
                        dve.wait_ge(sg_ready, 1)
                        dve.sem_inc(sg_ready, -1)
                        dve.sem_inc(pA_free, 1)
                        gated(now[1], 0)
                    if following:
                        s = following[1]
                        dve.wait_ge(a_ready, 1)
                        dve.sem_inc(a_ready, -1)
                        for n in range(2):
                            for h in range(KD):
                                last = dve.scalar_tensor_tensor(xm[:, s, n, h], h2T[:, s, h, 1:CH + 1], cm[:, n, h:h + 1],
                                                                xm[:, s, n, h], ALU.mult, ALU.add)
                        last.then_inc(xm_ready, 1)
                    if now:
                        i, s = now
                        for j in range(1, CT):
                            gated(s, j)
                        dve.drain()
                        dve.wait_ge(x_in[s], 16)
                        dve.sem_inc(x_in[s], -16)
                        c.link(dve.tensor_tensor(sg[:, s], sg[:, s], x1[:, s], ALU.add))
                        c.link(dve.tensor_tensor(sg[:, s], sg[:, s], row4(rows[:, 0, s, GATE * D:(GATE + 1) * D]), ALU.mult))
                        dve.tensor_tensor(x0[:, bass.ds(i * CT + s * TT, CT)], sg[:, s], xin[:, s], ALU.add).then_inc(x_free, 1)

                sweep(dve, step)


def binarized(kit, r, S, early, w1T, w2T):
    nc, ins, ident = kit.nc, kit.ins, S["ident"]
    with Room(nc, "bin") as q:
        w = [early.at["w1"], early.at["w2"]]
        sgn = [q.sb(f"s{n}", [P, H // P * D]) for n in range(2)]
        al = [q.sb("al0", [P, KH]), q.sb("al1", [P, KD])]
        ps = q.ps("ps", [P, 4, 4, P])
        signed, ready, turned, freed, steps = (q.sem("signed"), q.sem("ready"),
                                                       q.sem("turned"), q.sem("freed"), q.sem("steps"))
        shape = [(KH, D), (KD, H)]
        parts = [(n, a, k) for n in range(2) for a in range(shape[n][1] // P) for k in range(shape[n][0])]

        def view(t, n):
            return t[n][:].rearrange("p (k m) -> p k m", k=shape[n][0]) if t is sgn else t[n][:]

        with nc.Block() as block:
            @block.scalar
            def _(act):
                early.wait(act)
                for n in range(2):
                    act.activation(view(sgn, n), w[n][:], ACT.Sign).then_inc(signed, 1)
                for g in range(len(parts) // 4):
                    act.wait_ge(turned, g + 1)
                    n, a, k = parts[4 * g]
                    src = ps[:, g % 4].rearrange("p a b -> p (a b)")
                    out = w1T[:, a, k * P:(k + 4) * P] if n == 0 else w2T[:, a:a + 2].rearrange("p a b -> p (a b)")
                    act.activation(out, src, ACT.Copy).then_inc(freed, 1)

            @block.vector
            def _(dve):
                early.wait(dve)
                dve.wait_ge(signed, 2)
                c = Chain(dve, steps)
                for n in range(2):
                    k, m = shape[n]
                    c.link(dve.tensor_reduce(al[n][:], view(w, n), AX.X, ALU.add, apply_absolute_value=True))
                    c.link(dve.tensor_scalar(al[n][:], al[n][:], 1.0 / m, None, ALU.mult))
                    for j in range(k):
                        last = dve.scalar_tensor_tensor(view(sgn, n)[:, j], view(sgn, n)[:, j], al[n][:, j:j + 1],
                                                        view(w, n)[:, j], ALU.mult, ALU.subtract)
                    c.link(last)
                    dve.tensor_tensor(w[n][:], w[n][:], view(sgn, n), ALU.add).then_inc(ready, 1)

            @block.tensor
            def _(pe):
                for i, (n, a, k) in enumerate(parts):
                    g = i // 4
                    if i % 4 == 0:
                        pe.wait_ge(ready, n + 1)
                        if g >= 4:
                            pe.wait_ge(freed, g - 3)
                    mm = pe.transpose(ps[:, g % 4, i % 4], view(w, n)[:, k, a * P:(a + 1) * P], ident[:])
                    if i % 4 == 3:
                        mm.then_inc(turned, 1)


def phase_ffn(kit, S, early, soon):
    nc, ins = kit.nc, kit.ins
    x, rows, cols, ident = S["x0"], S["rows"], S["cols"], S["ident"]
    with Room(nc, "ffn") as r:
        w1T = r.sb("w1T", [P, KD, H])
        w2T = r.sb("w2T", [P, KH, D])
        binarized(kit, r, S, early, w1T, w2T)
        b1 = r.sb("b1", [P, KH])
        b2 = r.sb("b2", [P, D])
        n1 = r.sb("n1", [P, B, CT, D])
        fT = r.sb("fT", [P, B, KD, CH])
        g = r.sb("g", [P, B, KH, CH])
        o = r.sb("o", [P, B, CT, D])
        norm = Norm(r)
        pT = r.ps("pT", [P, KD, CH])
        pF = r.ps("pF", [P, 4, CH])
        pO = r.ps("pO", [P, 2, 512])
        loads, consts = r.sem("loads"), r.sem("consts")
        n_ready, turned, t_free, f_ready = r.sem("n_ready"), r.sem("turned"), r.sem("t_free"), r.sem("f_ready")
        w1_done, pF_free, g_ready = r.sem("w1_done"), r.sem("pF_free"), r.sem("g_ready")
        w2_done, o_free, steps = r.sem("w2_done"), r.sem("o_free"), r.sem("steps")
        with nc.Block() as block:
            @block.sync
            def _(sp):
                sp.dma_start(b1[:], ins["b1col"]).then_inc(loads, 16)
                sp.dma_start(b2[:], ins["b2"].partition_broadcast(P)).then_inc(loads, 16)
                soon.issue(sp)

            @block.scalar
            def _(act):
                act.wait_ge(loads, 32)
                act.wait_ge(consts, 1)

                def step(now, following, before):
                    if following:
                        norm.root(act, following[1])
                    if now:
                        s = now[1]
                        for m in range(KH):
                            act.wait_ge(w1_done, 1)
                            act.sem_inc(w1_done, -1)
                            act.activation(g[:, s, m], pF[:, m % 4], ACT.Gelu, bias=b1[:, m:m + 1]).then_inc(pF_free, 1)
                        act.drain().then_inc(g_ready, 1)
                    if following:
                        s = following[1]
                        act.wait_ge(turned, 1)
                        act.sem_inc(turned, -1)
                        for h in range(KD):
                            last = act.activation(fT[:, s, h], pT[:, h], ACT.Identity,
                                                  scale=cols[:, 0, 1, h, s:s + 1], bias=cols[:, 0, 0, h, s:s + 1])
                        last.then_inc(f_ready, 1)

                sweep(act, step)

            @block.tensor
            def _(pe):
                pe.sem_inc(pF_free, 4)

                def step(now, following, before):
                    if now:
                        s = now[1]
                        pe.wait_ge(f_ready, 1)
                        pe.sem_inc(f_ready, -1)
                        for m in range(KH):
                            pe.wait_ge(pF_free, 1)
                            pe.sem_inc(pF_free, -1)
                            for k in range(KD):
                                mm = pe.matmul(pF[:, m % 4], w1T[:, k, m * P:(m + 1) * P], fT[:, s, k],
                                               start=(k == 0), stop=(k == KD - 1))
                            mm.then_inc(w1_done, 1)
                    if following:
                        pe.wait_ge(n_ready, 1)
                        pe.sem_inc(n_ready, -1)
                        transposes(pe, pT, n1[:, following[1]], ident[:]).then_inc(turned, 1)
                    if before:
                        s = before[1]
                        pe.wait_ge(g_ready, 1)
                        pe.sem_inc(g_ready, -1)
                        for j in range(CT):
                            pe.wait_ge(o_free, 1)
                            pe.sem_inc(o_free, -1)
                            for k in range(KH):
                                mm = pe.matmul(pO[:, j % 2, 0:D], g[:, s, k, j * P:(j + 1) * P], w2T[:, k],
                                               start=(k == 0), stop=(k == KH - 1))
                            mm.then_inc(w2_done, 1)

                sweep(pe, step)

            @block.vector
            def _(dve):
                dve.wait_ge(loads, 32)
                dve.memset(norm.eps[:], EPS).then_inc(consts, 1)
                dve.sem_inc(o_free, 2)
                c = Chain(dve, steps)

                def step(now, following, before):
                    if following:
                        i, s = following
                        norm.stats_at(dve, c, s, x, i * CT + s * TT)
                        norm.apply_at(dve, c, s, n1[:, s], x, i * CT + s * TT).then_inc(n_ready, 1)
                    if before:
                        i, s = before
                        for j in range(CT):
                            dve.wait_ge(w2_done, 1)
                            dve.sem_inc(w2_done, -1)
                            dve.tensor_tensor(o[:, s, j], pO[:, j % 2, 0:D], b2[:], ALU.add).then_inc(o_free, 1)
                        dve.drain()
                        c.link(dve.tensor_tensor(o[:, s], o[:, s], row4(rows[:, 0, s, (3 + GATE) * D:(4 + GATE) * D]), ALU.mult))
                        xc = x[:, bass.ds(i * CT + s * TT, CT)]
                        c.link(dve.tensor_tensor(xc, xc, o[:, s], ALU.add))

                sweep(dve, step)

HA, DA = 16, 16
GH = 4
PAIRS = (0, 0, 0, 1, 1, 2), (0, 1, 2, 0, 1, 0)
KQ = len(PAIRS[0]) * DA
ROWS = KQ + 3


def phase_qkv(kit, S, early):
    nc, ins = kit.nc, kit.ins
    x, cols, ident, V = S["x0"], S["cols"], S["ident"], S["V"]
    with Room(nc, "qkv") as r:
        W, bqk, bv = [early.at[n] for n in ("wq", "wk", "wv")], early.at["bqk"], early.at["bv"]
        n1 = r.sb("n1", [P, B, CT, D])
        fT = r.sb("fT", [P, B, KD, CH])
        full = r.sb("full", [P, B, 4, CH])
        piece = r.sb("piece", [P, B, 3, 4, CH], BF16)
        norm = Norm(r)
        pT = r.ps("pT", [P, KD, CH])
        pF = r.ps("pF", [P, 4, CH])
        pV = r.ps("pV", [P, CT, D])
        consts = r.sem("consts")
        n_ready, turned, f_ready = r.sem("n_ready"), r.sem("turned"), r.sem("f_ready")
        qk_done, pF_free, v_done, v_free = r.sem("qk_done"), r.sem("pF_free"), r.sem("v_done"), r.sem("v_free")
        p1_ready, r1_ready, p2_ready, p3_ready = r.sem("p1_ready"), r.sem("r1_ready"), r.sem("p2_ready"), r.sem("p3_ready")
        stored, steps = [r.sem("stored0"), r.sem("stored1")], r.sem("steps")
        with nc.Block() as block:
            @block.sync
            def _(sp):
                def step(now, following, before):
                    if before:
                        i, s = before
                        sp.wait_ge(p3_ready, 1)
                        sp.sem_inc(p3_ready, -1)
                        for n in range(3):
                            for m in range(2):
                                sp.dma_start(S["qk"][m, n, 2 * s:2 * s + 2, :, bass.ds(i * CH, CH)].rearrange("m p t -> p m t"),
                                             piece[:, s, n, 2 * m:2 * m + 2]).then_inc(stored[s], 16)

                sweep(sp, step)
                for s in range(B):
                    sp.wait_ge(stored[s], 96)

            @block.scalar
            def _(act):
                early.wait(act)
                act.wait_ge(consts, 2)
                for s in range(B):
                    act.sem_inc(stored[s], 96)

                def split(s, m):
                    scale = 0.25 if m < 2 else 1.0
                    act.wait_ge(qk_done, 1)
                    act.sem_inc(qk_done, -1)
                    act.activation(full[:, s, m], pF[:, m], ACT.Identity, scale=scale, bias=bqk[:, m // 2, m % 2:m % 2 + 1])
                    act.activation(piece[:, s, 0, m], pF[:, m], ACT.Identity, scale=scale,
                                   bias=bqk[:, m // 2, m % 2:m % 2 + 1]).then_inc(pF_free, 1)

                def step(now, following, before):
                    if following:
                        norm.root(act, following[1])
                    if before:
                        s = before[1]
                        act.wait_ge(r1_ready, 1)
                        act.sem_inc(r1_ready, -1)
                        act.activation(piece[:, s, 1], full[:, s], ACT.Copy).then_inc(p2_ready, 1)
                    if now:
                        act.wait_ge(stored[now[1]], 96)
                        act.sem_inc(stored[now[1]], -96)
                        split(now[1], 0)
                        split(now[1], 1)
                    if following:
                        s = following[1]
                        act.wait_ge(turned, 1)
                        act.sem_inc(turned, -1)
                        for h in range(KD):
                            last = act.activation(fT[:, s, h], pT[:, h], ACT.Identity,
                                                  scale=cols[:, 1, 1, h, s:s + 1], bias=cols[:, 1, 0, h, s:s + 1])
                        last.then_inc(f_ready, 1)
                    if now:
                        split(now[1], 2)
                        split(now[1], 3)
                        act.drain().then_inc(p1_ready, 1)

                act.preload_act_table_set("sqrt_and_others")
                sweep(act, step)

            @block.tensor
            def _(pe):
                early.wait(pe)
                pe.sem_inc(pF_free, 4)

                def project(s, m):
                    pe.wait_ge(pF_free, 1)
                    pe.sem_inc(pF_free, -1)
                    for k in range(KD):
                        mm = pe.matmul(pF[:, m], W[m // 2][:, k, m % 2 * P:m % 2 * P + P], fT[:, s, k],
                                       start=(k == 0), stop=(k == KD - 1))
                    mm.then_inc(qk_done, 1)

                def step(now, following, before):
                    if now:
                        s = now[1]
                        pe.wait_ge(f_ready, 1)
                        pe.sem_inc(f_ready, -1)
                        pe.wait_ge(v_free, 1)
                        pe.sem_inc(v_free, -1)
                        for j in range(CT):
                            for k in range(KD):
                                mm = pe.matmul(pV[:, j], fT[:, s, k, j * P:(j + 1) * P], W[2][:, k],
                                               start=(k == 0), stop=(k == KD - 1))
                        mm.then_inc(v_done, 1)
                        project(s, 0)
                        project(s, 1)
                    if following:
                        pe.wait_ge(n_ready, 1)
                        pe.sem_inc(n_ready, -1)
                        transposes(pe, pT, n1[:, following[1]], ident[:]).then_inc(turned, 1)
                    if now:
                        project(s, 2)
                        project(s, 3)

                sweep(pe, step)

            @block.vector
            def _(dve):
                early.wait(dve)
                dve.tensor_scalar(bqk[:, 0], bqk[:, 0], 0.25, None, ALU.mult).then_inc(consts, 1)
                dve.memset(norm.eps[:], EPS).then_inc(consts, 1)
                dve.sem_inc(v_free, 1)
                c = Chain(dve, steps)

                def step(now, following, before):
                    if following:
                        i, s = following
                        norm.stats_at(dve, c, s, x, i * CT + s * TT)
                        norm.apply_at(dve, c, s, n1[:, s], x, i * CT + s * TT).then_inc(n_ready, 1)
                    if now:
                        i, s = now
                        dve.wait_ge(v_done, 1)
                        dve.sem_inc(v_done, -1)
                        for m in range(KD):
                            last = dve.tensor_tensor(V[:, 2 * s + m, bass.ds(i * CT, CT)], pV[:, :, m * P:(m + 1) * P],
                                                     row4(bv[:, m * P:(m + 1) * P]), ALU.add)
                        last.then_inc(v_free, 1)
                        dve.wait_ge(p1_ready, 1)
                        dve.sem_inc(p1_ready, -1)
                        dve.tensor_tensor(full[:, s], full[:, s], piece[:, s, 0], ALU.subtract).then_inc(r1_ready, 1)
                    if before:
                        s = before[1]
                        dve.wait_ge(p2_ready, 1)
                        dve.sem_inc(p2_ready, -1)
                        dve.tensor_tensor(piece[:, s, 2], full[:, s], piece[:, s, 1], ALU.subtract).then_inc(p3_ready, 1)

                sweep(dve, step)


def phase_attention(kit, S):
    nc, ins = kit.nc, kit.ins
    ident, identb, V, qk = S["ident"], S["identb"], S["V"], S["qk"]
    with Room(nc, "att") as r:
        Q = r.sb("Q", [P, 2, NC, GH, CH], BF16)
        K = r.sb("K", [P, 2, NC, GH, CH], BF16)
        Vg = r.sb("Vg", [P, 2, TT, GH, 32])
        Pr = r.sb("Pr", [P, 4, 2, CH])
        above = r.sb("above", [P, P], BF16)
        below = r.sb("below", [P, P], BF16)
        mx = r.sb("mx", [P, 2, GH * CT, NC])
        mneg = r.sb("mneg", [P, GH * CT])
        mrest = r.sb("mrest", [P, GH * CT])
        mp = r.sb("mp", [P, 3, GH * CT], BF16)
        mrow = r.sb("mrow", [3 * GH * CT, NC, P], BF16)
        O = r.sb("O", [P, CH])
        rden = r.sb("rden", [P, 2, CT, GH])
        ST = r.ps("ST", [P, 2, 2, CH])
        MX = r.ps("MX", [P, 3, CH])
        OV = r.ps("OV", [P, CH])
        masks, in_q = r.sem("masks"), [[r.sem(f"in{a}{c}") for c in range(NC)] for a in range(2)]
        m_in = [r.sem(f"m_in{c}") for c in range(NC)]
        qk_free, st_done, p_ready = r.sem("qk_free"), r.sem("st_done"), r.sem("p_ready")
        mx_done, mx_free = r.sem("mx_done"), r.sem("mx_free")
        mp_ready, mt_done, mrow_ready = r.sem("mp_ready"), r.sem("mt_done"), r.sem("mrow_ready")
        ov_done, o_ready, tr_done = r.sem("ov_done"), r.sem("o_ready"), r.sem("tr_done")
        vg_ready, vg_free, steps, consts = r.sem("vg_ready"), r.sem("vg_free"), r.sem("steps"), r.sem("consts")
        chunks = list(range(NC))[::-1]

        def load(sp, i, a, c):
            for t, m in ((Q, 0), (K, 1)):
                for n, x in enumerate(PAIRS[m]):
                    src = qk[m, x, bass.ds(i, 1), 64 * a:64 * a + 64, c * CH:(c + 1) * CH]
                    sp.dma_start(t[DA * n:DA * n + DA, a, c],
                                 src.rearrange("a (h d) t -> d (a h) t", d=DA)).then_inc(in_q[a][c], 16)

        def sp_group(sp, mxg, nxt):
            for c in chunks:
                if mxg is not None:
                    sp.wait_ge(mrow_ready, 1)
                    sp.sem_inc(mrow_ready, -1)
                    for n in range(3):
                        sp.dma_start(Q[KQ + n:KQ + n + 1, mxg[1], c].rearrange("a h (r p) -> a (h r) p", p=P),
                                     mrow[n * GH * CT:(n + 1) * GH * CT, c]
                                     ).then_inc(m_in[c], 16)
                if nxt is not None:
                    sp.wait_ge(qk_free, 1)
                    sp.sem_inc(qk_free, -1)
                    load(sp, nxt[0], nxt[1], c)

        LAST = 2 * sum(CT * (c + 1) for c in range(NC))

        def pe_group(pe, eg, mxg, before=None, first=False):
            def scores_t(c, n, e, hh):
                r0 = (n - CT * c) * P if n >= CT * c else 0
                h = 2 * (e % 2) + hh
                mm = pe.matmul(ST[:, e % 2, hh, r0:], K[0:ROWS, eg[1], n // CT, h, n % CT * P:(n % CT + 1) * P],
                               Q[0:ROWS, eg[1], c, h, r0:], start=True, stop=(n < CT * c))
                if n >= CT * c:
                    mm = pe.matmul(ST[:, e % 2, hh, r0:r0 + P], identb[:], below[:], start=False, stop=True)
                if hh:
                    mm.then_inc(st_done, 1)

            def pv(c, n, e, a):
                if n == 0 and (c < NC - 1 or before is not None):
                    pe.wait_ge(o_ready, 1)
                    pe.sem_inc(o_ready, -1)
                r0 = (n - CT * c) * P if n >= CT * c else 0
                for h in range(GH):
                    mm = pe.matmul(OV[32 * h:32 * h + 32, r0:], Vg[:, a, n, h], Pr[:, (e + h // 2) % 4, h % 2, r0:],
                                   start=(n == 0), stop=(n == CT * c + CT - 1), tile_position=(0, 32 * h),
                                   skip_group_check=True)
                if n == CT * c + CT - 1:
                    mm.then_inc(ov_done, 1)

            def maxima(c, n, h):
                rr, w = n % CT, c - n // CT
                last = n // CT == 0
                cols = (rr + 1) * P if last else CH
                if h == 0 and rr == 0 and c == NC - 1:
                    pe.wait_ge(in_q[mxg[1]][w], 16 * 2 * len(PAIRS[0]))
                    pe.sem_inc(in_q[mxg[1]][w], -(16 * 2 * len(PAIRS[0])))
                pe.wait_ge(mx_free, 1)
                pe.sem_inc(mx_free, -1)
                bank = MX[:, u[0] % 3]
                u[0] += 1
                mm = pe.matmul(bank[:, 0:cols], Q[0:KQ, mxg[1], c, h, rr * P:(rr + 1) * P],
                               K[0:KQ, mxg[1], w, h, 0:cols], start=True, stop=not last)
                if last:
                    mm = pe.matmul(bank[:, cols - P:cols], identb[:], above[:], start=False, stop=True)
                mm.then_inc(mx_done, 1)

            def turn_max():
                pe.wait_ge(mp_ready, 1)
                pe.sem_inc(mp_ready, -1)
                pe.wait_ge(mx_free, 1)
                pe.sem_inc(mx_free, -1)
                u[0] += 1
                pe.transpose(MX[:, (u[0] - 1) % 3].bitcast(BF16)[0:3 * GH * CT, 0:P],
                             mp[:].rearrange("p a b -> p (a b)"), identb[:]).then_inc(mt_done, 1)

            def turn_out():
                pe.wait_ge(mx_free, 1)
                pe.sem_inc(mx_free, -1)
                u[0] += 1
                for j in range(CT):
                    mm = pe.transpose(MX[:, (u[0] - 1) % 3, j * P:(j + 1) * P], O[:, j * P:(j + 1) * P], ident[:])
                mm.then_inc(tr_done, 1)

            u = [0]
            late = [] if first else [turn_max]
            lag = []
            if before is not None:
                late.append(turn_out)
                lag = [(0, CT - 1, LAST - 2, before[1])]
            if eg is not None:
                pe.wait_ge(vg_ready, 1)
                pe.sem_inc(vg_ready, -1)
            e = 0
            for c in chunks:
                if eg is not None:
                    pe.wait_ge(m_in[c], 48)
                    pe.sem_inc(m_in[c], -48)
                for n in range(CT * (c + 1)):
                    for pair in range(2):
                        if eg is not None and lag:
                            pe.wait_ge(p_ready, 1)
                            pe.sem_inc(p_ready, -1)
                        for hh in range(2):
                            if eg is not None:
                                scores_t(c, n, e, hh)
                            if mxg is not None:
                                maxima(c, n, 2 * pair + hh)
                        e += 1
                    if eg is not None:
                        if lag:
                            pv(*lag.pop(0))
                        lag.append((c, n, e - 2, eg[1]))
                    if n == 2:
                        for f in late:
                            f()
                        late = []
                if c:
                    late = ([turn_max] if mxg is not None else []) + ([turn_out] if eg is not None else [])
            if u[0] % 3 and mxg is not None:
                pe.wait_ge(mx_free, -u[0] % 3)
                pe.sem_inc(mx_free, -(-u[0] % 3))
            if mxg is None:
                pe.wait_ge(p_ready, 2)
                pe.sem_inc(p_ready, -2)
                pv(*lag[0])
                pe.wait_ge(o_ready, 1)
                pe.sem_inc(o_ready, -1)
                turn_out()

        def act_out(act, c_free):
            act.wait_ge(ov_done, 1)
            act.sem_inc(ov_done, -1)
            act.activation(O[:], OV[:], ACT.Copy).then_inc(o_ready, 1)
            if c_free:
                act.drain().then_inc(qk_free, 1)

        def act_group(act, c_free, before, before_free, last=False):
            e = 0
            owed, owed_free = before, before_free
            for c in chunks:
                for n in range(CT * (c + 1)):
                    r0 = (n - CT * c) * P if n >= CT * c else 0
                    for pair in range(2):
                        act.wait_ge(st_done, 1)
                        act.sem_inc(st_done, -1)
                        act.activation(Pr[:, e % 4, :, r0:], ST[:, e % 2, :, r0:], ACT.Exp).then_inc(p_ready, 1)
                        e += 1
                    if n == 0 and owed:
                        act_out(act, owed_free)
                owed, owed_free = True, c_free
            if last:
                act_out(act, c_free)

        def dve_group(dve, eg, mxg, before=None, first=False):
            ch = Chain(dve, steps)

            def maxima(c, n, h):
                rr, w = n % CT, c - n // CT
                cols = (rr + 1) * P if n // CT == 0 else CH
                dve.wait_ge(mx_done, 1)
                dve.sem_inc(mx_done, -1)
                u[0] += 1
                return dve.tensor_reduce(mx[:, c % 2, h * CT + rr, w:w + 1], MX[:, (u[0] - 1) % 3, 0:cols], AX.X, ALU.max)

            def piece_step(c, k):
                dve.wait_ge(steps, 1)
                dve.sem_inc(steps, -1)
                if k == 0:
                    last = dve.tensor_reduce(mneg[:], mx[:, c % 2, :, 0:c + 1], AX.X, ALU.max)
                elif k == 1:
                    last = dve.tensor_scalar(mneg[:], mneg[:], -1.0, None, ALU.mult)
                elif k == 2:
                    last = dve.tensor_copy(mp[:, 0], mneg[:])
                elif k == 3:
                    last = dve.tensor_tensor(mrest[:], mneg[:], mp[:, 0], ALU.subtract)
                elif k == 4:
                    last = dve.tensor_copy(mp[:, 1], mrest[:])
                else:
                    last = dve.tensor_tensor(mp[:, 2], mrest[:], mp[:, 1], ALU.subtract)
                last.then_inc(mp_ready if k == 5 else steps, 1)

            def row(c):
                dve.wait_ge(mt_done, 1)
                dve.sem_inc(mt_done, -1)
                dve.tensor_copy(mrow[:, c], MX[:, u[0] % 3].bitcast(BF16)[0:3 * GH * CT, 0:P]).then_inc(mrow_ready, 1)
                dve.drain().then_inc(mx_free, 1)
                u[0] += 1

            def out(c, eg):
                dve.wait_ge(tr_done, 1)
                dve.sem_inc(tr_done, -1)
                turned = MX[:, u[0] % 3].rearrange("p (r h d) -> p r h d", r=CT, h=GH)
                u[0] += 1
                ch.link(dve.reciprocal(rden[:, c % 2], turned[:, :, :, DA]))
                for j in range(CT):
                    last = dve.tensor_tensor(
                        V[:, bass.ds(eg[0], 1), c * CT + j, 64 * eg[1]:64 * eg[1] + 64].rearrange("p a (h d) -> p (a h) d", h=GH),
                        turned[:, j, :, 0:DA],
                        rden[:, c % 2, j].unsqueeze(2).broadcast_to([P, GH, DA]), ALU.mult)
                last.then_inc(mx_free, 1)
                if c == 0:
                    dve.drain().then_inc(vg_free, 1)

            u = [0]
            owed = [] if first else [(0, k) for k in range(6)]
            late = [] if first else [(row, (0,))]
            if mxg is None:
                for t in owed:
                    piece_step(*t)
            if before is not None:
                late.append((out, (0, before)))
            for c in chunks:
                for n in range(CT * (c + 1)):
                    if mxg is not None:
                        for h in range(GH):
                            maxima(c, n, h).then_inc(mx_free, 1)
                            if owed:
                                piece_step(*owed.pop(0))
                    if n == 2:
                        for f, k in late:
                            f(*k)
                        late = []
                if mxg is not None:
                    dve.drain().then_inc(steps, 1)
                    owed = [(c, k) for k in range(6)]
                    late.append((row, (c,)))
                if eg is not None:
                    late.append((out, (c, eg)))
            if u[0] % 3 and mxg is not None:
                dve.sem_inc(mx_free, -u[0] % 3)
            if mxg is None:
                out(0, eg)

        N2 = 2 * B
        with nc.Block() as block:
            @block.sync
            def _(sp):
                for a in range(2):
                    for c in chunks:
                        load(sp, 0, a, c)
                sp_group(sp, (0, 0), None)
                with sp.Fori(0, N2 - 1) as i:
                    sp_group(sp, (i, 1), (i + 1, 0))
                    sp_group(sp, (i + 1, 0), (i + 1, 1))
                sp_group(sp, (N2 - 1, 1), None)

            @block.gpsimd
            def _(pool):
                pool.memset(above[:], 0.0).then_inc(consts, 1)
                pool.memset(below[:], 0.0).then_inc(consts, 1)
                pool.wait_ge(consts, 2)
                pool.affine_select(out=above[:], in_=above[:], compare_op=ALU.is_ge, fill=NEG, base=0,
                                   pattern=[[-1, P]], channel_multiplier=1).then_inc(masks, 1)
                pool.affine_select(out=below[:], in_=below[:], compare_op=ALU.is_ge, fill=NEG, base=0,
                                   pattern=[[1, P]], channel_multiplier=-1).then_inc(masks, 1)
                pool.drain()
                pool.memset(K[KQ:ROWS], 1.0)
                pool.drain()
                pool.memset(Vg[:], 1.0)
                pool.drain()
                pool.sem_inc(vg_free, 2)
                with pool.Fori(0, N2) as i:
                    for a in range(2):
                        pool.wait_ge(vg_free, 1)
                        pool.sem_inc(vg_free, -1)
                        src = V[:, bass.ds(i, 1), :, 64 * a:64 * a + 64].rearrange("p a j n -> p (a j) n")
                        for h in range(GH):
                            last = pool.tensor_copy(Vg[:, a, :, h, 0:DA], src[:, :, h * DA:(h + 1) * DA])
                        last.then_inc(vg_ready, 1)

            @block.scalar
            def _(act):
                act_group(act, True, False, False)
                with act.Fori(0, N2 - 2) as _i:
                    act_group(act, True, True, True)
                    act_group(act, True, True, True)
                act_group(act, True, True, True)
                act_group(act, False, True, True)
                act_group(act, False, True, False, last=True)

            @block.tensor
            def _(pe):
                pe.wait_ge(masks, 2)
                pe.wait_ge(S["identb_ready"], 1)
                pe_group(pe, None, (0, 0), first=True)
                pe_group(pe, (0, 0), (0, 1))
                with pe.Fori(0, N2 - 1) as i:
                    pe_group(pe, (i, 1), (i + 1, 0), before=(i, 0))
                    pe_group(pe, (i + 1, 0), (i + 1, 1), before=(i, 1))
                pe_group(pe, (N2 - 1, 1), None, before=(N2 - 1, 0))

            @block.vector
            def _(dve):
                dve.tensor_copy(identb[:], ident[:]).then_inc(S["identb_ready"], 1)
                dve.sem_inc(mx_free, 3)
                dve_group(dve, None, (0, 0), first=True)
                dve_group(dve, (0, 0), (0, 1))
                with dve.Fori(0, N2 - 1) as i:
                    dve_group(dve, (i, 1), (i + 1, 0), before=(i, 0))
                    dve_group(dve, (i + 1, 0), (i + 1, 1), before=(i, 1))
                dve_group(dve, (N2 - 1, 1), None, before=(N2 - 1, 0))


XW = D + 2
NQ, NKV = 256, 512
R4 = 2 * B
FETCH = 9.0 / 8.0
ITERS = 50


def phase_route_scores(kit, S, soon):
    nc, ins = kit.nc, kit.ins
    x, rows, ident, A, xn, sc = S["x0"], S["rows"], S["ident"], S["V"], S["xn"], S["s4"]
    with Room(nc, "rts") as r:
        Wo = r.sb("Wo", [P, KD, D])
        bo = r.sb("bo", [P, D])
        tok = r.sb("tok", [P, 2, D])
        a = r.sb("a", [P, B, CT, D])
        aT = r.sb("aT", [P, B, KD, CH])
        h = r.sb("h", [P, B, CT, D])
        junk = r.sb("junk", [P, 2, CT, D])
        junk2 = r.sb("junk2", [P, B, CT, D])
        dots = r.sb("dots", [P, B, 2, CT])
        ss = r.sb("ss", [P, B, CT])
        norm = Norm(r)
        pT = r.ps("pT", [P, KD, CH])
        pA = r.ps("pA", [P, CT, D])
        loads, consts = r.sem("loads"), r.sem("consts")
        a_ready, turned, aT_ready, a_done, a_free = (r.sem("a_ready"), r.sem("turned"), r.sem("aT_ready"),
                                                     r.sem("a_done"), r.sem("a_free"))
        h_ready, ss_ready, steps, a_read = r.sem("h_ready"), r.sem("ss_ready"), r.sem("steps"), r.sem("a_read")
        with nc.Block() as block:
            @block.sync
            def _(sp):
                sp.dma_start(Wo[:], ins["wo"].rearrange("(k p) n -> p k n", p=P)).then_inc(loads, 16)
                sp.dma_start(bo[:], ins["bo"].partition_broadcast(P)).then_inc(loads, 16)
                for n, name in enumerate(("q_tok", "kv_tok")):
                    sp.dma_start(tok[:, n], ins[name].partition_broadcast(P)).then_inc(loads, 16)
                soon.issue(sp)

            @block.gpsimd
            def _(pool):

                def step(now, following, before):
                    if following:
                        i, s = following
                        pool.wait_ge(a_free, 1)
                        pool.sem_inc(a_free, -1)
                        for m in range(KD):
                            last = pool.tensor_copy(a[:, s, :, m * P:(m + 1) * P].unsqueeze(1),
                                                    A[:, 2 * s + m:2 * s + m + 1, bass.ds(i * CT, CT)])
                        last.then_inc(a_ready, 1)

                sweep(pool, step)

            @block.scalar
            def _(act):
                act.wait_ge(loads, 64)
                act.wait_ge(consts, 1)
                act.sem_inc(a_free, 2)

                def step(now, following, before):
                    if following:
                        s = following[1]
                        act.wait_ge(turned, 1)
                        act.sem_inc(turned, -1)
                        for k in range(KD):
                            last = act.activation(aT[:, s, k], pT[:, k], ACT.Copy)
                        last.then_inc(aT_ready, 1)
                        act.sem_inc(a_free, 1)
                    if now:
                        s = now[1]
                        act.wait_ge(h_ready, 1)
                        act.sem_inc(h_ready, -1)
                        for j in range(CT):
                            last = act.activation(junk2[:, s, j], h[:, s, j], ACT.Square, accum_out=ss[:, s, j:j + 1])
                        act.drain()
                        act.activation(ss[:, s], ss[:, s], ACT.Sqrt).then_inc(ss_ready, 1)
                    if following:
                        norm.root(act, following[1])

                act.preload_act_table_set("sqrt_and_others")
                sweep(act, step)

            @block.tensor
            def _(pe):
                pe.wait_ge(loads, 64)

                def step(now, following, before):
                    if following:
                        pe.wait_ge(a_ready, 1)
                        pe.sem_inc(a_ready, -1)
                        transposes(pe, pT, a[:, following[1]], ident[:]).then_inc(turned, 1)
                        pe.wait_ge(aT_ready, 1)
                        pe.sem_inc(aT_ready, -1)
                        pe.wait_ge(a_read, 1)
                        pe.sem_inc(a_read, -1)
                        s = following[1]
                        for j in range(CT):
                            for k in range(KD):
                                mm = pe.matmul(pA[:, j], aT[:, s, k, j * P:(j + 1) * P], Wo[:, k],
                                               start=(k == 0), stop=(k == KD - 1))
                        mm.then_inc(a_done, 1)

                sweep(pe, step)

            @block.vector
            def _(dve):
                dve.wait_ge(loads, 64)
                dve.memset(norm.eps[:], EPS).then_inc(consts, 1)
                c = Chain(dve, steps)

                def step(now, following, before):
                    if now:
                        i, s = now
                        norm.scaled(dve, c, s, lambda j: h[:, s, j], lambda j: flat(x[:, bass.ds(i * CT + s * TT + j, 1)]),
                                    rows[:, 1, s, (3 + SCALE) * D:(4 + SCALE) * D],
                                    rows[:, 1, s, (3 + SHIFT) * D:(4 + SHIFT) * D]).then_inc(h_ready, 1)
                        dve.drain()
                        for n in range(2):
                            for j in range(CT):
                                last = dve.tensor_tensor_reduce(junk[:, n, j], h[:, s, j], tok[:, n], 1.0, 0.0, ALU.mult,
                                                                ALU.add, dots[:, s, n, j:j + 1])
                        dve.drain()
                        dve.tensor_copy(sc[:].rearrange("p (n s) t -> p s n t", n=2)[:, s, :, bass.ds(i * CT, CT)], dots[:, s])
                    if following:
                        i, s = following
                        dve.wait_ge(a_done, 1)
                        dve.sem_inc(a_done, -1)
                        dve.tensor_tensor(h[:, s], pA[:], row4(bo[:]), ALU.add).then_inc(a_read, 1)
                        dve.drain()
                        c.link(dve.tensor_tensor(h[:, s], h[:, s], row4(rows[:, 1, s, GATE * D:(GATE + 1) * D]), ALU.mult))
                        xc = x[:, bass.ds(i * CT + s * TT, CT)]
                        c.link(dve.tensor_tensor(xc, xc, h[:, s], ALU.add))
                        norm.stats_at(dve, c, s, x, i * CT + s * TT)
                    if now:
                        i, s = now
                        dve.wait_ge(ss_ready, 1)
                        dve.sem_inc(ss_ready, -1)
                        c.link(dve.tensor_scalar(ss[:, s], ss[:, s], 1e-12, None, ALU.max))
                        c.link(dve.reciprocal(ss[:, s], ss[:, s]))
                        for j in range(CT):
                            dve.tensor_scalar(xn[:, bass.ds(i * CT + s * TT + j, 1), 0:D].rearrange("p a d -> p (a d)"),
                                              h[:, s, j], ss[:, s, j:j + 1], float(D) ** 0.5, ALU.mult, ALU.mult)
                        dve.drain()

                dve.sem_inc(a_read, 1)
                sweep(dve, step)


class Descent:

    def __init__(self, r, S):
        self.ident, self.s4, self.xn, self.rank = S["ident"], S["s4"], S["xn"], S["rank"]
        self.s17 = r.sb("s17", [P, R4, TT + 1])
        self.nu = r.sb("nu", [P, R4, TT + 1])
        self.t = r.sb("t17", [P, R4, TT + 1])
        self.e = r.sb("e", [P, R4, TT])
        self.es = r.sb("es", [P, R4])
        self.a = r.sb("a", [P, R4])
        self.lk = r.sb("lk", [P, R4])
        self.ln = r.sb("ln", [P, R4])
        self.m4 = r.sb("m4", [P, R4])
        self.md = r.sb("md", [R4, R4])
        self.m1 = r.sb("m1", [R4, 1])
        self.ones = r.sb("ones", [P, P])
        self.w = r.sb("w", [P, R4, TT])
        self.score = r.sb("score", [P, R4, TT])
        self.R = r.sb("R", [P, 2, T])
        self.junk = r.sb("junk", [P, T], BF16)
        self.tie = r.sb("tie", [P, P], BF16)
        self.lower = r.sb("lower", [P, P])
        self.cnt = r.sb("cnt", [P, R4, TT, 4])
        self.consts, self.mt, self.m_ready, self.mb = r.sem("consts"), r.sem("mt"), r.sem("m_ready"), r.sem("mb")
        self.w_ready, self.e_ready, self.es_ready = r.sem("w_ready"), r.sem("ce_ready"), r.sem("es_ready")
        self.ln_ready, self.score_in, self.score_ready = r.sem("ln_ready"), r.sem("score_in"), r.sem("score_ready")
        self.scores_final, self.r_ready, self.r_free = r.sem("scores_final"), r.sem("r_ready"), r.sem("r_free")

    def pool_start(self, pool):
        pool.memset(self.lower[:], 1.0).then_inc(self.consts, 1)
        pool.wait_ge(self.consts, 1)
        pool.affine_select(out=self.lower[:], in_=self.lower[:], compare_op=ALU.is_ge, fill=0.0, base=-1,
                           pattern=[[-1, P]], channel_multiplier=1).then_inc(self.consts, 1)

    def pe_start(self, pe, bank):
        pe.wait_ge(self.mt, 1)
        pe.transpose(bank[0:R4, 0:P], self.m4[:], self.ident[:]).then_inc(self.m_ready, 1)
        pe.wait_ge(self.mt, 2)
        pe.matmul(bank[:, 0:R4], self.ones[0:R4], self.md[:], start=True, stop=True).then_inc(self.mb, 1)
        pe.wait_ge(self.mt, 3)

    def dve_start(self, dve, c, bank):
        dve.memset(self.ones[:], 1.0)
        dve.memset(self.cnt[:], 0.0)
        for n, k in enumerate(min(n * FETCH, T) for n in (NQ, NKV)):
            dve.memset(self.lk[:, n * B:(n + 1) * B], math.log(k))
        dve.memset(self.nu[:], 0.0)
        dve.tensor_reduce(self.m4[:], self.s4[:], AX.X, ALU.max).then_inc(self.mt, 1)
        dve.wait_ge(self.m_ready, 1)
        c.link(dve.tensor_reduce(self.m1[:], bank[0:R4, 0:P], AX.X, ALU.max))
        dve.tensor_scalar(self.md[:], self.ident[0:R4, 0:R4], self.m1[:], None, ALU.mult).then_inc(self.mt, 1)
        dve.tensor_copy(self.s17[:, :, 0:TT], self.s4[:])
        dve.wait_ge(self.mb, 1)
        c.link(dve.tensor_copy(self.s17[:, :, TT], bank[:, 0:R4]))
        dve.sem_inc(self.mt, 1)
        self.dve_weights(dve)

    def act_exp(self, act):
        act.wait_ge(self.w_ready, 1)
        act.sem_inc(self.w_ready, -1)
        act.activation(self.e[:], self.w[:], ACT.Exp).then_inc(self.e_ready, 1)

    def dve_sum(self, dve):
        dve.wait_ge(self.e_ready, 1)
        dve.sem_inc(self.e_ready, -1)
        dve.tensor_reduce(self.es[:], self.e[:], AX.X, ALU.add).then_inc(self.es_ready, 1)

    def pe_sum(self, pe, bank):
        pe.wait_ge(self.es_ready, 1)
        pe.sem_inc(self.es_ready, -1)
        return pe.matmul(bank[:, 0:R4], self.ones[:], self.es[:], start=True, stop=True)

    def act_log(self, act, bank):
        act.activation(self.ln[:], bank[:, 0:R4], ACT.Ln).then_inc(self.ln_ready, 1)

    def dve_weights(self, dve):
        dve.tensor_tensor(self.w[:], self.nu[:, :, TT:TT + 1].broadcast_to([P, R4, TT]), self.nu[:, :, 0:TT],
                          ALU.subtract).then_inc(self.w_ready, 1)

    def dve_step(self, dve, c):
        dve.wait_ge(self.ln_ready, 1)
        dve.sem_inc(self.ln_ready, -1)
        c.link(dve.tensor_tensor(self.ln[:], self.ln[:], self.nu[:, :, TT], ALU.subtract))
        c.link(dve.tensor_tensor(self.a[:], self.lk[:], self.ln[:], ALU.subtract))
        c.link(dve.tensor_tensor(self.t[:], self.s17[:], self.a[:].unsqueeze(2).broadcast_to([P, R4, TT + 1]), ALU.add))
        c.link(dve.scalar_tensor_tensor(self.nu[:], self.t[:], 0.0, self.s17[:], ALU.max, ALU.subtract))
        self.dve_weights(dve)

    def dve_scores(self, dve, c):
        dve.wait_ge(self.w_ready, 1)
        dve.sem_inc(self.w_ready, -1)
        c.link(dve.tensor_scalar(self.w[:], self.t[:, :, 0:TT], 0.0, None, ALU.min))
        dve.sem_inc(self.score_in, 1)
        dve.wait_ge(self.score_ready, 1)
        dve.sem_inc(self.scores_final, 1)
        c.link(dve.tensor_scalar(self.e[:], self.score[:], -1.0, 1.0, ALU.mult, ALU.add))
        for n in range(2):
            dve.tensor_tensor(self.xn[:, :, D + n].rearrange("p (s t) -> p s t", s=B),
                              self.score[:, n * B:(n + 1) * B], self.e[:, n * B:(n + 1) * B], ALU.add)
        dve.wait_ge(self.consts, 2)
        dve.sem_inc(self.r_free, 2)

    def act_scores(self, act):
        act.wait_ge(self.score_in, 1)
        act.sem_inc(self.score_in, -1)
        act.activation(self.score[:], self.w[:], ACT.Exp).then_inc(self.score_ready, 1)

    def pe_row(self, pe, bank, n, q):
        for j in range(CT):
            mm = pe.transpose(bank[:, j * P:(j + 1) * P], self.score[:, n, q * CT + j:q * CT + j + 1].broadcast_to([P, P]),
                              self.ident[:])
        return mm

    def act_row(self, act, bank, n, q):
        if q == 0:
            act.wait_ge(self.r_free, 1)
            act.sem_inc(self.r_free, -1)
        return act.activation(self.R[:, n % 2, q * CH:(q + 1) * CH], bank, ACT.Copy)

    def dve_rank(self, dve, n, j):
        Rn, sj = self.R[:, n % 2], self.score[:, n, j:j + 1]
        if j == 0:
            dve.wait_ge(self.r_ready, 1)
            dve.sem_inc(self.r_ready, -1)
        dve.drain()
        if j:
            dve.tensor_scalar(self.junk[:, 0:j * P], Rn[:, 0:j * P], sj, 0.0, ALU.is_ge, ALU.add,
                              accum_out=self.cnt[:, n, j, 0:1])
        dve.tensor_scalar(self.junk[:, j * P:T], Rn[:, j * P:T], sj, 0.0, ALU.is_gt, ALU.add,
                          accum_out=self.cnt[:, n, j, 1:2])
        dve.scalar_tensor_tensor(self.tie[:], Rn[:, j * P:(j + 1) * P], sj, self.lower[:],
                                 ALU.is_equal, ALU.mult, accum_out=self.cnt[:, n, j, 2:3])
        if j == TT - 1:
            dve.drain().then_inc(self.r_free, 1)

HB, DH = 8, 64
HID = HB * DH
KG = HID // P


def phase_light(kit, S, early):
    nc, ins = kit.nc, kit.ins
    x, xn, rows, ident = S["x0"], S["xn"], S["rows"], S["ident"]
    with Room(nc, "lgt") as r:
        Wq, Wkv, Wo, gamma = (early.at[n] for n in ("Wq", "Wkv", "Wo", "gamma"))
        xc = r.sb("xc", [P, CT, D])
        xT = r.sb("xT", [P, KD, CH])
        qk = S["hT"][:].rearrange("p a b t -> p (a b t)")[:, 0:2 * B * KG * CH].rearrange(
            "p (m s g t) -> p m s g t", m=2, s=B, g=KG)
        v = r.sb("v", [P, B, CT, HID])
        mx = r.sb("mx", [P, 2, HB])
        den = r.sb("den", [P, 2, HB])
        Pr = r.sb("Pr", [P, 2, HB, P])
        PT = r.sb("PT", [P, HB, P])
        OT = r.sb("OT", [P, KG, P])
        y = r.sb("y", [P, 2, D])
        t = r.sb("t", [P, D])
        pu = r.ps("pu", [P, 4, 512])
        pS = r.ps("pS", [P, 2, HB, P])
        x_ready, x_free, full, free = r.sem("x_ready"), r.sem("x_free"), r.sem("full"), r.sem("free")
        s_done, s_free, mx_ready, e_ready, p_ready = (r.sem("s_done"), r.sem("s_free"), r.sem("mx_ready"),
                                                      r.sem("e_ready"), r.sem("p_ready"))
        evac, y_ready, steps = {n: r.sem("evac_" + n) for n in ("xT", "qk", "v", "PT", "OT")}, r.sem("y_ready"), r.sem("steps")
        p_free, y_free = r.sem("p_free"), r.sem("y_free")
        rt = Descent(r, S)
        UP = NC // 2
        PER = 3
        AHEAD = ITERS - UP * B * CT * PER
        proj = [("x", h) for h in range(KD)] + [(n, j) for n in ("q", "k", "v") for j in range(CT)]
        SKIP = -(len(proj) + AHEAD) % 4
        share = [(proj[0:2], proj[2:4]), (proj[4:6], proj[6:7]), (proj[7:9], proj[9:10]), (proj[10:12], proj[12:14])]

        def slot(h):
            return h % 2 * (HB // 2) + h // 2

        def pe_unit(pe, u, s, kind, j):
            pe.wait_ge(free, 1)
            pe.sem_inc(free, -1)
            out = pu[:, u % 4]
            if kind == "x":
                if j == 0:
                    pe.wait_ge(x_ready, 1)
                    pe.sem_inc(x_ready, -1)
                for n in range(CT):
                    mm = pe.transpose(out[:, n * P:(n + 1) * P], xc[:, n, j * P:(j + 1) * P], ident[:])
            else:
                if (kind, j) == ("q", 0):
                    pe.wait_ge(evac["xT"], 2)
                    pe.sem_inc(evac["xT"], -2)
                for k in range(KD):
                    if kind == "q":
                        w, m = Wq[:, k, j * P:(j + 1) * P], xT[:, k]
                    elif kind == "k":
                        w, m = Wkv[:, k, j * P:(j + 1) * P], xT[:, k]
                    else:
                        w, m = xT[:, k, j * P:(j + 1) * P], Wkv[:, k, HID:2 * HID]
                    mm = pe.matmul(out, w, m, start=(k == 0), stop=(k == KD - 1))
            mm.then_inc(full, 1)

        def act_unit(act, u, s, kind, j):
            act.wait_ge(full, 1)
            act.sem_inc(full, -1)
            src = pu[:, u % 4]
            if kind == "x":
                act.activation(xT[:, j], src, ACT.Copy, scale=gamma[:, j:j + 1]).then_inc(evac["xT"], 1)
                act.drain().then_inc(free, 1)
                if j == KD - 1:
                    act.sem_inc(x_free, 1)
            else:
                if kind == "q":
                    act.activation(qk[:, 0, s, j], src, ACT.Copy, scale=DH ** -0.5).then_inc(free, 1)
                elif kind == "k":
                    act.activation(qk[:, 1, s, j], src, ACT.Copy).then_inc(free, 1)
                else:
                    act.activation(v[:, s, j], src, ACT.Copy).then_inc(free, 1)
                if j == CT - 1 and kind != "q":
                    act.drain().then_inc(evac["qk" if kind == "k" else "v"], 1)

        def pe_scores(pe, s, w):
            if w == 0:
                pe.wait_ge(evac["qk"], 1)
                pe.sem_inc(evac["qk"], -1)
            pe.wait_ge(s_free, 1)
            pe.sem_inc(s_free, -1)
            for h in range(HB):
                at = slice(DH * (h % 2), DH * (h % 2) + DH)
                mm = pe.matmul(pS[:, w % 2, slot(h)], qk[at, 0, s, h // 2, w * P:(w + 1) * P],
                               qk[at, 1, s, h // 2, w * P:(w + 1) * P], start=True, stop=True)
            mm.then_inc(s_done, 1)

        def act_exp(act, w):
            act.wait_ge(mx_ready, 1)
            act.sem_inc(mx_ready, -1)
            act.wait_ge(p_free, 1)
            act.sem_inc(p_free, -1)
            for h in range(HB):
                last = act.activation(Pr[:, w % 2, h], pS[:, w % 2, h], ACT.Exp, bias=mx[:, w % 2, h:h + 1],
                                      accum_out=den[:, w % 2, h:h + 1])
            last.then_inc(e_ready, 1)
            act.drain().then_inc(s_free, 1)

        def dve_max(dve, c, w):
            dve.wait_ge(s_done, 1)
            dve.sem_inc(s_done, -1)
            c.link(dve.tensor_reduce(mx[:, w % 2], pS[:, w % 2], AX.X, ALU.max))
            dve.tensor_scalar(mx[:, w % 2], mx[:, w % 2], -1.0, None, ALU.mult).then_inc(mx_ready, 1)

        def pe_sum(pe, u):
            pe.wait_ge(free, 1)
            pe.sem_inc(free, -1)
            rt.pe_sum(pe, pu[:, u % 4]).then_inc(full, 1)

        def act_log(act, u):
            act.wait_ge(full, 1)
            act.sem_inc(full, -1)
            rt.act_log(act, pu[:, u % 4])
            act.drain().then_inc(free, 1)

        def pe_row(pe, u, n, q):
            pe.wait_ge(free, 1)
            pe.sem_inc(free, -1)
            rt.pe_row(pe, pu[:, u % 4], n, q).then_inc(full, 1)

        def act_row(act, u, n, q):
            act.wait_ge(full, 1)
            act.sem_inc(full, -1)
            rt.act_row(act, pu[:, u % 4], n, q)
            act.drain().then_inc(free, 1)
            if q == CT - 1:
                act.sem_inc(rt.r_ready, 1)

        def pe_chunk(pe, s, more, nxt, descend, row=None):
            u = 0
            for w in range(CT):
                for half in range(2):
                    pe.wait_ge(free, 1)
                    pe.sem_inc(free, -1)
                    if half == 0:
                        pe.wait_ge(p_ready, 1)
                        pe.sem_inc(p_ready, -1)
                    for h in range(4):
                        mm = pe.transpose(pu[:, u % 4, h * P:(h + 1) * P], Pr[:, w % 2, 4 * half + h], ident[:])
                    mm.then_inc(full, 1)
                    u += 1
                if w < CT - 1:
                    pe_scores(pe, s, w + 1)
                elif nxt:
                    pe_scores(pe, 1 - s, 0)
                if descend:
                    pe_sum(pe, u)
                    u += 1
                pe.wait_ge(free, 1)
                pe.sem_inc(free, -1)
                pe.wait_ge(evac["PT"], 1)
                pe.sem_inc(evac["PT"], -1)
                if w == 0:
                    pe.wait_ge(evac["v"], 1)
                    pe.sem_inc(evac["v"], -1)
                for h in range(HB):
                    at = DH * (h % 2)
                    mm = pe.matmul(pu[at:at + DH, u % 4, h // 2 * P:(h // 2 + 1) * P], v[:, s, w, h * DH:(h + 1) * DH],
                                   PT[:, slot(h)], start=True, stop=True, tile_position=(0, at), skip_group_check=True)
                mm.then_inc(full, 1)
                u += 1
                if more:
                    for kind, j in share[w][0]:
                        pe_unit(pe, u, 1 - s, kind, j)
                        u += 1
                if descend:
                    pe_sum(pe, u)
                    u += 1
                pe.wait_ge(free, 1)
                pe.sem_inc(free, -1)
                pe.wait_ge(evac["OT"], 1)
                pe.sem_inc(evac["OT"], -1)
                for k in range(KG):
                    mm = pe.matmul(pu[:, u % 4, 0:D], OT[:, k], Wo[:, k], start=(k == 0), stop=(k == KG - 1))
                mm.then_inc(full, 1)
                u += 1
                if more:
                    for kind, j in share[w][1]:
                        pe_unit(pe, u, 1 - s, kind, j)
                        u += 1
                if descend:
                    pe_sum(pe, u)
                    u += 1
                if row is not None:
                    pe_row(pe, u, row, w)
                    u += 1
            skip = -u % 4
            for _ in range(skip):
                pe.wait_ge(free, 1)
                pe.sem_inc(free, -1)

        def act_chunk(act, s, more, nxt, descend, row=None):
            u = 0
            for w in range(CT):
                if descend:
                    rt.act_exp(act)
                for half in range(2):
                    act.wait_ge(full, 1)
                    act.sem_inc(full, -1)
                    last = act.activation(PT[:, 4 * half:4 * half + 4].rearrange("p a b -> p (a b)"), pu[:, u % 4], ACT.Copy)
                    if half == 0:
                        last.then_inc(free, 1)
                    u += 1
                last.then_inc(evac["PT"], 1)
                act.drain().then_inc(free, 1)
                act.sem_inc(p_free, 1)
                if descend:
                    act_log(act, u)
                    u += 1
                act.wait_ge(full, 1)
                act.sem_inc(full, -1)
                act.activation(OT[:].rearrange("p a b -> p (a b)"), pu[:, u % 4], ACT.Copy).then_inc(evac["OT"], 1)
                act.drain().then_inc(free, 1)
                u += 1
                if descend:
                    rt.act_exp(act)
                if w < CT - 1 or nxt:
                    act_exp(act, (w + 1) % CT)
                if more:
                    for kind, j in share[w][0]:
                        act_unit(act, u, 1 - s, kind, j)
                        u += 1
                if descend:
                    act_log(act, u)
                    u += 1
                act.wait_ge(full, 1)
                act.sem_inc(full, -1)
                act.wait_ge(y_free, 1)
                act.sem_inc(y_free, -1)
                act.activation(y[:, w % 2], pu[:, u % 4, 0:D], ACT.Copy).then_inc(y_ready, 1)
                act.drain().then_inc(free, 1)
                u += 1
                if descend:
                    rt.act_exp(act)
                if more:
                    for kind, j in share[w][1]:
                        act_unit(act, u, 1 - s, kind, j)
                        u += 1
                if descend:
                    act_log(act, u)
                    u += 1
                if row is not None:
                    act_row(act, u, row, w)
                    u += 1
            skip = -u % 4
            if skip:
                act.sem_inc(free, skip)

        def dve_chunk(dve, c, s, i, nxt, descend, ranks=None):
            for w in range(CT):
                if descend:
                    rt.dve_sum(dve)
                if w < CT - 1 or nxt:
                    dve_max(dve, c, (w + 1) % CT)
                if descend:
                    rt.dve_step(dve, c)
                    rt.dve_sum(dve)
                if ranks is not None:
                    for j in range(2):
                        rt.dve_rank(dve, ranks, w * CT + j)
                if w < CT - 1 or nxt:
                    dve_normalise(dve, c, (w + 1) % CT)
                if descend:
                    rt.dve_step(dve, c)
                    rt.dve_sum(dve)
                if ranks is not None:
                    for j in range(2, CT):
                        rt.dve_rank(dve, ranks, w * CT + j)
                dve.wait_ge(y_ready, 1)
                dve.sem_inc(y_ready, -1)
                c.link(dve.tensor_tensor(t[:], y[:, w % 2], rows[:, 1, s, (3 + GATE) * D:(4 + GATE) * D], ALU.mult))
                xw = flat(x[:, bass.ds(i * CT + (s * TT + w), 1)])
                c.link(dve.tensor_tensor(xw, xw, t[:], ALU.add))
                dve.sem_inc(y_free, 1)
                if descend:
                    rt.dve_step(dve, c)

        def dve_normalise(dve, c, w):
            dve.wait_ge(e_ready, 1)
            dve.sem_inc(e_ready, -1)
            c.link(dve.reciprocal(den[:, w % 2], den[:, w % 2]))
            dve.tensor_tensor(Pr[:, w % 2], Pr[:, w % 2], den[:, w % 2].unsqueeze(2).broadcast_to([P, HB, P]),
                              ALU.mult).then_inc(p_ready, 1)

        def pool_chunk(pool, i, s):
            pool.wait_ge(x_free, 1)
            pool.sem_inc(x_free, -1)
            pool.tensor_copy(xc[:], xn[:, bass.ds(i * CT + s * TT, CT), 0:D]).then_inc(x_ready, 1)

        with nc.Block() as block:
            @block.gpsimd
            def _(pool):
                rt.pool_start(pool)
                pool_chunk(pool, 0, 0)
                with pool.Fori(0, NC - 1) as i:
                    pool_chunk(pool, i, 1)
                    pool_chunk(pool, i + 1, 0)
                pool_chunk(pool, NC - 1, 1)

            @block.tensor
            def _(pe):
                early.wait(pe)
                pe.sem_inc(s_free, 2)
                pe.sem_inc(free, 4)
                rt.pe_start(pe, pS[:, 1, 0])
                for u, (kind, j) in enumerate(proj):
                    pe_unit(pe, u, 0, kind, j)
                pe_scores(pe, 0, 0)
                for u in range(len(proj), len(proj) + AHEAD):
                    pe_sum(pe, u)
                if SKIP:
                    pe.wait_ge(free, SKIP)
                    pe.sem_inc(free, -SKIP)
                with pe.Fori(0, UP) as _i:
                    pe_chunk(pe, 0, True, True, True)
                    pe_chunk(pe, 1, True, True, True)
                pe.wait_ge(rt.scores_final, 1)
                for q in range(CT):
                    pe_row(pe, q, 0, q)
                for n in range(R4):
                    pe_chunk(pe, n % 2, n < R4 - 1, n < R4 - 1, False, n + 1 if n < R4 - 1 else None)

            @block.scalar
            def _(act):
                early.wait(act)
                act.preload_act_table_set("natural_log_exp_and_others")
                act.sem_inc(x_free, 1)
                act.sem_inc(p_free, 2)
                for u, (kind, j) in enumerate(proj):
                    act_unit(act, u, 0, kind, j)
                act_exp(act, 0)
                for u in range(len(proj), len(proj) + AHEAD):
                    rt.act_exp(act)
                    act_log(act, u)
                if SKIP:
                    act.sem_inc(free, SKIP)
                with act.Fori(0, UP) as _i:
                    act_chunk(act, 0, True, True, True)
                    act_chunk(act, 1, True, True, True)
                rt.act_scores(act)
                for q in range(CT):
                    act_row(act, q, 0, q)
                for n in range(R4):
                    act_chunk(act, n % 2, n < R4 - 1, n < R4 - 1, False, n + 1 if n < R4 - 1 else None)

            @block.vector
            def _(dve):
                c = Chain(dve, steps)
                dve.sem_inc(y_free, 2)
                rt.dve_start(dve, c, pS[:, 1, 0])
                dve_max(dve, c, 0)
                dve_normalise(dve, c, 0)
                for _ in range(AHEAD):
                    rt.dve_sum(dve)
                    rt.dve_step(dve, c)
                with dve.Fori(0, UP) as i:
                    dve_chunk(dve, c, 0, i, True, True)
                    dve_chunk(dve, c, 1, i, True, True)
                rt.dve_scores(dve, c)
                for n in range(R4):
                    dve_chunk(dve, c, n % 2, UP + n // 2, n < R4 - 1, False, n)
                dve.tensor_reduce(S["rank"][:], rt.cnt[:], AX.X, ALU.add)


def phase_heavy(kit, S, out_d):
    nc, ins = kit.nc, kit.ins
    x, xn, rows, ident, rank = S["x0"], S["xn"], S["rows"], S["ident"], S["rank"]
    TQ, TK = NQ // P, NKV // P
    NG = TQ + TK
    with Room(nc, "hvy") as r:
        Wq = r.sb("Wq", [P, KD, HID])
        Wkv = r.sb("Wkv", [P, KD, 2 * HID])
        Wo = r.sb("Wo", [P, KG, D])
        gamma = r.sb("gamma", [P, KD])
        iota = r.sb("iota", [P, NKV])
        zero = r.sb("zero", [1, XW])
        rc = r.sb("rc", [P, 2, CT])
        gb = r.sb("gb", [P, D])
        G = r.sb("G", [P, 2, NQ + NKV])
        X = r.sb("X", [P, NG, XW])
        xT = r.sb("xT", [P, KD, NQ + NKV])
        flat_h = S["hT"][:].rearrange("p a b t -> p (a b t)")
        qT = flat_h[:, 0:KG * NQ].rearrange("p (g t) -> p g t", g=KG)
        kT = flat_h[:, KG * NQ:KG * (NQ + NKV)].rearrange("p (g t) -> p g t", g=KG)
        v = flat_h[:, KG * (NQ + NKV):KG * (NQ + NKV) + TK * HID].rearrange("p (j n) -> p j n", j=TK)
        mx = r.sb("mx", [P, 4])
        den = r.sb("den", [P, 4])
        Pr = r.sb("Pr", [P, 4, NKV])
        PT = r.sb("PT", [P, 2, TK, NQ])
        OT = r.sb("OT", [P, KG, NQ])
        Y = r.sb("Y", [P, TQ, D])
        Gs = r.sb("Gs", [P, 2, CT, NQ])
        GT = r.sb("GT", [P, 2, TQ, CH])
        o = r.sb("o", [P, 2, CT, D])
        pu = r.ps("pu", [P, 8, 512])
        loads, iota_in, consts, g_ready, g_free = r.sem("loads"), r.sem("iota_in"), r.sem("consts"), r.sem("g_ready"), r.sem("g_free")
        gathered, x_ready, full, free = r.sem("gathered"), r.sem("x_ready"), r.sem("full"), r.sem("free")
        xT_ready, qkv_ready, s_done, s_free = r.sem("xT_ready"), r.sem("qkv_ready"), r.sem("s_done"), r.sem("s_free")
        mx_ready, e_ready, p_ready, p_free = r.sem("mx_ready"), r.sem("e_ready"), r.sem("p_ready"), r.sem("p_free")
        PT_ready, OT_ready, y_ready, all_free = r.sem("PT_ready"), r.sem("OT_ready"), r.sem("y_ready"), r.sem("all_free")
        gs_ready, gs_free, turned, GT_ready = r.sem("gs_ready"), r.sem("gs_free"), r.sem("turned"), r.sem("GT_ready")
        back, out_ready, stored, steps = r.sem("back"), r.sem("out_ready"), r.sem("stored"), r.sem("steps")
        added, o_full, o_free = r.sem("added"), r.sem("o_full"), r.sem("o_free")
        ranks = rank[:].rearrange("p (n s) t -> p n (s t)", s=B)
        LOOK = 3
        E = HB * TQ
        NU, NS = 3, 4

        def pe_scores(pe, e):
            h, qt = e // TQ, e % TQ
            at = slice(DH * (h % 2), DH * (h % 2) + DH)
            pe.wait_ge(s_free, 1)
            pe.sem_inc(s_free, -1)
            pe.matmul(pu[:, NU + e % NS], qT[at, h // 2, qt * P:(qt + 1) * P], kT[at, h // 2],
                      start=True, stop=True).then_inc(s_done, 1)

        with nc.Block() as block:
            @block.sync
            def _(sp):
                sp.dma_start(iota[:], ins["iota"].partition_broadcast(P)).then_inc(iota_in, 16)
                sp.dma_start(gamma[:], ins["ghcol"]).then_inc(loads, 16)
                for w, name in ((Wq, "wq_heavy"), (Wkv, "wkv_heavy"), (Wo, "wo_heavy")):
                    sp.dma_start(w[:], blocks(ins[name])).then_inc(loads, 16)
                o_v = out_d.rearrange("(c j p) d -> c p j d", j=CT, p=P)
                with sp.Fori(0, B) as b:
                    with sp.Fori(0, NC) as c:
                        sp.wait_ge(out_ready, 1)
                        sp.sem_inc(out_ready, -1)
                        sp.dma_start(o_v[bass.ds(b * NC + c, 1)].rearrange("a p j d -> p (a j) d"),
                                     x[:, bass.ds(b * TT + c * CT, CT)]).then_inc(stored, 16)
                        sp.wait_ge(stored, 16)
                        sp.sem_inc(stored, -16)

            @block.tensor
            def _(pe):
                pe.wait_ge(consts, 1)
                pe.sem_inc(free, NU)
                pe.sem_inc(s_free, NS)
                pe.sem_inc(o_free, 1)
                with pe.Fori(0, B) as b:
                    for j in range(NG):
                        pe.matmul(pu[:, j, 0:XW], zero[:, 0:P], zero[:], start=True, stop=False)
                    with pe.Fori(0, NC) as c:
                        for t in range(CT):
                            pe.wait_ge(g_ready, 1)
                            pe.sem_inc(g_ready, -1)
                            for j in range(NG):
                                mm = pe.matmul(pu[:, j, 0:XW], G[:, t % 2, j * P:(j + 1) * P],
                                               xn[:, bass.ds(b * TT + (c * CT + t), 1)].rearrange("p a d -> p (a d)"),
                                               start=False, stop=False)
                            mm.then_inc(g_free, 1)
                    for j in range(NG):
                        mm = pe.matmul(pu[:, j, 0:XW], zero[:, 0:P], zero[:], start=False, stop=True)
                    mm.then_inc(gathered, 1)
                    pe.wait_ge(x_ready, 1)
                    pe.sem_inc(x_ready, -1)
                    u = 0
                    for h in range(KD):
                        for first, n in ((TQ, TK), (0, TQ)):
                            pe.wait_ge(free, 1)
                            pe.sem_inc(free, -1)
                            for j in range(n):
                                mm = pe.transpose(pu[:, u % NU, j * P:(j + 1) * P], X[:, first + j, h * P:(h + 1) * P], ident[:])
                            mm.then_inc(full, 1)
                            u += 1
                    pe.wait_ge(xT_ready, 1)
                    pe.sem_inc(xT_ready, -1)
                    pe.wait_ge(loads, 64)
                    for kind, j in [(n, j) for n in ("q", "k", "v") for j in range(CT)]:
                        pe.wait_ge(free, 1)
                        pe.sem_inc(free, -1)
                        for k in range(KD):
                            if kind == "q":
                                mm = pe.matmul(pu[:, u % NU, 0:NQ], Wq[:, k, j * P:(j + 1) * P], xT[:, k, 0:NQ],
                                               start=(k == 0), stop=(k == KD - 1))
                            elif kind == "k":
                                mm = pe.matmul(pu[:, u % NU], Wkv[:, k, j * P:(j + 1) * P], xT[:, k, NQ:],
                                               start=(k == 0), stop=(k == KD - 1))
                            else:
                                mm = pe.matmul(pu[:, u % NU], xT[:, k, NQ + j * P:NQ + (j + 1) * P], Wkv[:, k, HID:],
                                               start=(k == 0), stop=(k == KD - 1))
                        mm.then_inc(full, 1)
                        u += 1
                    pe.wait_ge(qkv_ready, 1)
                    pe.sem_inc(qkv_ready, -1)
                    for e in range(LOOK):
                        pe_scores(pe, e)
                    for e in range(E):
                        h, qt = e // TQ, e % TQ
                        pe.wait_ge(p_ready, 1)
                        pe.sem_inc(p_ready, -1)
                        pe.wait_ge(free, 1)
                        pe.sem_inc(free, -1)
                        for j in range(TK):
                            mm = pe.transpose(pu[:, u % NU, j * P:(j + 1) * P], Pr[:, e % 4, j * P:(j + 1) * P], ident[:])
                        mm.then_inc(full, 1)
                        u += 1
                        if e + LOOK < E:
                            pe_scores(pe, e + LOOK)
                        if qt == TQ - 1:
                            if h % 2 == 0:
                                pe.wait_ge(o_free, 1)
                                pe.sem_inc(o_free, -1)
                            pe.wait_ge(PT_ready, 1)
                            pe.sem_inc(PT_ready, -1)
                            at = DH * (h % 2)
                            for j in range(TK):
                                mm = pe.matmul(pu[at:at + DH, 7, 0:NQ], v[:, j, h * DH:(h + 1) * DH], PT[:, h % 2, j],
                                               start=(j == 0), stop=(j == TK - 1), tile_position=(0, at), skip_group_check=True)
                            if h % 2:
                                mm.then_inc(o_full, 1)
                    pe.wait_ge(OT_ready, 1)
                    pe.sem_inc(OT_ready, -1)
                    pe.wait_ge(free, 1)
                    pe.sem_inc(free, -1)
                    for j in range(TQ):
                        for k in range(KG):
                            mm = pe.matmul(pu[:, u % NU, j * D:(j + 1) * D], OT[:, k, j * P:(j + 1) * P], Wo[:, k],
                                           start=(k == 0), stop=(k == KG - 1))
                    mm.then_inc(full, 1)
                    pe.wait_ge(y_ready, 1)
                    pe.sem_inc(y_ready, -1)
                    pe.wait_ge(free, NU)
                    pe.sem_inc(free, -NU)
                    pe.sem_inc(free, NU)

                    def turn(c):
                        pe.wait_ge(gs_ready, 1)
                        pe.sem_inc(gs_ready, -1)
                        for k in range(TQ):
                            for t in range(CT):
                                mm = pe.transpose(pu[:, k, t * P:(t + 1) * P], Gs[:, c % 2, t, k * P:(k + 1) * P], ident[:])
                        mm.then_inc(turned, 1)

                    turn(0)
                    for c in range(NC):
                        pe.wait_ge(GT_ready, 1)
                        pe.sem_inc(GT_ready, -1)
                        if c < NC - 1:
                            turn(c + 1)
                        if c >= 2:
                            pe.wait_ge(added, 1)
                            pe.sem_inc(added, -1)
                        for t in range(CT):
                            for k in range(TQ):
                                mm = pe.matmul(pu[:, 4 + 2 * (c % 2) + t // 2, t % 2 * D:(t % 2 + 1) * D],
                                               GT[:, c % 2, k, t * P:(t + 1) * P], Y[:, k],
                                               start=(k == 0), stop=(k == TQ - 1))
                        mm.then_inc(back, 1)
                    pe.wait_ge(added, 2)
                    pe.sem_inc(added, -2)

            @block.scalar
            def _(act):
                act.wait_ge(loads, 64)
                with act.Fori(0, B) as b:
                    act.wait_ge(gathered, 1)
                    act.sem_inc(gathered, -1)
                    act.activation(X[:], pu[:, 0:NG, 0:XW], ACT.Copy).then_inc(x_ready, 1)
                    u = 0
                    for h in range(KD):
                        for lo, hi in ((NQ, NQ + NKV), (0, NQ)):
                            act.wait_ge(full, 1)
                            act.sem_inc(full, -1)
                            act.activation(xT[:, h, lo:hi], pu[:, u % NU, 0:hi - lo], ACT.Copy,
                                           scale=gamma[:, h:h + 1]).then_inc(free, 1)
                            u += 1
                    act.drain().then_inc(xT_ready, 1)
                    for kind, j in [(n, j) for n in ("q", "k", "v") for j in range(CT)]:
                        act.wait_ge(full, 1)
                        act.sem_inc(full, -1)
                        if kind == "q":
                            last = act.activation(qT[:, j], pu[:, u % NU, 0:NQ], ACT.Copy, scale=DH ** -0.5)
                        elif kind == "k":
                            last = act.activation(kT[:, j], pu[:, u % NU], ACT.Copy)
                        else:
                            last = act.activation(v[:, j], pu[:, u % NU], ACT.Copy, scale=X[:, TQ + j, D + 1:D + 2])
                        last.then_inc(free, 1)
                        u += 1
                    act.drain().then_inc(qkv_ready, 1)

                    def exp(e):
                        act.wait_ge(mx_ready, 1)
                        act.sem_inc(mx_ready, -1)
                        act.wait_ge(p_free, 1)
                        act.sem_inc(p_free, -1)
                        act.activation(Pr[:, e % 4], pu[:, NU + e % NS], ACT.Exp, bias=mx[:, e % 4:e % 4 + 1],
                                       accum_out=den[:, e % 4:e % 4 + 1]).then_inc(e_ready, 1)
                        act.drain().then_inc(s_free, 1)

                    for e in range(LOOK - 1):
                        exp(e)
                    for e in range(E):
                        h, qt = e // TQ, e % TQ
                        if e + LOOK - 1 < E:
                            exp(e + LOOK - 1)
                        act.wait_ge(full, 1)
                        act.sem_inc(full, -1)
                        act.activation(PT[:, h % 2, :, qt * P:(qt + 1) * P],
                                       pu[:, u % NU].rearrange("p (j n) -> p j n", j=TK), ACT.Copy).then_inc(free, 1)
                        u += 1
                        act.drain().then_inc(p_free, 1)
                        if qt == TQ - 1:
                            act.sem_inc(PT_ready, 1)
                        if qt == TQ - 1 and h % 2:
                            act.wait_ge(o_full, 1)
                            act.sem_inc(o_full, -1)
                            act.activation(OT[:, h // 2], pu[:, 7, 0:NQ], ACT.Copy).then_inc(o_free, 1)
                    act.drain().then_inc(OT_ready, 1)
                    act.wait_ge(full, 1)
                    act.sem_inc(full, -1)
                    for j in range(TQ):
                        last = act.activation(Y[:, j], pu[:, u % NU, j * D:(j + 1) * D], ACT.Copy, scale=X[:, j, D:D + 1])
                    act.drain().then_inc(y_ready, 1)
                    act.sem_inc(free, 1)
                    for c in range(NC):
                        act.wait_ge(turned, 1)
                        act.sem_inc(turned, -1)
                        act.activation(GT[:, c % 2], pu[:, 0:TQ], ACT.Copy).then_inc(GT_ready, 1)

            @block.vector
            def _(dve):
                dve.memset(zero[:], 0.0).then_inc(consts, 1)
                dve.wait_ge(iota_in, 16)
                dve.sem_inc(g_free, 2)
                dve.sem_inc(p_free, 4)
                ch = Chain(dve, steps)
                gates = rows[:, 1, :, (3 + GATE) * D:(4 + GATE) * D]
                with dve.Fori(0, B) as b:
                    dve.tensor_copy(gb[:].unsqueeze(1), gates[:, bass.ds(b, 1)])
                    with dve.Fori(0, NC) as c:
                        ch.link(dve.tensor_copy(rc[:], ranks[:, :, bass.ds(b * TT + c * CT, CT)]))
                        for t in range(CT):
                            dve.wait_ge(g_free, 1)
                            dve.sem_inc(g_free, -1)
                            dve.tensor_scalar(G[:, t % 2, 0:NQ], iota[:, 0:NQ], rc[:, 0, t:t + 1], None, ALU.is_equal)
                            dve.tensor_scalar(G[:, t % 2, NQ:], iota[:], rc[:, 1, t:t + 1], None, ALU.is_equal)
                            dve.drain().then_inc(g_ready, 1)

                    def max_of(e):
                        dve.wait_ge(s_done, 1)
                        dve.sem_inc(s_done, -1)
                        ch.link(dve.tensor_reduce(mx[:, e % 4:e % 4 + 1], pu[:, NU + e % NS], AX.X, ALU.max))
                        dve.tensor_scalar(mx[:, e % 4:e % 4 + 1], mx[:, e % 4:e % 4 + 1], -1.0, None,
                                          ALU.mult).then_inc(mx_ready, 1)

                    def normalise(e):
                        dve.wait_ge(e_ready, 1)
                        dve.sem_inc(e_ready, -1)
                        d = den[:, e % 4:e % 4 + 1]
                        ch.link(dve.reciprocal(d, d))
                        dve.tensor_scalar(Pr[:, e % 4], Pr[:, e % 4], d, None, ALU.mult).then_inc(p_ready, 1)

                    for e in range(LOOK):
                        max_of(e)
                    normalise(0)
                    for e in range(E):
                        if e + 1 < E:
                            normalise(e + 1)
                        if e + LOOK < E:
                            max_of(e + LOOK)
                    dve.drain()

                    def one_hot(c):
                        ch.link(dve.tensor_copy(rc[:], ranks[:, :, bass.ds(b * TT + c * CT, CT)]))
                        for t in range(CT):
                            dve.tensor_scalar(Gs[:, c % 2, t], iota[:, 0:NQ], rc[:, 0, t:t + 1], None, ALU.is_equal)
                        dve.drain().then_inc(gs_ready, 1)

                    one_hot(0)
                    one_hot(1)
                    for c in range(NC):
                        dve.wait_ge(back, 1)
                        dve.sem_inc(back, -1)
                        if c + 2 < NC:
                            one_hot(c + 2)
                        ch.link(dve.tensor_tensor(o[:, c % 2], pu[:, 4 + 2 * (c % 2):6 + 2 * (c % 2)].rearrange("p a (j d) -> p (a j) d", d=D),
                                                  row4(gb[:]), ALU.mult))
                        dve.sem_inc(added, 1)
                        xc = x[:, bass.ds(b * TT + c * CT, CT)]
                        ch.link(dve.tensor_tensor(xc, xc, o[:, c % 2], ALU.add))
                        dve.sem_inc(out_ready, 1)


def two_layers(nc, ins, out_d):
    with ExitStack() as ctx:
        kit = Kit(nc, ins, ctx)

        def sb(name, shape, dt=F32):
            return ctx.enter_context(nc.sbuf_tensor(name, shape, dt))

        S = {
            "rows": sb("rows", [P, 2, B, 6 * D]),
            "cols": sb("cols", [P, 2, 2, KD, B]),
            "x0": sb("x", [P, NT, D]),
            "hT": sb("hT", [P, KD, B, T + 1]),
            "ident": sb("ident", [P, P]),
            "identb": sb("identb", [P, P], BF16),
            "lncol": sb("lncol", [P, 2, KD]),
            "identb_ready": ctx.enter_context(nc.semaphore("identb_ready")),
            "qk": nc.dram_tensor("qk_pieces", [2, 3, 2 * B, P, T], BF16, kind="Internal").ap(),
        }
        S["V"] = S["hT"][:].rearrange("p a b t -> p (a b t)")[:, 0:NT * D].rearrange("p (i t n) -> p i t n", i=4, t=TT)
        square = [P, KD, D]
        with Early(nc, "cmw", {
            "Wo": (square, blocks(ins["WoT"])), "Wfk": ([P, KD, H], blocks(ins["WfkT"])),
            "Wfv": ([P, KH, D], blocks(ins["WfvT"])), "Wfr": (square, blocks(ins["WfrT"])),
            "ln2": ([P, 2, KD], ins["ln2col"]), "cm": ([P, 2, KD], ins["cmcol"]),
        }) as mix_weights:
            with Early(nc, "kvw", {
                "Wk": (square, blocks(ins["WkT"])), "Wv": (square, blocks(ins["WvT"])),
                "Wr": (square, blocks(ins["WrT"])), "tm": ([P, 3, KD], ins["tmcol"]), "uw": ([P, 2, KD], ins["uwcol"]),
            }) as wkv_weights:
                phase_norms(kit, S, [wkv_weights, mix_weights])
                phase_wkv(kit, S, wkv_weights)
            with Early(nc, "ffw", {
                "w1": ([P, KH, D], blocks(ins["w1"])), "w2": ([P, KD, H], blocks(ins["w2"])),
            }) as ffn_weights:
                phase_channel_mix(kit, S, mix_weights, ffn_weights)
                with Early(nc, "qkw", {
                    "wq": (square, blocks(ins["wq"])), "wk": (square, blocks(ins["wk"])), "wv": (square, blocks(ins["wv"])),
                    "bqk": ([P, 2, KD], ins["bqkcol"]), "bv": ([P, D], ins["bv"].partition_broadcast(P)),
                }) as qkv_weights:
                    phase_ffn(kit, S, ffn_weights, qkv_weights)
                    phase_qkv(kit, S, qkv_weights)
        phase_attention(kit, S)
        S["xn"] = sb("xn", [P, NT, XW])
        S["s4"] = sb("s4", [P, R4, TT])
        S["rank"] = sb("rank", [P, R4, TT])
        with Early(nc, "lgw", {
            "Wq": ([P, KD, HID], blocks(ins["wq_light"])), "Wkv": ([P, KD, 2 * HID], blocks(ins["wkv_light"])),
            "Wo": ([P, KG, D], blocks(ins["wo_light"])), "gamma": ([P, KD], ins["glcol"]),
        }) as light_weights:
            phase_route_scores(kit, S, light_weights)
            phase_light(kit, S, light_weights)
        phase_heavy(kit, S, out_d)


def _laid_out(I):
    def rows(a):
        return np.ascontiguousarray(a)

    def col(v):
        return np.asarray(v).reshape(KD, P).T

    def cols(*vs):
        return np.ascontiguousarray(np.stack([col(v) for v in vs], 1))

    a = {"x": rows(I["L0_attn_x"].reshape(B * T, D))}
    for l in (0, 1):
        a[f"cT{l}"] = rows(I[f"L{l}_c"].T)
        a[f"L{l}_wmod"] = rows(I[f"L{l}_wmod"])
    for n in ("ln0_w", "ln0_b"):
        a[n] = rows(I["L0_attn_" + n])
    for n in ("Wk", "Wv", "Wr", "Wo", "Wfk", "Wfv", "Wfr"):
        a[n + "T"] = rows(I["L0_attn_" + n].T)
    a["lncol"] = cols(I["L0_attn_ln1_w"], I["L0_attn_ln1_b"])
    a["ln2col"] = cols(I["L0_attn_ln2_w"], I["L0_attn_ln2_b"])
    a["tmcol"] = cols(I["L0_attn_tmk"], I["L0_attn_tmv"], I["L0_attn_tmr"])
    a["uwcol"] = cols(I["L0_attn_time_first"], I["L0_attn_time_decay"])
    a["cmcol"] = cols(I["L0_attn_cmk"], I["L0_attn_cmr"])
    for n in ("w1", "w2", "b2"):
        a[n] = rows(I["L0_ffn_" + n])
    a["b1col"] = rows(I["L0_ffn_b1"].reshape(KH, P).T)
    for n in ("wq", "wk", "wv", "wo", "bv", "bo"):
        a[n] = rows(I["L1_attn_" + n])
    a["bqkcol"] = cols(I["L1_attn_bq"], I["L1_attn_bk"])
    a["q_tok"] = rows(I["L1_ffn_q_routing_token"])
    a["kv_tok"] = rows(I["L1_ffn_kv_routing_token"])
    for n in ("wq_light", "wkv_light", "wo_light", "wq_heavy", "wo_heavy"):
        a[n] = rows(I["L1_ffn_" + n])
    a["wkv_heavy"] = rows(I["L1_ffn_wkv_heavy"].reshape(HB, 2, DH, D).transpose(3, 1, 0, 2).reshape(D, 2 * HID))
    a["glcol"] = rows(col(I["L1_ffn_gamma_light"]))
    a["ghcol"] = rows(col(I["L1_ffn_gamma_heavy"]))
    a["ident"] = np.eye(P, dtype=np.float32)
    a["iota"] = np.arange(NKV, dtype=np.float32)
    return a


def kernel(**inputs):
    import concourse.bacc as _bacc
    from concourse.bass_utils import run_bass_kernel_spmd as _run

    nc = _bacc.Bacc("TRN2", target_bir_lowering=False, num_devices=1)
    arrays = _laid_out(inputs)
    ins = {n: nc.dram_tensor(f"in_{n}", a.shape, mybir.dt.from_np(a.dtype), kind="ExternalInput").ap()
           for n, a in arrays.items()}
    out = nc.dram_tensor("out", (B * T, D), F32, kind="ExternalOutput").ap()
    two_layers(nc, ins, out)
    r = _run(nc, [{f"in_{n}": a for n, a in arrays.items()}], core_ids=[0])
    return r.results[0]["out"].reshape(B, T, D)
```
